# Optimizing a Trainium2 kernel written in Bass

```python
import numpy as np
import jax
import jax.numpy as jnp

def _softmax(x, axis=-1):
    return jax.nn.softmax(x, axis=axis)

def _gelu(x):
    return jax.nn.gelu(x, approximate=True)

def _silu(x):
    return jax.nn.silu(x)

def _sigmoid(x):
    return jax.nn.sigmoid(x)

def _layernorm(x, axis=-1, eps=1e-05):
    m = jnp.mean(x, axis=axis, keepdims=True)
    v = jnp.var(x, axis=axis, keepdims=True)
    return (x - m) / jnp.sqrt(v + eps)

def _scatter_add(tgt, idx, src, axis=0):
    return tgt.at[idx].add(src)

def _segment_sum(src, seg, n):
    return jax.ops.segment_sum(src, seg, n)
kernel_name = 'mk_sandwich_d2_jaxref_r8_5a8083'

def setup_inputs(seed: int=0):
    np.random.seed(seed)
    _w = jnp.asarray

    def _L0_attn_setup():
        import math
        import jax, jax.numpy as jnp
        import numpy as np
        EMBED_DIM = 128
        ZDIM = 128
        CHUNK = 256
        DSTATE = 16
        DT_RANK = math.ceil(EMBED_DIM / 16)

        def silu(x):
            return x * jax.nn.sigmoid(x)

        def rmsnorm(x, w, eps=1e-05):
            var = jnp.mean(x * x, axis=-1, keepdims=True)
            return x * jax.lax.rsqrt(var + eps) * w

        def _rotary(v, sin, cos):
            x1, x2 = jnp.split(v, 2, axis=-1)
            return jnp.concatenate([x1 * cos - x2 * sin, x2 * cos + x1 * sin], axis=-1)

        def rel_pos_bias(alpha, beta, n):
            half = ZDIM // 2
            freqs = jnp.exp(jnp.arange(half, dtype=jnp.float32) * (-math.log(10000.0) / half))
            ang = jnp.arange(n, dtype=jnp.float32)[:, None] * freqs[None, :]
            sin, cos = (jnp.sin(ang), jnp.cos(ang))
            a = _rotary(jnp.broadcast_to(alpha, (n, ZDIM)), sin, cos)
            b = _rotary(jnp.broadcast_to(beta, (n, ZDIM)), sin, cos)
            return jnp.einsum('mk,nk->mn', a, b)

        def s6(u, xproj_w, dt_w, dt_b, A_log, D_p):
            x_dbl = u @ xproj_w.T
            dt, Bm, Cm = jnp.split(x_dbl, [DT_RANK, DT_RANK + DSTATE], axis=-1)
            dt = jax.nn.softplus(dt @ dt_w.T + dt_b)
            A = -jnp.exp(A_log)

            def step(h, inp):
                dt_t, B_t, C_t, u_t = inp
                dA = jnp.exp(dt_t[..., None] * A)
                h = dA * h + (dt_t * u_t)[..., None] * B_t[:, None, :]
                y = jnp.einsum('bdn,bn->bd', h, C_t)
                return (h, y)
            B, L, D = u.shape
            h0 = jnp.zeros((B, D, DSTATE), u.dtype)
            xs = (dt.transpose(1, 0, 2), Bm.transpose(1, 0, 2), Cm.transpose(1, 0, 2), u.transpose(1, 0, 2))
            _, ys = jax.lax.scan(step, h0, xs)
            return ys.transpose(1, 0, 2) + u * D_p
        key = jax.random.key(seed)
        ks = jax.random.split(key, 12)
        std = 0.02
        B, L, D = (2, 512, EMBED_DIM)
        f32 = jnp.float32
        inp = {'x': jax.random.normal(ks[0], (B, L, D), f32), 'norm_w': jnp.ones((D,), f32), 'v_w': jax.random.normal(ks[1], (D, D), f32) * std, 'v_b': jnp.zeros((D,), f32), 'mx_w': jax.random.normal(ks[2], (ZDIM + D + 2 * D, D), f32) * std, 'mx_b': jnp.zeros((ZDIM + 3 * D,), f32), 'h_w': jax.random.normal(ks[3], (D, D), f32) * std, 'h_b': jnp.zeros((D,), f32), 'gamma': jax.random.normal(ks[4], (2, ZDIM), f32) * std, 'beta': jnp.zeros((2, ZDIM), f32), 'alpha_rb': jax.random.normal(ks[5], (1, ZDIM), f32) * std, 'beta_rb': jax.random.normal(ks[6], (1, ZDIM), f32) * std, 'xproj_w': jax.random.normal(ks[7], (DT_RANK + 2 * DSTATE, D), f32) * std, 'dt_w': jax.random.normal(ks[8], (D, DT_RANK), f32) * std, 'dt_b': jnp.full((D,), -4.6, f32), 'A_log': jnp.log(jnp.broadcast_to(jnp.arange(1, DSTATE + 1, dtype=f32), (D, DSTATE))), 'D_p': jnp.ones((D,), f32)}
        return inp
    _L0_attn_in = _L0_attn_setup()

    def _L0_ffn_setup():
        import jax, jax.numpy as jnp
        import numpy as np
        DIM = 128
        HIDDEN = 384
        SCALE = 1.0 / 127.0

        def _dequant(w_int, dtype):
            return w_int.astype(dtype) * jnp.asarray(SCALE, dtype)
        key = jax.random.key(seed)
        k_x, k_g, k_u, k_d = jax.random.split(key, 4)
        x = jax.random.normal(k_x, (4, 256, DIM), dtype=jnp.float32)
        w_gate = jax.random.randint(k_g, (HIDDEN, DIM), -127, 128, dtype=jnp.int32)
        w_up = jax.random.randint(k_u, (HIDDEN, DIM), -127, 128, dtype=jnp.int32)
        w_down = jax.random.randint(k_d, (DIM, HIDDEN), -127, 128, dtype=jnp.int32)
        return {'x': x, 'w_gate': w_gate, 'w_up': w_up, 'w_down': w_down}
    _L0_ffn_in = _L0_ffn_setup()

    def _L1_attn_setup():
        import jax, jax.numpy as jnp
        import numpy as np
        D_MODEL = 128
        N_HEADS = 16
        HEAD_DIM = D_MODEL // N_HEADS
        MAX_SHIFT = HEAD_DIM // 2
        BATCH, SEQ = (2, 256)

        def _forward(x, Wq, bq, Wk, bk, Wv, bv, Wo, bo, W_cross, shift_weights, gate):
            b, s, _ = x.shape
            H, hd = (W_cross.shape[0], W_cross.shape[1])
            ms = shift_weights.shape[1]
            Q = (x @ Wq.T + bq).reshape(b, s, H, hd)
            K = (x @ Wk.T + bk).reshape(b, s, H, hd)
            V = (x @ Wv.T + bv).reshape(b, s, H, hd)
            Qt = jnp.einsum('bqhf,hfg->bqhg', Q, W_cross)
            scores_cross = jnp.einsum('bqhd,bkhd->bhqk', Qt, K)
            f = jnp.arange(hd)[:, None]
            g = jnp.arange(hd)[None, :]
            tau = g - f
            valid = (tau >= 0) & (tau < ms)
            M = jnp.where(valid[None], shift_weights[:, jnp.clip(tau, 0, ms - 1)], 0.0)
            K_mixed = jnp.einsum('hfg,bkhg->bkhf', M, K)
            scores_conv = jnp.einsum('bqhf,bkhf->bhqk', Q, K_mixed)
            gt = jax.nn.sigmoid(gate).reshape(1, H, 1, 1)
            scale = hd ** (-0.5)
            scores = (gt * scores_cross + (1.0 - gt) * scores_conv) * scale
            causal = jnp.tril(jnp.ones((s, s), dtype=bool))
            scores = jnp.where(causal[None, None], scores, -jnp.inf)
            attn = jax.nn.softmax(scores, axis=-1)
            out = jnp.einsum('bhqk,bkhd->bqhd', attn, V).reshape(b, s, H * hd)
            return out @ Wo.T + bo
        key = jax.random.key(seed)
        ks = jax.random.split(key, 12)
        s = 0.02
        x = jax.random.normal(ks[0], (BATCH, SEQ, D_MODEL), dtype=jnp.float32)
        Wq = jax.random.normal(ks[1], (D_MODEL, D_MODEL), dtype=jnp.float32) * s
        bq = jnp.zeros((D_MODEL,), jnp.float32)
        Wk = jax.random.normal(ks[2], (D_MODEL, D_MODEL), dtype=jnp.float32) * s
        bk = jnp.zeros((D_MODEL,), jnp.float32)
        Wv = jax.random.normal(ks[3], (D_MODEL, D_MODEL), dtype=jnp.float32) * s
        bv = jnp.zeros((D_MODEL,), jnp.float32)
        Wo = jax.random.normal(ks[4], (D_MODEL, D_MODEL), dtype=jnp.float32) * s
        bo = jnp.zeros((D_MODEL,), jnp.float32)
        eye = jnp.broadcast_to(jnp.eye(HEAD_DIM, dtype=jnp.float32), (N_HEADS, HEAD_DIM, HEAD_DIM))
        W_cross = eye + 0.01 * jax.random.normal(ks[5], (N_HEADS, HEAD_DIM, HEAD_DIM), dtype=jnp.float32)
        decay = jnp.exp(-jnp.arange(MAX_SHIFT, dtype=jnp.float32) / (MAX_SHIFT / 4.0))
        shift_weights = jnp.broadcast_to(decay, (N_HEADS, MAX_SHIFT)).copy()
        gate = jnp.zeros((N_HEADS,), jnp.float32)
        return {'x': x, 'Wq': Wq, 'bq': bq, 'Wk': Wk, 'bk': bk, 'Wv': Wv, 'bv': bv, 'Wo': Wo, 'bo': bo, 'W_cross': W_cross, 'shift_weights': shift_weights, 'gate': gate}
    _L1_attn_in = _L1_attn_setup()

    def _L1_ffn_setup():
        import jax, jax.numpy as jnp
        import numpy as np
        DIM = 128
        DEPTH = 2
        HEADS = 8
        DIM_HEAD = 64
        WINDOW = 64
        INNER = HEADS * DIM_HEAD
        HID = int(DIM * 4 * 2 / 3)
        B, N = (2, 1024)
        QK_SCALE = 8.0

        def shift_token(t):
            t1, t2 = jnp.split(t, 2, axis=-1)
            t2 = jnp.pad(t2, ((0, 0), (1, 0), (0, 0)))[:, :-1]
            return jnp.concatenate([t1, t2], axis=-1)

        def l2norm(t):
            return t / jnp.clip(jnp.linalg.norm(t, axis=-1, keepdims=True), 1e-12)

        def rotate_half(x):
            x1, x2 = jnp.split(x, 2, axis=-1)
            return jnp.concatenate([-x2, x1], axis=-1)

        def rotary_xpos(q, k):
            n = q.shape[-2]
            half_idx = jnp.arange(0, DIM_HEAD, 2, dtype=jnp.float32)
            inv_freq = 1.0 / 10000.0 ** (half_idx / DIM_HEAD)
            t = jnp.arange(n, dtype=jnp.float32)
            freqs = t[:, None] * inv_freq[None, :]
            freqs = jnp.concatenate([freqs, freqs], axis=-1)
            base = (half_idx + 0.4 * DIM_HEAD) / (1.4 * DIM_HEAD)
            power = (t - n // 2) / float(WINDOW // 2)
            scale = base[None, :] ** power[:, None]
            scale = jnp.concatenate([scale, scale], axis=-1)
            cos, sin = (jnp.cos(freqs), jnp.sin(freqs))
            q = q * cos * scale + rotate_half(q) * sin * scale
            k = k * cos / scale + rotate_half(k) * sin / scale
            return (q, k)

        def local_attention(q, k, v):
            b, h, n, d = q.shape
            w = n // WINDOW
            bq = q.reshape(b, h, w, WINDOW, d) * QK_SCALE
            bk = k.reshape(b, h, w, WINDOW, d)
            bv = v.reshape(b, h, w, WINDOW, d)

            def look_around(t):
                p = jnp.pad(t, ((0, 0), (0, 0), (1, 0), (0, 0), (0, 0)))
                return jnp.concatenate([p[:, :, :w], p[:, :, 1:]], axis=3)
            bk, bv = (look_around(bk), look_around(bv))
            bt = jnp.arange(n).reshape(w, WINDOW)
            btp = jnp.pad(bt, ((1, 0), (0, 0)), constant_values=-1)
            btk = jnp.concatenate([btp[:w], btp[1:]], axis=1)
            sim = jnp.einsum('bhwid,bhwjd->bhwij', bq, bk)
            i = bt[:, :, None]
            j = btk[:, None, :]
            mask = (i < j) | (i > j + WINDOW) | (j == -1)
            sim = jnp.where(mask, -jnp.finfo(sim.dtype).max, sim)
            attn = jax.nn.softmax(sim, axis=-1)
            out = jnp.einsum('bhwij,bhwjd->bhwid', attn, bv)
            return out.reshape(b, h, n, d)

        def _layer(x, wqkv, qs, ksc, wo, lg, lb, w1, b1, w2, b2):
            b, n, _ = x.shape
            h = shift_token(x)
            qkv = h @ wqkv
            q, k, v = jnp.split(qkv, 3, axis=-1)
            to_heads = lambda t: t.reshape(b, n, HEADS, DIM_HEAD).transpose(0, 2, 1, 3)
            q, k, v = (to_heads(q), to_heads(k), to_heads(v))
            q = l2norm(q) * qs
            k = l2norm(k) * ksc
            q, k = rotary_xpos(q, k)
            o = local_attention(q, k, v)
            o = o.transpose(0, 2, 1, 3).reshape(b, n, INNER)
            x = x + o @ wo
            h = shift_token(x)
            mu = h.mean(-1, keepdims=True)
            var = h.var(-1, keepdims=True)
            h = (h - mu) / jnp.sqrt(var + 1e-05) * lg + lb
            h = h @ w1 + b1
            a, g = jnp.split(h, 2, axis=-1)
            h = a * jax.nn.gelu(g, approximate=False)
            x = x + h @ w2 + b2
            return x
        key = jax.random.key(seed)
        ks = jax.random.split(key, 6)
        return {'x': jax.random.normal(ks[0], (B, N, DIM), jnp.float32), 'wqkv': jax.random.normal(ks[1], (DEPTH, DIM, 3 * INNER), jnp.float32) * 0.02, 'q_scale': jnp.ones((DEPTH, DIM_HEAD), jnp.float32), 'k_scale': jnp.ones((DEPTH, DIM_HEAD), jnp.float32), 'wo': jax.random.normal(ks[2], (DEPTH, INNER, DIM), jnp.float32) * 0.02, 'ln_g': jnp.ones((DEPTH, DIM), jnp.float32), 'ln_b': jnp.zeros((DEPTH, DIM), jnp.float32), 'w1': jax.random.normal(ks[3], (DEPTH, DIM, 2 * HID), jnp.float32) * 0.02, 'b1': jnp.zeros((DEPTH, 2 * HID), jnp.float32), 'w2': jax.random.normal(ks[4], (DEPTH, HID, DIM), jnp.float32) * 0.02, 'b2': jnp.zeros((DEPTH, DIM), jnp.float32)}
    _L1_ffn_in = _L1_ffn_setup()
    _d = {'L0_attn_x': _L0_attn_in['x'], 'L0_attn_norm_w': _L0_attn_in['norm_w'], 'L0_attn_v_w': _L0_attn_in['v_w'], 'L0_attn_v_b': _L0_attn_in['v_b'], 'L0_attn_mx_w': _L0_attn_in['mx_w'], 'L0_attn_mx_b': _L0_attn_in['mx_b'], 'L0_attn_h_w': _L0_attn_in['h_w'], 'L0_attn_h_b': _L0_attn_in['h_b'], 'L0_attn_gamma': _L0_attn_in['gamma'], 'L0_attn_beta': _L0_attn_in['beta'], 'L0_attn_alpha_rb': _L0_attn_in['alpha_rb'], 'L0_attn_beta_rb': _L0_attn_in['beta_rb'], 'L0_attn_xproj_w': _L0_attn_in['xproj_w'], 'L0_attn_dt_w': _L0_attn_in['dt_w'], 'L0_attn_dt_b': _L0_attn_in['dt_b'], 'L0_attn_A_log': _L0_attn_in['A_log'], 'L0_attn_D_p': _L0_attn_in['D_p'], 'L0_ffn_w_gate': _L0_ffn_in['w_gate'], 'L0_ffn_w_up': _L0_ffn_in['w_up'], 'L0_ffn_w_down': _L0_ffn_in['w_down'], 'L1_attn_Wq': _L1_attn_in['Wq'], 'L1_attn_bq': _L1_attn_in['bq'], 'L1_attn_Wk': _L1_attn_in['Wk'], 'L1_attn_bk': _L1_attn_in['bk'], 'L1_attn_Wv': _L1_attn_in['Wv'], 'L1_attn_bv': _L1_attn_in['bv'], 'L1_attn_Wo': _L1_attn_in['Wo'], 'L1_attn_bo': _L1_attn_in['bo'], 'L1_attn_W_cross': _L1_attn_in['W_cross'], 'L1_attn_shift_weights': _L1_attn_in['shift_weights'], 'L1_attn_gate': _L1_attn_in['gate'], 'L1_ffn_wqkv': _L1_ffn_in['wqkv'], 'L1_ffn_q_scale': _L1_ffn_in['q_scale'], 'L1_ffn_k_scale': _L1_ffn_in['k_scale'], 'L1_ffn_wo': _L1_ffn_in['wo'], 'L1_ffn_ln_g': _L1_ffn_in['ln_g'], 'L1_ffn_ln_b': _L1_ffn_in['ln_b'], 'L1_ffn_w1': _L1_ffn_in['w1'], 'L1_ffn_b1': _L1_ffn_in['b1'], 'L1_ffn_w2': _L1_ffn_in['w2'], 'L1_ffn_b2': _L1_ffn_in['b2']}
    _x0 = _d['L0_attn_x']
    _d['L0_attn_x'] = jax.random.normal(jax.random.fold_in(jax.random.key(seed), 1), (8, 512, 128), dtype=_x0.dtype)
    del _x0
    return _d

def reference(L0_attn_x, L0_attn_norm_w, L0_attn_v_w, L0_attn_v_b, L0_attn_mx_w, L0_attn_mx_b, L0_attn_h_w, L0_attn_h_b, L0_attn_gamma, L0_attn_beta, L0_attn_alpha_rb, L0_attn_beta_rb, L0_attn_xproj_w, L0_attn_dt_w, L0_attn_dt_b, L0_attn_A_log, L0_attn_D_p, L0_ffn_w_gate, L0_ffn_w_up, L0_ffn_w_down, L1_attn_Wq, L1_attn_bq, L1_attn_Wk, L1_attn_bk, L1_attn_Wv, L1_attn_bv, L1_attn_Wo, L1_attn_bo, L1_attn_W_cross, L1_attn_shift_weights, L1_attn_gate, L1_ffn_wqkv, L1_ffn_q_scale, L1_ffn_k_scale, L1_ffn_wo, L1_ffn_ln_g, L1_ffn_ln_b, L1_ffn_w1, L1_ffn_b1, L1_ffn_w2, L1_ffn_b2):

    def _L0_attn_ref(x, norm_w, v_w, v_b, mx_w, mx_b, h_w, h_b, gamma, beta, alpha_rb, beta_rb, xproj_w, dt_w, dt_b, A_log, D_p):
        import math
        import jax, jax.numpy as jnp
        import numpy as np
        EMBED_DIM = 128
        ZDIM = 128
        CHUNK = 256
        DSTATE = 16
        DT_RANK = math.ceil(EMBED_DIM / 16)

        def silu(x):
            return x * jax.nn.sigmoid(x)

        def rmsnorm(x, w, eps=1e-05):
            var = jnp.mean(x * x, axis=-1, keepdims=True)
            return x * jax.lax.rsqrt(var + eps) * w

        def _rotary(v, sin, cos):
            x1, x2 = jnp.split(v, 2, axis=-1)
            return jnp.concatenate([x1 * cos - x2 * sin, x2 * cos + x1 * sin], axis=-1)

        def rel_pos_bias(alpha, beta, n):
            half = ZDIM // 2
            freqs = jnp.exp(jnp.arange(half, dtype=jnp.float32) * (-math.log(10000.0) / half))
            ang = jnp.arange(n, dtype=jnp.float32)[:, None] * freqs[None, :]
            sin, cos = (jnp.sin(ang), jnp.cos(ang))
            a = _rotary(jnp.broadcast_to(alpha, (n, ZDIM)), sin, cos)
            b = _rotary(jnp.broadcast_to(beta, (n, ZDIM)), sin, cos)
            return jnp.einsum('mk,nk->mn', a, b)

        def s6(u, xproj_w, dt_w, dt_b, A_log, D_p):
            x_dbl = u @ xproj_w.T
            dt, Bm, Cm = jnp.split(x_dbl, [DT_RANK, DT_RANK + DSTATE], axis=-1)
            dt = jax.nn.softplus(dt @ dt_w.T + dt_b)
            A = -jnp.exp(A_log)

            def step(h, inp):
                dt_t, B_t, C_t, u_t = inp
                dA = jnp.exp(dt_t[..., None] * A)
                h = dA * h + (dt_t * u_t)[..., None] * B_t[:, None, :]
                y = jnp.einsum('bdn,bn->bd', h, C_t)
                return (h, y)
            B, L, D = u.shape
            h0 = jnp.zeros((B, D, DSTATE), u.dtype)
            xs = (dt.transpose(1, 0, 2), Bm.transpose(1, 0, 2), Cm.transpose(1, 0, 2), u.transpose(1, 0, 2))
            _, ys = jax.lax.scan(step, h0, xs)
            return ys.transpose(1, 0, 2) + u * D_p
        B, L, D = x.shape
        residual = x
        xn = rmsnorm(x, norm_w)
        v = silu(xn @ v_w.T + v_b)
        mx = silu(s6(xn, xproj_w, dt_w, dt_b, A_log, D_p))
        base = mx @ mx_w.T + mx_b
        u, zr, hx = jnp.split(base, [D, D + ZDIM + D], axis=-1)
        u = jax.nn.sigmoid(u)
        zr = silu(zr)
        z, r = jnp.split(zr, [ZDIM], axis=-1)
        z = z[..., None, :] * gamma + beta
        q, k = (z[..., 0, :], z[..., 1, :])
        c = min(CHUNK, L)
        nc = L // c
        qh = q.reshape(B, nc, c, ZDIM) * ZDIM ** (-0.5)
        kh = k.reshape(B, nc, c, ZDIM)
        vh = v.reshape(B, nc, c, D)
        bias = rel_pos_bias(alpha_rb, beta_rb, c)
        mask = jnp.triu(jnp.full((c, c), -jnp.inf, jnp.float32), 1)
        qk = jnp.einsum('bnqz,bnkz->bnqk', qh, kh) + bias + mask
        attn = jax.nn.softmax(qk.astype(jnp.float32), axis=-1).astype(qk.dtype)
        h = jnp.einsum('bnqk,bnkd->bnqd', attn, vh).reshape(B, L, D)
        h = silu(hx + h * r @ h_w.T + h_b)
        return residual + u * (h - residual)

    def _L0_ffn_ref(x, w_gate, w_up, w_down):
        import jax, jax.numpy as jnp
        import numpy as np
        DIM = 128
        HIDDEN = 384
        SCALE = 1.0 / 127.0

        def _dequant(w_int, dtype):
            return w_int.astype(dtype) * jnp.asarray(SCALE, dtype)
        wg = _dequant(w_gate, x.dtype)
        wu = _dequant(w_up, x.dtype)
        wd = _dequant(w_down, x.dtype)
        gate = jnp.einsum('bsd,hd->bsh', x, wg)
        up = jnp.einsum('bsd,hd->bsh', x, wu)
        h = jax.nn.silu(gate) * up
        return jnp.einsum('bsh,dh->bsd', h, wd)

    def _L1_attn_ref(x, Wq, bq, Wk, bk, Wv, bv, Wo, bo, W_cross, shift_weights, gate):
        import jax, jax.numpy as jnp
        import numpy as np
        D_MODEL = 128
        N_HEADS = 16
        HEAD_DIM = D_MODEL // N_HEADS
        MAX_SHIFT = HEAD_DIM // 2
        BATCH, SEQ = (2, 256)

        def _forward(x, Wq, bq, Wk, bk, Wv, bv, Wo, bo, W_cross, shift_weights, gate):
            b, s, _ = x.shape
            H, hd = (W_cross.shape[0], W_cross.shape[1])
            ms = shift_weights.shape[1]
            Q = (x @ Wq.T + bq).reshape(b, s, H, hd)
            K = (x @ Wk.T + bk).reshape(b, s, H, hd)
            V = (x @ Wv.T + bv).reshape(b, s, H, hd)
            Qt = jnp.einsum('bqhf,hfg->bqhg', Q, W_cross)
            scores_cross = jnp.einsum('bqhd,bkhd->bhqk', Qt, K)
            f = jnp.arange(hd)[:, None]
            g = jnp.arange(hd)[None, :]
            tau = g - f
            valid = (tau >= 0) & (tau < ms)
            M = jnp.where(valid[None], shift_weights[:, jnp.clip(tau, 0, ms - 1)], 0.0)
            K_mixed = jnp.einsum('hfg,bkhg->bkhf', M, K)
            scores_conv = jnp.einsum('bqhf,bkhf->bhqk', Q, K_mixed)
            gt = jax.nn.sigmoid(gate).reshape(1, H, 1, 1)
            scale = hd ** (-0.5)
            scores = (gt * scores_cross + (1.0 - gt) * scores_conv) * scale
            causal = jnp.tril(jnp.ones((s, s), dtype=bool))
            scores = jnp.where(causal[None, None], scores, -jnp.inf)
            attn = jax.nn.softmax(scores, axis=-1)
            out = jnp.einsum('bhqk,bkhd->bqhd', attn, V).reshape(b, s, H * hd)
            return out @ Wo.T + bo
        return _forward(x, Wq, bq, Wk, bk, Wv, bv, Wo, bo, W_cross, shift_weights, gate)

    def _L1_ffn_ref(x, wqkv, q_scale, k_scale, wo, ln_g, ln_b, w1, b1, w2, b2):
        import jax, jax.numpy as jnp
        import numpy as np
        DIM = 128
        DEPTH = 2
        HEADS = 8
        DIM_HEAD = 64
        WINDOW = 64
        INNER = HEADS * DIM_HEAD
        HID = int(DIM * 4 * 2 / 3)
        B, N = (2, 1024)
        QK_SCALE = 8.0

        def shift_token(t):
            t1, t2 = jnp.split(t, 2, axis=-1)
            t2 = jnp.pad(t2, ((0, 0), (1, 0), (0, 0)))[:, :-1]
            return jnp.concatenate([t1, t2], axis=-1)

        def l2norm(t):
            return t / jnp.clip(jnp.linalg.norm(t, axis=-1, keepdims=True), 1e-12)

        def rotate_half(x):
            x1, x2 = jnp.split(x, 2, axis=-1)
            return jnp.concatenate([-x2, x1], axis=-1)

        def rotary_xpos(q, k):
            n = q.shape[-2]
            half_idx = jnp.arange(0, DIM_HEAD, 2, dtype=jnp.float32)
            inv_freq = 1.0 / 10000.0 ** (half_idx / DIM_HEAD)
            t = jnp.arange(n, dtype=jnp.float32)
            freqs = t[:, None] * inv_freq[None, :]
            freqs = jnp.concatenate([freqs, freqs], axis=-1)
            base = (half_idx + 0.4 * DIM_HEAD) / (1.4 * DIM_HEAD)
            power = (t - n // 2) / float(WINDOW // 2)
            scale = base[None, :] ** power[:, None]
            scale = jnp.concatenate([scale, scale], axis=-1)
            cos, sin = (jnp.cos(freqs), jnp.sin(freqs))
            q = q * cos * scale + rotate_half(q) * sin * scale
            k = k * cos / scale + rotate_half(k) * sin / scale
            return (q, k)

        def local_attention(q, k, v):
            b, h, n, d = q.shape
            w = n // WINDOW
            bq = q.reshape(b, h, w, WINDOW, d) * QK_SCALE
            bk = k.reshape(b, h, w, WINDOW, d)
            bv = v.reshape(b, h, w, WINDOW, d)

            def look_around(t):
                p = jnp.pad(t, ((0, 0), (0, 0), (1, 0), (0, 0), (0, 0)))
                return jnp.concatenate([p[:, :, :w], p[:, :, 1:]], axis=3)
            bk, bv = (look_around(bk), look_around(bv))
            bt = jnp.arange(n).reshape(w, WINDOW)
            btp = jnp.pad(bt, ((1, 0), (0, 0)), constant_values=-1)
            btk = jnp.concatenate([btp[:w], btp[1:]], axis=1)
            sim = jnp.einsum('bhwid,bhwjd->bhwij', bq, bk)
            i = bt[:, :, None]
            j = btk[:, None, :]
            mask = (i < j) | (i > j + WINDOW) | (j == -1)
            sim = jnp.where(mask, -jnp.finfo(sim.dtype).max, sim)
            attn = jax.nn.softmax(sim, axis=-1)
            out = jnp.einsum('bhwij,bhwjd->bhwid', attn, bv)
            return out.reshape(b, h, n, d)

        def _layer(x, wqkv, qs, ksc, wo, lg, lb, w1, b1, w2, b2):
            b, n, _ = x.shape
            h = shift_token(x)
            qkv = h @ wqkv
            q, k, v = jnp.split(qkv, 3, axis=-1)
            to_heads = lambda t: t.reshape(b, n, HEADS, DIM_HEAD).transpose(0, 2, 1, 3)
            q, k, v = (to_heads(q), to_heads(k), to_heads(v))
            q = l2norm(q) * qs
            k = l2norm(k) * ksc
            q, k = rotary_xpos(q, k)
            o = local_attention(q, k, v)
            o = o.transpose(0, 2, 1, 3).reshape(b, n, INNER)
            x = x + o @ wo
            h = shift_token(x)
            mu = h.mean(-1, keepdims=True)
            var = h.var(-1, keepdims=True)
            h = (h - mu) / jnp.sqrt(var + 1e-05) * lg + lb
            h = h @ w1 + b1
            a, g = jnp.split(h, 2, axis=-1)
            h = a * jax.nn.gelu(g, approximate=False)
            x = x + h @ w2 + b2
            return x
        for l in range(DEPTH):
            x = _layer(x, wqkv[l], q_scale[l], k_scale[l], wo[l], ln_g[l], ln_b[l], w1[l], b1[l], w2[l], b2[l])
        return x
    x = L0_attn_x
    x = x + _layernorm(_L0_attn_ref(_layernorm(x, axis=-1), L0_attn_norm_w, L0_attn_v_w, L0_attn_v_b, L0_attn_mx_w, L0_attn_mx_b, L0_attn_h_w, L0_attn_h_b, L0_attn_gamma, L0_attn_beta, L0_attn_alpha_rb, L0_attn_beta_rb, L0_attn_xproj_w, L0_attn_dt_w, L0_attn_dt_b, L0_attn_A_log, L0_attn_D_p), axis=-1)
    x = x + _layernorm(_L0_ffn_ref(_layernorm(x, axis=-1), L0_ffn_w_gate, L0_ffn_w_up, L0_ffn_w_down), axis=-1)
    x = x + _layernorm(_L1_attn_ref(_layernorm(x, axis=-1), L1_attn_Wq, L1_attn_bq, L1_attn_Wk, L1_attn_bk, L1_attn_Wv, L1_attn_bv, L1_attn_Wo, L1_attn_bo, L1_attn_W_cross, L1_attn_shift_weights, L1_attn_gate), axis=-1)
    x = x + _layernorm(_L1_ffn_ref(_layernorm(x, axis=-1), L1_ffn_wqkv, L1_ffn_q_scale, L1_ffn_k_scale, L1_ffn_wo, L1_ffn_ln_g, L1_ffn_ln_b, L1_ffn_w1, L1_ffn_b1, L1_ffn_w2, L1_ffn_b2), axis=-1)
    return x

_drawn_inputs = setup_inputs


def setup_inputs(seed=0):
    import zlib

    import numpy as np

    out = dict(_drawn_inputs(seed))
    spreads = {'L0_attn_norm_w': (1.0, 0.6),
     'L0_attn_v_b': (0.0, 0.8),
     'L0_attn_mx_b': (0.0, 0.1),
     'L0_attn_h_b': (0.0, 0.293),
     'L0_attn_beta': (0.0, 2.0),
     'L0_attn_dt_b': (-4.599999904632568, 0.6),
     'L0_attn_D_p': (1.0, 0.6),
     'L1_attn_bq': (0.0, 0.8),
     'L1_attn_bk': (0.0, 2.0),
     'L1_attn_bv': (0.0, 0.1),
     'L1_attn_bo': (0.0, 0.1),
     'L1_attn_gate': (0.0, 0.8),
     'L1_ffn_q_scale': (1.0, 0.6),
     'L1_ffn_k_scale': (1.0, 0.6),
     'L1_ffn_ln_g': (1.0, 0.6),
     'L1_ffn_ln_b': (0.0, 0.8),
     'L1_ffn_b1': (0.0, 0.8),
     'L1_ffn_b2': (0.0, 2.0)}
    factors = {'L0_attn_v_w': 8.0,
     'L0_attn_h_w': 8.0,
     'L0_attn_gamma': 64.0,
     'L0_attn_alpha_rb': 25.236,
     'L0_attn_beta_rb': 32.244,
     'L0_attn_xproj_w': 8.0,
     'L0_attn_dt_w': 8.0,
     'L0_attn_A_log': 8.0,
     'L1_attn_Wq': 8.0,
     'L1_attn_Wk': 8.0,
     'L1_attn_W_cross': 8.0,
     'L1_attn_shift_weights': 8.0,
     'L1_ffn_wqkv': 2.956,
     'L1_ffn_wo': 3.069,
     'L1_ffn_w1': 8.0,
     'L1_ffn_w2': 8.0}
    for name, (base, spread) in spreads.items():
        noise = np.random.default_rng([zlib.crc32(name.encode()), seed]).standard_normal(out[name].shape)
        drawn = base * np.exp(spread * noise) if base else spread * noise
        out[name] = jnp.asarray(drawn.astype(out[name].dtype))
    for name, factor in factors.items():
        out[name] = (out[name] * factor).astype(out[name].dtype)
    return out
```

```python
from contextlib import ExitStack
import math

import numpy as np

import concourse.bass as bass
from concourse import mybir

ALU = mybir.AluOpType
ACT = mybir.ActivationFunctionType
AX = mybir.AxisListType
F32 = mybir.dt.float32
BF16 = mybir.dt.bfloat16
I32 = mybir.dt.int32
U16 = mybir.dt.uint16

P = 128
BATCH, SEQ, DIM = 8, 512, 128
NJ = SEQ // P
STREAMS = 2
STATES = 16
RANK = 8
CHUNK = 256
HIDDEN_CHUNKS = 3
HEADS, HEAD_DIM = 16, 8
PAIRS = HEADS // 2
SPLITS = 6
STACK = SPLITS * HEAD_DIM
PARTS = 3
DEPTH, LHEADS, LDIM, WINDOW = 2, 8, 64, 64
INNER = LHEADS * LDIM
HID = 341
HID_ROWS = (128, 128, HID - 256)
EPS = 1e-5
NEG = -1e30
TWO10 = 1024.0
LNEXP = "natural_log_exp_and_others"
SIGMOID = "sigmoid_and_others"
GELU = "gelu_and_others"

COLS = {}
_n = 0
for _name, _w in (("norm_w", 1), ("bz", 1), ("br", 1), ("gamma0", 1), ("gamma1", 1), ("beta0", 1), ("beta1", 1),
                  ("dt_b", 1), ("D_p", 1), ("alpha", 1), ("alpha_sw", 1), ("beta_rb", 1), ("beta_rb_sw", 1),
                  ("bq", 1), ("bk", 1), ("gate", 1), ("lg", 2), ("lb", 2), ("shift", 4), ("W_cross", 8),
                  ("A_log", 16), ("b1a", 6), ("b1g", 6)):
    COLS[_name] = (_n, _n + _w)
    _n += _w
NCOLS = _n
ROWS = {}
_n = 0
for _name, _w in (("v_b", 128), ("bu", 128), ("bhx", 128), ("h_b", 128), ("bv", 128), ("bo", 128), ("b2", 256),
                  ("qs", 128), ("qs_sw", 128), ("ks", 128), ("ks_sw", 128)):
    ROWS[_name] = (_n, _n + _w)
    _n += _w
NROWS = _n
WTS = {}
_n = 0
for _name, _w in (("v_w", 128), ("mx_w", 512), ("h_w", 128), ("bc_w", 96), ("dtl_w", 8), ("dt_w", 128),
                  ("Wq", 128), ("Wk", 128), ("Wv", 128), ("Wo", 128), ("wqkv", 2 * 1536), ("wo", 2 * 512),
                  ("w1", 2 * 2 * HID), ("w2", 2 * 384)):
    WTS[_name] = (_n, _n + _w)
    _n += _w
NWTS = _n
CST = {}
_n = 0
for _name, _w in (("ident", 128), ("mean", 128), ("causal", 128), ("blocks", 128), ("taps", 32),
                  ("eps", 1)):
    CST[_name] = (_n, _n + _w)
    _n += _w
NCST = _n
TAB = {_name: 256 * _i for _i, _name in enumerate(("cos0", "sin0", "qcos", "qsin", "kcos", "ksin"))}
BCST = {}
_n = 0
for _name, _w in (("ident", 128), ("causal", 128), ("causal_T", 128), ("window0", 128), ("window", 128), ("select", 32 * 128)):
    BCST[_name] = (_n, _n + _w)
    _n += _w
NBCST = _n


class PsumRing:

    def __init__(self, psum, slots, done):
        self.psum, self.slots, self.done = psum, slots, done
        self.freed = [[] for _ in range(slots)]
        self.n = 0
        self.groups = 0
        self.where = {}

    def take(self, pe, name, freed_by):
        slot = self.n % self.slots
        self.n += 1
        for s, value in self.freed[slot]:
            pe.wait_ge(s, value)
        self.freed[slot] = freed_by
        self.where[name] = [slot, None]
        return self.psum[:, slot, :]

    def full(self, ins, name):
        self.groups += 1
        self.where[name][1] = self.groups
        ins.then_inc(self.done, 1)

    def read(self, eng, name):
        slot, value = self.where[name]
        eng.wait_ge(self.done, value)
        return self.psum[:, slot, :]


def build(nc, x_d, colp_d, rowp_d, wts_d, ints_d, cst_d, tab_d, bcst_d, ones_d, out_d, iterations=BATCH // STREAMS):
    ctx = ExitStack()
    with ctx:
        def sb(name, shape, dt=F32):
            return ctx.enter_context(nc.sbuf_tensor(name, shape, dt))

        sems = {}

        def sem(name):
            if name not in sems:
                sems[name] = ctx.enter_context(nc.semaphore(name))
            return sems[name]

        split_scratch = nc.dram_tensor("split_scratch", (STREAMS, 2, SPLITS, P, SEQ), BF16, kind="Internal").ap()
        max_scratch = nc.dram_tensor("max_scratch", (STREAMS, PARTS, HEADS, SEQ), BF16, kind="Internal").ap()

        colp = sb("colp", [P, NCOLS])
        rowp = sb("rowp", [P, NROWS])
        wts = sb("wts", [P, NWTS])
        cst = sb("cst", [P, NCST])
        bcst = sb("bcst", [P, NBCST], BF16)
        ffw = sb("ffw", [P, 9, 128])
        arena = sb("arena", [P, STREAMS, 24, SEQ])
        work = sb("work", [P, 16, SEQ])
        v_ext = sb("v_ext", [P, STREAMS, NJ, HEADS, 9])
        v_prev = sb("v_prev", [P, 2, INNER])
        score_bias = sb("score_bias", [P, 384])
        tables = sb("tables", [P, DEPTH, 4, NJ, LDIM])
        mix = sb("mix", [P, P])
        stats = sb("stats", [P, STREAMS, NJ, 6])
        mv = sb("mv", [P, STREAMS, 8, NJ, 2])
        lnv = sb("lnv", [P, STREAMS, 8, NJ])
        rstd = sb("rstd", [P, STREAMS, 8, NJ])
        rms = sb("rms", [P, STREAMS, 6, NJ])
        small = sb("small", [P, 128])
        sm1 = sb("sm1", [P, STREAMS, 4, 4])
        neg_max = sb("neg_max", [P, STREAMS, NJ, HEADS])
        nm_res = sb("nm_res", [P, STREAMS, NJ, HEADS])
        nm_parts = sb("nm_parts", [P, STREAMS, NJ, PARTS * HEADS], BF16)
        nm_cols = sb("nm_cols", [PARTS * HEADS, STREAMS, SEQ], BF16)
        inv_sum = sb("inv_sum", [P, STREAMS, NJ, HEADS])
        ssq = sb("ssq", [P, 2, 2, LHEADS])
        lnss = sb("lnss", [P, 2, 2, LHEADS])
        invn = sb("invn", [P, 4, 2, LHEADS])
        lmax = sb("lmax", [P, 2, LHEADS])
        lsum = sb("lsum", [P, 2, LHEADS])
        psum = ctx.enter_context(nc.psum_tensor("psum", [P, 4, 1024], F32))
        long_acc = psum[:, 3, :]

        def col(name, i=0, rows=P):
            a = COLS[name][0] + i
            return colp[0:rows, a:a + 1]

        def row(name, i=0, w=128):
            a = ROWS[name][0] + i * w
            return rowp[:, a:a + w]

        def row4(name, i=0):
            return row(name, i).unsqueeze(1).to_broadcast([P, NJ, 128])

        def wt(name, a=0, w=128, rows=P):
            a += WTS[name][0]
            return wts[0:rows, a:a + w]

        def const(name, a=0, w=128):
            a += CST[name][0]
            return cst[:, a:a + w]

        def table_in(name):
            return A(1, 0, 3)[:, TAB[name]:TAB[name] + 256]

        def bconst(name, a=0, w=128, rows=P):
            a += BCST[name][0]
            return bcst[0:rows, a:a + w]

        def A(s, i, n=1):
            return arena[:, s, i:i + n, :].rearrange("p a n -> p (a n)")

        def blocks(ap, w=128):
            return ap.rearrange("p (j d) -> p j d", d=w)

        ident = const("ident")
        identb = bconst("ident")
        eps = const("eps", 0, 1)
        ffw_gate, ffw_up, ffw_down = ffw[:, 0:3, :], ffw[:, 3:6, :], ffw[:, 6:9, :]

        with nc.Block() as block:
            @block.sync
            def _(sp):
                loaded = sem("params_loaded")
                sp.dma_start(cst[:, :], cst_d).then_inc(loaded, 16)
                sp.dma_start(bcst[:, :].bitcast(U16), bcst_d).then_inc(loaded, 16)
                sp.dma_start(colp[:, :], colp_d).then_inc(loaded, 16)
                sp.dma_start(rowp[:, :], rowp_d.to_broadcast([P, NROWS])).then_inc(loaded, 16)
                sp.dma_start(A(0, 0, 3)[:, 0:1152].bitcast(I32), ints_d).then_inc(loaded, 16)
                sp.dma_start(wts[:, :], wts_d).then_inc(loaded, 16)
                sp.dma_start(A(1, 0, 3), tab_d).then_inc(loaded, 16)
                sp.wait_ge(loaded, 112)

            @block.gpsimd
            def _(pool):
                nc.gpsimd.memset(v_ext[:, :, :, :, 8:9], 1.0)
                nc.gpsimd.memset(v_prev[:, :, :], 0.0)

            @block.scalar
            def _(act):
                act.wait_ge(sem("params_loaded"), 112)
                nc.scalar.activation(small[:, 0:1], col("gate"), ACT.Sigmoid).then_inc(sem("param_funcs"), 1)
                nc.scalar.activation(small[:, 16:32], colp[:, COLS["A_log"][0]:COLS["A_log"][1]],
                                     ACT.Exp).then_inc(sem("param_funcs"), 1)

            @block.tensor
            def _(pe):
                pe.wait_ge(sem("bias_operands"), 2)
                nc.tensor.matmul(psum[:, 0, 0:128], A(0, 4)[:, 0:128], A(0, 5)[:, 0:128], start=True, stop=True)
                nc.tensor.matmul(psum[:, 0, 128:384], A(0, 4)[:, 128:256], A(0, 5)[:, 0:256], start=True,
                                 stop=True).then_inc(sem("bias_products"), 1)

            @block.vector
            def _(dve):
                steps = [0]

                def step(ins):
                    steps[0] += 1
                    ins.then_inc(sem("param_step"), 1)
                    dve.wait_ge(sem("param_step"), steps[0])

                dve.wait_ge(sem("params_loaded"), 112)
                nc.vector.tensor_scalar(A(0, 6)[:, 0:256], table_in("sin0"), col("alpha_sw"), None, ALU.mult)
                step(nc.vector.tensor_scalar(A(0, 7)[:, 0:256], table_in("sin0"), col("beta_rb_sw"), None, ALU.mult))
                nc.vector.scalar_tensor_tensor(out=A(0, 4)[:, 0:256], in0=table_in("cos0"), scalar=col("alpha"),
                                               in1=A(0, 6)[:, 0:256], op0=ALU.mult, op1=ALU.add).then_inc(sem("bias_operands"), 1)
                nc.vector.scalar_tensor_tensor(out=A(0, 5)[:, 0:256], in0=table_in("cos0"), scalar=col("beta_rb"),
                                               in1=A(0, 7)[:, 0:256], op0=ALU.mult, op1=ALU.add).then_inc(sem("bias_operands"), 1)
                step(nc.vector.tensor_scalar(ffw[:, :, :].rearrange("p a n -> p (a n)"), A(0, 0, 3)[:, 0:1152].bitcast(I32),
                                             1.0 / 127.0, None, ALU.mult))
                for name in ("gamma0", "beta0"):
                    step(nc.vector.tensor_scalar(col(name), col(name), 128 ** -0.5, None, ALU.mult))
                step(nc.vector.tensor_tensor(row("h_b"), row("h_b"), row("bhx"), ALU.add))
                for l in range(DEPTH):
                    for t, (tab, vec, f) in enumerate((("qcos", "qs", 8.0 * TWO10), ("qsin", "qs_sw", 8.0 * TWO10),
                                                       ("kcos", "ks", TWO10), ("ksin", "ks_sw", TWO10))):
                        scale = row(vec, l, 64).unsqueeze(1).to_broadcast([P, NJ, LDIM])
                        nc.vector.scalar_tensor_tensor(out=tables[:, l, t, :, :], in0=blocks(table_in(tab), LDIM),
                                                       scalar=f, in1=scale, op0=ALU.mult, op1=ALU.mult)
                dve.wait_ge(sem("param_funcs"), 2)
                A_log = colp[:, COLS["A_log"][0]:COLS["A_log"][1]]
                step(nc.vector.tensor_scalar(A_log, small[:, 16:32], -1.0, None, ALU.mult))
                s8 = HEAD_DIM ** -0.5
                nc.vector.tensor_scalar(small[:, 1:2], small[:, 0:1], s8, None, ALU.mult)
                step(nc.vector.tensor_scalar(small[:, 2:3], small[:, 0:1], -s8, s8, ALU.mult, ALU.add))
                W = colp[:, COLS["W_cross"][0]:COLS["W_cross"][1]]
                step(nc.vector.tensor_scalar(small[:, 32:40], const("taps", 0, 8), col("shift"), None, ALU.mult))
                for tau in range(1, 4):
                    step(nc.vector.scalar_tensor_tensor(out=small[:, 32:40], in0=const("taps", 8 * tau, 8),
                                                        scalar=col("shift", tau), in1=small[:, 32:40],
                                                        op0=ALU.mult, op1=ALU.add))
                step(nc.vector.tensor_scalar(small[:, 40:48], small[:, 32:40], small[:, 2:3], None, ALU.mult))
                step(nc.vector.scalar_tensor_tensor(out=small[:, 48:56], in0=W, scalar=small[:, 1:2],
                                                    in1=small[:, 40:48], op0=ALU.mult, op1=ALU.add))
                step(nc.vector.tensor_tensor(blocks(mix[:, :], 8), blocks(const("blocks"), 8),
                                             small[:, 48:56].unsqueeze(1).to_broadcast([P, HEADS, 8]), ALU.mult))
                dve.wait_ge(sem("bias_products"), 1)
                step(nc.vector.tensor_copy(score_bias[:, :], psum[:, 0, 0:384]))
                for a in (0, 256):
                    step(nc.vector.tensor_tensor(score_bias[:, a:a + 128], score_bias[:, a:a + 128], const("causal"), ALU.add))

        x_v = x_d.rearrange("(i s) (j p) d -> i s p j d", s=STREAMS, p=P)
        out_v = out_d.rearrange("(i s) (j p) d -> i s p j d", s=STREAMS, p=P)
        layernorms = STREAMS
        units = [(s, j) for s in range(STREAMS) for j in range(NJ)]

        def moves(l, u):
            s, j = units[u]
            return ((3, 4)[j % 2]) * (l * STREAMS + s) + (1, 2, 3, 4)[j]

        X0, X1, X2, X3 = 0, 1, 0, 1
        XR, RES, XRT, VAL, DT, DTU = 1, 2, 3, 4, 5, 6
        SPZ, SPE, SPU, SPL, BCR, BCS, DTLOW, VB, VSIG = 7, 8, 9, 10, 11, 12, 13, 14, 15
        YD, YSIG, MX, ZSIG, RSIG, ZF, RF, QF, KF, UB, USIG, SB, PROB_T = 7, 8, 9, 10, 11, 12, 13, 14, 15, 16, 17, 18, 20
        HR, HB, HSIG, HO, HN = 5, 6, 10, 8, 22
        FXN, FXNT, FSIG, FG, FH, FO = 2, 3, 4, 7, 10, 13
        AXN, AXNT, QT, QRES, KRES, QPARTS, KPARTS, QSTK, KSTK, AO, AOT, AOUT = 2, 3, 4, 5, 6, 7, 18, 10, 14, 4, 5, 6
        YA, Y1, YB, HT, LQT, LKT, LV = 2, 3, 23, 4, 6, 10, 14
        LP, LPT, LOT = 18, 20, 22
        HT2, CEN, SQF, RLN, HNT, HGB, GG, HH = 4, 5, 6, 7, 8, 9, 10, 13
        W_DA, W_DBU, W_H, W_HC = 0, 3, 5, 7

        loop = nc.Fori(0, iterations)
        it = ctx.enter_context(loop)
        sems_before = dict(sems)
        sems.clear()
        body = nc.Block()
        with body as block:
            ring = PsumRing(psum, 3, sem("products"))

            @block.tensor
            def _(pe):
                take, full = ring.take, ring.full
                mm = nc.tensor.matmul

                def transposes(name, s, src, ready, freed):
                    pe.wait_ge(*ready)
                    ps = take(pe, (name, s), freed)
                    for j in range(NJ):
                        ins = nc.tensor.transpose(ps[:, j * 128:(j + 1) * 128], src[:, j * 128:(j + 1) * 128], ident)
                    full(ins, (name, s))

                for s in range(STREAMS):
                    transposes("xrT", s, A(s, XR), (sem("xr"), s + 1), [(sem("xrT"), s + 1)])
                for s in range(STREAMS):
                    pe.wait_ge(sem("xrT"), s + 1)
                    u = A(s, XRT)
                    ps = take(pe, ("bcdt", s), [(sem("bc_low"), s + 1), (sem("dt_low"), s + 1)])
                    mm(ps[0:96, 0:512], wt("bc_w", 0, 96), u, start=True, stop=True)
                    full(mm(ps[0:RANK, 512:1024], wt("dtl_w", 0, RANK), u, start=True, stop=True), ("bcdt", s))
                for s in range(STREAMS):
                    pe.wait_ge(sem("dt_low"), s + 1)
                    ps = take(pe, ("dt", s), [(sem("sp_z"), s + 1)])
                    full(mm(ps[:, 0:512], wt("dt_w", rows=RANK), A(s, DTLOW)[0:RANK, :], start=True, stop=True), ("dt", s))
                    ps = take(pe, ("v", s), [(sem("v_raw"), s + 1)])
                    for j in range(NJ):
                        ins = mm(ps[:, j * 128:(j + 1) * 128], A(s, XRT)[:, j * 128:(j + 1) * 128], wt("v_w"),
                                 start=True, stop=True)
                    full(ins, ("v", s))
                for s in range(STREAMS):
                    pe.wait_ge(sem("bc_parts"), s + 1)
                    parts = A(s, BCS).bitcast(BF16)[0:96, 0:512]
                    for n in range(STATES + 1):
                        i = s * STATES + n
                        if n < STATES:
                            ps = take(pe, ("bc", s, n), [(sem("hc"), i + 1)])
                            mm(ps[:, 0:512], bconst("select", n * 128, rows=96), parts, start=True, stop=True)
                            full(mm(ps[:, 512:1024], bconst("select", (16 + n) * 128, rows=96), parts,
                                    start=True, stop=True), ("bc", s, n))
                        if n > 0:
                            pe.wait_ge(sem("hc"), i)
                            mm(long_acc[:, s * 512:(s + 1) * 512], ident, work[:, W_HC + (i - 1) % 2, :],
                               start=(n == 1), stop=(n == STATES)).then_inc(sem("y_products"), 1)
                for s in range(STREAMS):
                    pe.wait_ge(sem("mx"), s + 1)
                    m = A(s, MX)
                    ps = take(pe, ("zr", s), [(sem("z"), s + 1), (sem("r"), s + 1)])
                    mm(ps[:, 0:512], wt("mx_w", 128), m, start=True, stop=True)
                    full(mm(ps[:, 512:1024], wt("mx_w", 256), m, start=True, stop=True), ("zr", s))
                    ps = take(pe, ("u", s), [(sem("u_raw"), s + 1)])
                    for j in range(NJ):
                        ins = mm(ps[:, j * 128:(j + 1) * 128], m[:, j * 128:(j + 1) * 128], wt("mx_w", 0), start=True, stop=True)
                    full(ins, ("u", s))
                for s in range(STREAMS):
                    pe.wait_ge(sem("qk_cols"), 2 * (s + 1))
                    ps = take(pe, ("scores", s), [(sem("scores_biased"), s + 1)])
                    q, k = A(s, QF), A(s, KF)
                    for c in range(2):
                        a = c * CHUNK
                        mm(ps[:, c * 512:c * 512 + 128], q[:, a:a + 128], k[:, a:a + 128], start=True, stop=True)
                        ins = mm(ps[:, c * 512 + 128:c * 512 + 384], q[:, a + 128:a + 256], k[:, a:a + 256],
                                 start=True, stop=True)
                    full(ins, ("scores", s))
                for s in range(STREAMS):
                    pe.wait_ge(sem("probs"), s + 1)
                    ps = take(pe, ("probsT", s), [(sem("probsT"), s + 1)])
                    p = A(s, SB, 2)
                    for c in range(2):
                        for i in range(3):
                            ins = nc.tensor.transpose(ps[:, c * 512 + i * 128:c * 512 + (i + 1) * 128],
                                                      p[:, c * 384 + i * 128:c * 384 + (i + 1) * 128], ident)
                    full(ins, ("probsT", s))
                for s in range(STREAMS):
                    pe.wait_ge(sem("probsT"), s + 1)
                    pe.wait_ge(sem("v_rows"), s + 1)
                    ps = take(pe, ("av", s), [(sem("hr"), s + 1)])
                    v, pt = A(s, VAL), A(s, PROB_T, 2)
                    for c in range(2):
                        mm(ps[:, c * 256:c * 256 + 128], v[:, c * 256:c * 256 + 128], pt[:, c * 384:c * 384 + 128],
                           start=True, stop=True)
                        mm(ps[:, c * 256 + 128:c * 256 + 256], v[:, c * 256:c * 256 + 128],
                           pt[:, c * 384 + 128:c * 384 + 256], start=True, stop=False)
                        ins = mm(ps[:, c * 256 + 128:c * 256 + 256], v[:, c * 256 + 128:c * 256 + 256],
                                 pt[:, c * 384 + 256:c * 384 + 384], start=False, stop=True)
                    full(ins, ("av", s))
                for s in range(STREAMS):
                    pe.wait_ge(sem("hr"), s + 1)
                    ps = take(pe, ("h", s), [(sem("h_raw"), s + 1)])
                    for j in range(NJ):
                        b = slice(j * 128, (j + 1) * 128)
                        mm(ps[:, b], A(s, MX)[:, b], wt("mx_w", 384), start=True, stop=False)
                        ins = mm(ps[:, b], A(s, HR)[:, b], wt("h_w"), start=False, stop=True)
                    full(ins, ("h", s))
                for s in range(STREAMS):
                    transposes("fxT", s, A(s, FXN), (sem("fxn"), s + 1), [(sem("fxT"), s + 1)])
                for s in range(STREAMS):
                    pe.wait_ge(sem("fxT"), s + 1)
                    for c in range(HIDDEN_CHUNKS):
                        ps = take(pe, ("gu", s, c), [(sem("fh"), s * 3 + c + 1)])
                        mm(ps[:, 0:512], ffw_gate[:, c, :], A(s, FXNT), start=True, stop=True)
                        full(mm(ps[:, 512:1024], ffw_up[:, c, :], A(s, FXNT), start=True, stop=True), ("gu", s, c))
                for s in range(STREAMS):
                    pe.wait_ge(sem("fh"), 3 * (s + 1))
                    ps = take(pe, ("down", s), [(sem("fo"), s + 1)])
                    for j in range(NJ):
                        for c in range(HIDDEN_CHUNKS):
                            ins = mm(ps[:, j * 128:(j + 1) * 128], A(s, FH + c)[:, j * 128:(j + 1) * 128], ffw_down[:, c, :],
                                     start=(c == 0), stop=(c == 2))
                    full(ins, ("down", s))
                for s in range(STREAMS):
                    transposes("axT", s, A(s, AXN), (sem("axn"), s + 1), [(sem("axT"), s + 1)])
                for s in range(STREAMS):
                    pe.wait_ge(sem("axT"), s + 1)
                    ps = take(pe, ("QK", s), [(sem("QT"), s + 1), (sem("k_parts"), s + 1)])
                    mm(ps[:, 0:512], wt("Wq"), A(s, AXNT), start=True, stop=True)
                    full(mm(ps[:, 512:1024], wt("Wk"), A(s, AXNT), start=True, stop=True), ("QK", s))
                    ps = take(pe, ("V", s), [(sem("v_ext"), s + 1)])
                    for j in range(NJ):
                        ins = mm(ps[:, j * 128:(j + 1) * 128], A(s, AXNT)[:, j * 128:(j + 1) * 128], wt("Wv"),
                                 start=True, stop=True)
                    full(ins, ("V", s))
                    pe.wait_ge(sem("QT"), s + 1)
                    ps = take(pe, ("QG", s), [(sem("q_parts"), s + 1)])
                    full(mm(ps[:, 0:512], mix[:, :], A(s, QT), start=True, stop=True), ("QG", s))
                def stack(s, i, e, rows):
                    t = A(s, i, 4).bitcast(BF16).rearrange("p (a n) -> p a n", a=PAIRS)
                    return t[e * 64:e * 64 + rows]

                for s in range(STREAMS):
                    pe.wait_ge(sem(f"stacked{s}"), 16 * 6)
                    for j in range(NJ):
                        keys = (j + 1) * 128
                        for p in range(PAIRS):
                            i = (s * NJ + j) * PAIRS + p
                            ps = take(pe, ("s1", s, j, p), [(sem("row_max"), i + 1)])
                            for e in range(2):
                                mm(ps[:, e * 512:e * 512 + keys], stack(s, QSTK, e, STACK)[:, p, j * 128:keys],
                                   stack(s, KSTK, e, STACK)[:, p, 0:keys], start=True, stop=False)
                            for e in range(2):
                                ins = mm(ps[:, e * 512 + j * 128:e * 512 + keys], identb, bconst("causal"), start=False, stop=True)
                            full(ins, ("s1", s, j, p))
                for s in range(STREAMS):
                    pe.wait_ge(sem("nm_parts"), s + 1)
                    ps = take(pe, ("nmT", s), [(sem("nm_cols"), s + 1)])
                    for j in range(NJ):
                        ins = nc.tensor.transpose(ps.bitcast(BF16)[0:PARTS * HEADS, j * 128:(j + 1) * 128], nm_parts[:, s, j, :], identb)
                    full(ins, ("nmT", s))
                for s in range(STREAMS):
                    pe.wait_ge(sem(f"maxima_stacked{s}"), 32)
                    if s > 0:
                        pe.wait_ge(sem("ao"), s)
                    else:
                        pe.wait_ge(sem("yd"), STREAMS)

                    def values(p):
                        pe.wait_ge(sem("exps"), NJ * (s * PAIRS + p + 1))
                        pt = work[:, 8 * (p % 2):8 * (p % 2) + 8, :].rearrange("p (k e) n -> p k e n", e=2)
                        for e in range(2):
                            h = e * PAIRS + p
                            for j in range(NJ):
                                o = (j // 2) * 512 + (j % 2) * 144 + h * 9
                                for jk in range(j + 1):
                                    ins = mm(long_acc[:, o:o + 9], pt[:, jk, e, (j - jk) * 128:(j - jk + 1) * 128],
                                             v_ext[:, s, jk, h, :], start=(jk == 0), stop=(jk == j))
                        ins.then_inc(sem("value_products"), 1)

                    for p in range(PAIRS):
                        for jk in range(NJ):
                            w = SEQ - jk * 128
                            i = (s * PAIRS + p) * NJ + jk
                            ps = take(pe, ("s2", s, p, jk), [(sem("exps"), i + 1)])
                            for e in range(2):
                                mm(ps[:, e * 512:e * 512 + w], stack(s, KSTK, e, STACK + PARTS)[:, p, jk * 128:(jk + 1) * 128],
                                   stack(s, QSTK, e, STACK + PARTS)[:, p, jk * 128:SEQ], start=True, stop=False)
                            for e in range(2):
                                ins = mm(ps[:, e * 512:e * 512 + 128], identb, bconst("causal_T"), start=False, stop=True)
                            full(ins, ("s2", s, p, jk))
                        if p > 0:
                            values(p - 1)
                    values(PAIRS - 1)
                for s in range(STREAMS):
                    transposes("aoT", s, A(s, AO), (sem("ao"), s + 1), [(sem("aoT"), s + 1)])
                for s in range(STREAMS):
                    pe.wait_ge(sem("aoT"), s + 1)
                    ps = take(pe, ("proj", s), [(sem("aout"), s + 1)])
                    for j in range(NJ):
                        ins = mm(ps[:, j * 128:(j + 1) * 128], A(s, AOT)[:, j * 128:(j + 1) * 128], wt("Wo"), start=True, stop=True)
                    full(ins, ("proj", s))
                for l in range(DEPTH):
                    ls = l * STREAMS
                    for s in range(STREAMS):
                        transposes(("yT", l), s, A(s, YA if l == 0 else YB), (sem("y_in"), ls + s + 1),
                                   [(sem("shift_a"), ls + s + 1), (sem("shift_b"), ls + s + 1)])
                    lu = l * len(units)
                    wq = WTS["wqkv"][0] + l * 1536

                    def qkv(u):
                        s, j = units[u]
                        if j == 0:
                            pe.wait_ge(sem("shift_a"), ls + s + 1)
                            pe.wait_ge(sem("shift_b"), ls + s + 1)
                        lhs = A(s, HT)[:, j * 128:(j + 1) * 128]
                        ps = take(pe, ("lqk", l, u), [(sem("squares"), 2 * (lu + u + 1)), (sem("turned"), 2 * (lu + u + 1))])
                        mm(ps[:, 0:512], lhs, wts[:, wq:wq + 512], start=True, stop=True)
                        full(mm(ps[:, 512:1024], lhs, wts[:, wq + 512:wq + 1024], start=True, stop=True), ("lqk", l, u))
                        ps = take(pe, ("lv", l, u), [(sem("lv"), lu + u + 1)])
                        full(mm(ps[:, 0:512], lhs, wts[:, wq + 1024:wq + 1536], start=True, stop=True), ("lv", l, u))

                    def qk_transposes(u):
                        pe.wait_ge(sem("rotated"), 2 * (lu + u + 1))
                        ps = take(pe, ("lqkT", l, u), [(sem("lqT"), lu + u + 1), (sem("lkT"), lu + u + 1)])
                        for t in range(2):
                            src = work[:, 8 * (u % 2) + 6 + t, :]
                            for g in range(4):
                                a = t * 512 + g * 128
                                ins = nc.tensor.transpose(ps[:, a:a + 128], src[:, g * 128:(g + 1) * 128], ident)
                        full(ins, ("lqkT", l, u))

                    def window_scores(u):
                        s, j = units[u]
                        pe.wait_ge(sem("lqT"), lu + u + 1)
                        pe.wait_ge(sem("lkT"), lu + u + 1)
                        ps = take(pe, ("ls", l, u), [(sem("lexp"), lu + u + 1)])
                        q = A(s, LQT, 4).rearrange("p (g n) -> p g n", g=4)
                        k = A(s, LKT, 4).rearrange("p (g n) -> p g n", g=4)
                        mask = bconst("window0" if j == 0 else "window").unsqueeze(1).to_broadcast([P, 4, 128])
                        t = j * 128
                        for e in range(2):
                            mm(blocks(ps[:, e * 512:(e + 1) * 512]), identb, mask, start=True, stop=True, skip_group_check=True)
                        for g in range(4):
                            for e in range(2):
                                r = slice(e * 64, (e + 1) * 64)
                                o = e * 512 + g * 128
                                mm(ps[0:64, o:o + 64], q[r, g, t:t + 64], k[r, g, t:t + 64], start=False, stop=True,
                                   skip_group_check=True)
                                if j > 0:
                                    mm(ps[0:64, o + 64:o + 128], q[r, g, t:t + 64], k[r, g, t - 64:t], start=False, stop=True,
                                       skip_group_check=True)
                                ins = mm(ps[64:128, o:o + 128], q[r, g, t + 64:t + 128], k[r, g, t:t + 128],
                                         start=False, stop=True, skip_group_check=True)
                        full(ins, ("ls", l, u))

                    def prob_transposes(u):
                        pe.wait_ge(sem("lprobs"), lu + u + 1)
                        ps = take(pe, ("lpT", l, u), [(sem("lpT_a"), lu + u + 1), (sem("lpT_b"), lu + u + 1)])
                        p = A(u % 2, LP, 2)
                        for i in range(LHEADS):
                            ins = nc.tensor.transpose(ps[:, i * 128:(i + 1) * 128], p[:, i * 128:(i + 1) * 128], ident)
                        full(ins, ("lpT", l, u))

                    def window_values(u):
                        s, j = units[u]
                        pe.wait_ge(sem("lpT_a"), lu + u + 1)
                        pe.wait_ge(sem("lpT_b"), lu + u + 1)
                        pe.wait_ge(sem(f"v_moved{u % 2}"), 16 * moves(l, u))
                        ps = take(pe, ("lo", l, u), [(sem("lo"), lu + u + 1)])
                        pt = A(u % 2, LPT, 2)
                        for g in range(4):
                            for e in range(2):
                                r = slice(e * 64, (e + 1) * 64)
                                h = (2 * g + e) * 64
                                c = (e * 4 + g) * 128
                                mm(ps[r, g * 128:g * 128 + 64], v_prev[:, u % 2, h:h + 64], pt[:, c:c + 64], start=True, stop=True)
                                ins = mm(ps[r, g * 128 + 64:g * 128 + 128], A(s, LV + j)[:, h:h + 64], pt[:, c + 64:c + 128],
                                         start=True, stop=True)
                        full(ins, ("lo", l, u))

                    def window_project(u):
                        pe.wait_ge(sem("lo"), lu + u + 1)
                        ps = take(pe, ("lproj", l, u), [(sem("y1"), lu + u + 1)])
                        for g in range(4):
                            ins = mm(ps[:, 0:128], A(u % 2, LOT)[:, g * 128:(g + 1) * 128], wt("wo", l * 512 + g * 128),
                                     start=(g == 0), stop=(g == 3))
                        full(ins, ("lproj", l, u))

                    stages = (qkv, qk_transposes, window_scores, prob_transposes, window_values, window_project)
                    for t in range(len(units) + len(stages) - 1):
                        for d, stage in enumerate(stages):
                            if 0 <= t - d < len(units):
                                stage(t - d)
                    for s in range(STREAMS):
                        transposes(("y1T", l), s, A(s, Y1), (sem("y1"), lu + NJ * (s + 1)),
                                   [(sem("shift2_a"), ls + s + 1), (sem("shift2_b"), ls + s + 1)])
                    for s in range(STREAMS):
                        pe.wait_ge(sem("shift2_a"), ls + s + 1)
                        pe.wait_ge(sem("shift2_b"), ls + s + 1)
                        ps = take(pe, ("mean", l, s), [(sem("centred"), ls + s + 1)])
                        full(mm(ps[:, 0:512], const("mean"), A(s, HT2), start=True, stop=True), ("mean", l, s))
                    for s in range(STREAMS):
                        pe.wait_ge(sem("centred_sq"), ls + s + 1)
                        ps = take(pe, ("var", l, s), [(sem("var_ln"), ls + s + 1)])
                        full(mm(ps[:, 0:512], const("mean"), A(s, SQF), start=True, stop=True), ("var", l, s))
                    for s in range(STREAMS):
                        pe.wait_ge(sem("hgb"), ls + s + 1)
                        for c in range(HIDDEN_CHUNKS):
                            m = HID_ROWS[c]
                            ps = take(pe, ("ag", l, s, c), [(sem("hh"), 3 * (ls + s) + c + 1)])
                            a = l * 2 * HID + c * 128
                            mm(ps[0:m, 0:512], wt("w1", a, m), A(s, HGB), start=True, stop=True)
                            full(mm(ps[0:m, 512:1024], wt("w1", a + HID, m), A(s, HGB), start=True, stop=True), ("ag", l, s, c))
                    for s in range(STREAMS):
                        pe.wait_ge(sem("hh"), 3 * (ls + s + 1))
                        ps = take(pe, ("w2", l, s), [(sem("y_raw"), ls + s + 1)])
                        for j in range(NJ):
                            for c in range(HIDDEN_CHUNKS):
                                m = HID_ROWS[c]
                                ins = mm(ps[:, j * 128:(j + 1) * 128], A(s, HH + c)[0:m, j * 128:(j + 1) * 128],
                                         wt("w2", l * 384 + c * 128, rows=m), start=(c == 0), stop=(c == 2))
                        full(ins, ("w2", l, s))

            @block.vector
            def _(dve):
                steps = [0]

                def step(ins):
                    steps[0] += 1
                    ins.then_inc(sem("dve_step"), 1)

                def settle():
                    dve.wait_ge(sem("dve_step"), steps[0])

                tt, ts, stt = nc.vector.tensor_tensor, nc.vector.tensor_scalar, nc.vector.scalar_tensor_tensor

                def ln_stats(k, s, src):
                    for j in range(NJ):
                        step(nc.vector.bn_stats(stats[:, s, j, :], src[:, j * 128:(j + 1) * 128]))
                    settle()
                    for j in range(NJ):
                        ins = nc.vector.bn_aggr(mv[:, s, k, j, :], stats[:, s, j, :])
                    ins.then_inc(sem("ln_var"), 1)

                def ln_apply(k, s, src, dst, scale=None, signal=None):
                    for j in range(NJ):
                        ins = ts(dst[:, j * 128:(j + 1) * 128], src[:, j * 128:(j + 1) * 128], mv[:, s, k, j, 0:1],
                                 (rstd[:, s, k, :] if scale is None else scale)[:, j:j + 1], ALU.subtract, ALU.mult)
                        if signal is None:
                            step(ins)
                    if signal is not None:
                        ins.then_inc(signal, 1)

                def ln_ready(k, s):
                    dve.wait_ge(sem("ln_rstd"), k * STREAMS + s + 1)

                for s in range(STREAMS):
                    dve.wait_ge(sem(f"x_loaded{s}"), 16)
                    ln_stats(0, s, A(s, X0))
                for s in range(STREAMS):
                    ln_ready(0, s)
                    dve.wait_ge(sem("ln_var"), s + 1)
                    r = rstd[:, s, 0, :]
                    step(tt(rms[:, s, 0, :], r, r, ALU.mult))
                    settle()
                    tt(rms[:, s, 1, :], rms[:, s, 0, :], mv[:, s, 0, :, 1], ALU.mult).then_inc(sem("mean_sq"), 1)
                    ln_apply(0, s, A(s, X0), A(s, RES))
                for s in range(STREAMS):
                    dve.wait_ge(sem("rms"), s + 1)
                    step(tt(rms[:, s, 4, :], rms[:, s, 3, :], rstd[:, s, 0, :], ALU.mult))
                    settle()
                    ln_apply(0, s, A(s, X0), A(s, XR), rms[:, s, 4, :], sem("xr"))
                for s in range(STREAMS):
                    ps = ring.read(dve, ("bcdt", s))
                    dve.wait_ge(sem("bc_high"), s + 1)
                    bcs = A(s, BCS).bitcast(BF16)[:, 0:512]
                    tmp = A(s, BCS).bitcast(BF16)[:, 512:1024]
                    res = A(s, BCR)
                    tt(res[0:96, :], ps[0:96, 0:512], bcs[0:96, :], ALU.subtract).then_inc(sem("bc_low"), 1)
                    dve.wait_ge(sem("bc_low"), s + 1)
                    step(nc.vector.tensor_copy(bcs[32:64, :], res[32:64, :]))
                    step(nc.vector.tensor_copy(tmp[64:96, :], res[64:96, :]))
                    settle()
                    tt(bcs[64:96, :], res[64:96, :], tmp[64:96, :], ALU.subtract).then_inc(sem("bc_parts"), 1)
                for s in range(STREAMS):
                    ps = ring.read(dve, ("dt", s))
                    ts(A(s, SPZ), ps[:, 0:512], col("dt_b"), None, ALU.add).then_inc(sem("sp_z"), 1)
                    ps = ring.read(dve, ("v", s))
                    tt(blocks(A(s, VB)), blocks(ps[:, 0:512]), row4("v_b"), ALU.add).then_inc(sem("v_raw"), 1)
                for s in range(STREAMS):
                    dve.wait_ge(sem("sp_exp"), s + 1)
                    ts(A(s, SPU), A(s, SPE), 1.0, None, ALU.add).then_inc(sem("sp_1pe"), 1)
                    dve.wait_ge(sem("sp_1pe"), s + 1)
                    step(stt(out=A(s, SPE), in0=A(s, SPU), scalar=1.0, in1=A(s, SPE), op0=ALU.subtract, op1=ALU.subtract))
                    step(nc.vector.reciprocal(A(s, DTU), A(s, SPU)))
                    settle()
                    step(tt(A(s, SPE), A(s, SPE), A(s, DTU), ALU.mult))
                    dve.wait_ge(sem("sp_ln"), s + 1)
                    settle()
                    step(tt(A(s, SPL), A(s, SPL), A(s, SPE), ALU.subtract))
                    settle()
                    stt(out=A(s, DT), in0=A(s, SPZ), scalar=0.0, in1=A(s, SPL), op0=ALU.max, op1=ALU.add).then_inc(sem("dt"), 1)
                    dve.wait_ge(sem("dt"), s + 1)
                    tt(A(s, DTU), A(s, DT), A(s, XRT), ALU.mult).then_inc(sem("dtu"), 1)
                for s in range(STREAMS):
                    dve.wait_ge(sem("dtu"), s + 1)

                    def drive(n):
                        i = s * STATES + n
                        ps = ring.read(dve, ("bc", s, n))
                        if i >= 2:
                            dve.wait_ge(sem("h"), i - 1)
                        tt(work[:, W_DBU + i % 2, :], A(s, DTU), ps[:, 0:512], ALU.mult).then_inc(sem("dbu"), 1)

                    drive(0)
                    for n in range(STATES):
                        i = s * STATES + n
                        dve.wait_ge(sem("da"), i + 1)
                        dve.wait_ge(sem("dbu"), i + 1)
                        if i >= 2:
                            dve.wait_ge(sem("hc"), i - 1)
                        nc.vector.tensor_tensor_scan(work[:, W_H + i % 2, :], work[:, W_DA + i % 3, :], work[:, W_DBU + i % 2, :],
                                                     0.0, ALU.mult, ALU.add).then_inc(sem("h"), 1)
                        if n + 1 < STATES:
                            drive(n + 1)
                        ps = ring.read(dve, ("bc", s, n))
                        if i >= 2:
                            dve.wait_ge(sem("y_products"), i - 1)
                        dve.wait_ge(sem("h"), i + 1)
                        tt(work[:, W_HC + i % 2, :], work[:, W_H + i % 2, :], ps[:, 512:1024], ALU.mult).then_inc(sem("hc"), 1)
                    dve.wait_ge(sem("y_products"), STATES * (s + 1))
                    stt(out=A(s, YD), in0=A(s, XRT), scalar=col("D_p"), in1=long_acc[:, s * 512:(s + 1) * 512],
                        op0=ALU.mult, op1=ALU.add).then_inc(sem("yd"), 1)
                for s in range(STREAMS):
                    dve.wait_ge(sem("y_sig"), s + 1)
                    dve.wait_ge(sem("yd"), s + 1)
                    tt(A(s, MX), A(s, YD), A(s, YSIG), ALU.mult).then_inc(sem("mx"), 1)
                for s in range(STREAMS):
                    dve.wait_ge(sem("v_sig"), s + 1)
                    tt(A(s, VAL), A(s, VB), A(s, VSIG), ALU.mult).then_inc(sem("v_rows"), 1)
                for s in range(STREAMS):
                    ps = ring.read(dve, ("zr", s))
                    dve.wait_ge(sem("z_sig"), s + 1)
                    stt(out=A(s, ZF), in0=ps[:, 0:512], scalar=col("bz"), in1=A(s, ZSIG), op0=ALU.add,
                        op1=ALU.mult).then_inc(sem("z"), 1)
                    dve.wait_ge(sem("r_sig"), s + 1)
                    dve.wait_ge(sem("z"), s + 1)
                    dve.wait_ge(sem("v_rows"), STREAMS)
                    ts(A(s, QF), A(s, ZF), col("gamma0"), col("beta0"), ALU.mult, ALU.add).then_inc(sem("qk_cols"), 1)
                    ts(A(s, KF), A(s, ZF), col("gamma1"), col("beta1"), ALU.mult, ALU.add).then_inc(sem("qk_cols"), 1)
                    stt(out=A(s, RF), in0=ps[:, 512:1024], scalar=col("br"), in1=A(s, RSIG), op0=ALU.add,
                        op1=ALU.mult).then_inc(sem("r"), 1)
                    ps = ring.read(dve, ("u", s))
                    tt(blocks(A(s, UB)), blocks(ps[:, 0:512]), row4("bu"), ALU.add).then_inc(sem("u_raw"), 1)
                for s in range(STREAMS):
                    ps = ring.read(dve, ("scores", s))
                    sbv = A(s, SB, 2)[:, 0:768].rearrange("p (c n) -> p c n", c=2)
                    tt(sbv, ps.rearrange("p (c n) -> p c n", c=2)[:, :, 0:384],
                       score_bias[:, :].unsqueeze(1).to_broadcast([P, 2, 384]), ALU.add).then_inc(sem("scores_biased"), 1)
                    dve.wait_ge(sem("scores_biased"), s + 1)
                    step(nc.vector.tensor_reduce(sm1[:, s, 0, 0:2], sbv[:, :, 0:128], AX.X, ALU.max, negate=True))
                    nc.vector.tensor_reduce(sm1[:, s, 0, 2:4], sbv[:, :, 128:384], AX.X, ALU.max,
                                            negate=True).then_inc(sem("score_max"), 1)
                for s in range(STREAMS):
                    dve.wait_ge(sem("score_exp"), s + 1)
                    step(nc.vector.reciprocal(sm1[:, s, 2, :], sm1[:, s, 1, :]))
                    settle()
                    for c in range(2):
                        ts(A(s, SB, 2)[:, c * 384:c * 384 + 128], A(s, SB, 2)[:, c * 384:c * 384 + 128],
                           sm1[:, s, 2, c:c + 1], None, ALU.mult)
                        ins = ts(A(s, SB, 2)[:, c * 384 + 128:c * 384 + 384], A(s, SB, 2)[:, c * 384 + 128:c * 384 + 384],
                                 sm1[:, s, 2, 2 + c:3 + c], None, ALU.mult)
                    ins.then_inc(sem("probs"), 1)
                for s in range(STREAMS):
                    ps = ring.read(dve, ("av", s))
                    dve.wait_ge(sem("r"), s + 1)
                    tt(A(s, HR), ps[:, 0:512], A(s, RF), ALU.mult).then_inc(sem("hr"), 1)
                for s in range(STREAMS):
                    ps = ring.read(dve, ("h", s))
                    tt(blocks(A(s, HB)), blocks(ps[:, 0:512]), row4("h_b"), ALU.add).then_inc(sem("h_raw"), 1)
                for s in range(STREAMS):
                    dve.wait_ge(sem("h_sig"), s + 1)
                    dve.wait_ge(sem("h_raw"), s + 1)
                    step(tt(A(s, HO), A(s, HB), A(s, HSIG), ALU.mult))
                    settle()
                    step(tt(A(s, HO), A(s, HO), A(s, RES), ALU.subtract))
                    settle()
                    step(tt(A(s, HO), A(s, HO), A(s, USIG), ALU.mult))
                    settle()
                    step(tt(A(s, HO), A(s, HO), A(s, RES), ALU.add))
                    settle()
                    ln_stats(1, s, A(s, HO))

                def sublayer_end(k, s, src, x_old, x_new):
                    ln_ready(k, s)
                    dve.wait_ge(sem("ln_var"), k * STREAMS + s + 1)
                    ln_apply(k, s, src, A(s, HN))
                    settle()
                    step(tt(A(s, x_new), A(s, x_old), A(s, HN), ALU.add))
                    settle()
                    ln_stats(k + 1, s, A(s, x_new))

                for s in range(STREAMS):
                    sublayer_end(1, s, A(s, HO), X0, X1)
                for s in range(STREAMS):
                    ln_ready(2, s)
                    dve.wait_ge(sem("ln_var"), 2 * STREAMS + s + 1)
                    ln_apply(2, s, A(s, X1), A(s, FXN), None, sem("fxn"))
                for s in range(STREAMS):
                    for c in range(HIDDEN_CHUNKS):
                        ps = ring.read(dve, ("gu", s, c))
                        dve.wait_ge(sem("f_sig"), s * 3 + c + 1)
                        step(tt(A(s, FG + c), ps[:, 0:512], A(s, FSIG + c), ALU.mult))
                        settle()
                        tt(A(s, FH + c), ps[:, 512:1024], A(s, FG + c), ALU.mult).then_inc(sem("fh"), 1)
                for s in range(STREAMS):
                    ps = ring.read(dve, ("down", s))
                    nc.vector.tensor_copy(A(s, FO), ps[:, 0:512]).then_inc(sem("fo"), 1)
                    dve.wait_ge(sem("fo"), s + 1)
                    ln_stats(3, s, A(s, FO))
                for s in range(STREAMS):
                    sublayer_end(3, s, A(s, FO), X1, X2)
                for s in range(STREAMS):
                    ln_ready(4, s)
                    dve.wait_ge(sem("ln_var"), 4 * STREAMS + s + 1)
                    ln_apply(4, s, A(s, X2), A(s, AXN), None, sem("axn"))
                def parts(s, i):
                    return A(s, i, 2).bitcast(BF16).rearrange("p (c n) -> p c n", n=512)

                for s in range(STREAMS):
                    ps = ring.read(dve, ("QK", s))
                    kp = parts(s, KPARTS)
                    dve.wait_ge(sem("k_high"), s + 1)
                    stt(out=A(s, KRES), in0=ps[:, 512:1024], scalar=col("bk"), in1=kp[:, 0, :], op0=ALU.add,
                        op1=ALU.subtract).then_inc(sem("k_parts"), 1)
                    dve.wait_ge(sem("k_parts"), s + 1)
                    step(nc.vector.tensor_copy(kp[:, 1, :], A(s, KRES)))
                    settle()
                    tt(kp[:, 2, :], A(s, KRES), kp[:, 1, :], ALU.subtract).then_inc(sem("k_split"), 1)
                    ps = ring.read(dve, ("V", s))
                    for j in range(NJ):
                        ins = tt(v_ext[:, s, j, :, 0:8], blocks(ps[:, j * 128:(j + 1) * 128], 8), blocks(row("bv"), 8), ALU.add)
                    ins.then_inc(sem("v_ext"), 1)
                    ps = ring.read(dve, ("QG", s))
                    qp = parts(s, QPARTS)
                    dve.wait_ge(sem("q_high"), s + 1)
                    tt(A(s, QRES), ps[:, 0:512], qp[:, 0, :], ALU.subtract).then_inc(sem("q_parts"), 1)
                    dve.wait_ge(sem("q_parts"), s + 1)
                    step(nc.vector.tensor_copy(qp[:, 1, :], A(s, QRES)))
                    settle()
                    tt(qp[:, 2, :], A(s, QRES), qp[:, 1, :], ALU.subtract).then_inc(sem("q_split"), 1)
                for s in range(STREAMS):
                    nm = neg_max[:, s, :, :].rearrange("p j (e a) -> p j e a", e=2)
                    for j in range(NJ):
                        for p in range(PAIRS):
                            ps = ring.read(dve, ("s1", s, j, p))
                            nc.vector.tensor_reduce(nm[:, j, :, p], ps.rearrange("p (e n) -> p e n", e=2)[:, :, 0:(j + 1) * 128],
                                                    AX.X, ALU.max, negate=True).then_inc(sem("row_max"), 1)
                    dve.wait_ge(sem("row_max"), NJ * PAIRS * (s + 1))
                    nmp = nm_parts[:, s, :, :].rearrange("p j (c h) -> p j c h", c=PARTS)
                    step(nc.vector.tensor_copy(nmp[:, :, 0, :], neg_max[:, s, :, :]))
                    settle()
                    step(tt(nm_res[:, s, :, :], neg_max[:, s, :, :], nmp[:, :, 0, :], ALU.subtract))
                    settle()
                    step(nc.vector.tensor_copy(nmp[:, :, 1, :], nm_res[:, s, :, :]))
                    settle()
                    tt(nmp[:, :, 2, :], nm_res[:, s, :, :], nmp[:, :, 1, :], ALU.subtract).then_inc(sem("nm_parts"), 1)
                for s in range(STREAMS):
                    dve.wait_ge(sem("value_products"), PAIRS * (s + 1))
                    o = long_acc.rearrange("p (b n) -> p b n", b=2)[:, :, 0:288].rearrange("p b (j h d) -> p b j h d", j=2, d=9)
                    for b in range(2):
                        step(nc.vector.reciprocal(inv_sum[:, s, 2 * b:2 * b + 2, :], o[:, b, :, :, 8]))
                    settle()
                    ao = A(s, AO).rearrange("p (j h d) -> p j h d", j=NJ, d=8)
                    for j in range(NJ):
                        ins = tt(ao[:, j, :, :], o[:, j // 2, j % 2, :, 0:8], inv_sum[:, s, j, :].unsqueeze(2).to_broadcast([P, HEADS, 8]), ALU.mult)
                    ins.then_inc(sem("ao"), 1)
                for s in range(STREAMS):
                    ps = ring.read(dve, ("proj", s))
                    tt(blocks(A(s, AOUT)), blocks(ps[:, 0:512]), row4("bo"), ALU.add).then_inc(sem("aout"), 1)
                    dve.wait_ge(sem("aout"), s + 1)
                    ln_stats(5, s, A(s, AOUT))
                for s in range(STREAMS):
                    sublayer_end(5, s, A(s, AOUT), X2, X3)
                for s in range(STREAMS):
                    ln_ready(6, s)
                    dve.wait_ge(sem("ln_var"), 6 * STREAMS + s + 1)
                    ln_apply(6, s, A(s, X3), A(s, YA), None, sem("y_in"))
                for l in range(DEPTH):
                    ls = l * STREAMS
                    lu = l * len(units)
                    for s in range(STREAMS):
                        ps = ring.read(dve, (("yT", l), s))
                        step(nc.vector.memset(A(s, HT)[64:128, 0:1], 0.0))
                        nc.vector.tensor_copy(A(s, HT)[64:128, 1:512], ps[64:128, 0:511]).then_inc(sem("shift_b"), 1)

                    def rotate(u):
                        s, j = units[u]
                        ps = ring.read(dve, ("lqk", l, u))
                        if lu + u >= 2:
                            dve.wait_ge(sem("rotated"), 2 * (lu + u - 1))
                        else:
                            dve.wait_ge(sem("value_products"), PAIRS * STREAMS)
                        w = 8 * (u % 2)
                        for t in range(2):
                            v = ps[:, t * 512:(t + 1) * 512].rearrange("p (h d) -> p h d", d=LDIM)
                            cos = tables[:, l, 2 * t, j, :].unsqueeze(1).to_broadcast([P, LHEADS, LDIM])
                            sin = tables[:, l, 2 * t + 1, j, :]
                            t1 = work[:, w + 2 + 2 * t, :].rearrange("p (h d) -> p h d", d=LDIM)
                            t2 = work[:, w + 3 + 2 * t, :].rearrange("p (h d) -> p h d", d=LDIM)
                            if t == 1:
                                dve.wait_ge(sem("squares"), 2 * (lu + u) + 1)
                            tt(t1, v, cos, ALU.mult)
                            tt(t2[:, :, 0:32], v[:, :, 32:64], sin[:, 0:32].unsqueeze(1).to_broadcast([P, LHEADS, 32]), ALU.mult)
                            ins = tt(t2[:, :, 32:64], v[:, :, 0:32], sin[:, 32:64].unsqueeze(1).to_broadcast([P, LHEADS, 32]), ALU.mult)
                            ins.then_inc(sem("turned"), 1)
                        dve.wait_ge(sem("squares"), 2 * (lu + u + 1))
                        if lu + u >= 2:
                            dve.wait_ge(sem("inv_norm"), lu + u - 1)
                        step(nc.vector.tensor_reduce(ssq[:, u % 2, :, :], work[:, w:w + 2, :].rearrange("p t (h d) -> p t h d", d=LDIM),
                                                     AX.X, ALU.add))
                        settle()
                        ts(ssq[:, u % 2, :, :], ssq[:, u % 2, :, :], 1e-24, None, ALU.max).then_inc(sem("sum_sq"), 1)

                    def key_evac(u):
                        s, j = units[u]
                        ps = ring.read(dve, ("lqkT", l, u))
                        k = A(s, LKT, 4).rearrange("p (g n) -> p g n", g=4)
                        nc.vector.tensor_copy(k[:, :, j * 128:(j + 1) * 128], blocks(ps[:, 512:1024])).then_inc(sem("lkT"), 1)

                    def maxima(u):
                        ps = ring.read(dve, ("ls", l, u))
                        b = u % 2
                        if lu + u >= 2:
                            dve.wait_ge(sem("lexp"), lu + u - 1)
                        step(nc.vector.tensor_reduce(lmax[:, b, :], ps.rearrange("p (i n) -> p i n", n=128), AX.X, ALU.max, negate=True))
                        settle()
                        inv_q = invn[:, u % 4, 0, :].rearrange("p (g e) -> p e g", e=2)
                        m = lmax[:, b, :].rearrange("p (e g) -> p e g", e=2)
                        tt(m, m, inv_q, ALU.mult).then_inc(sem("lbias"), 1)
                        dve.wait_ge(sem("lexp"), lu + u + 1)
                        nc.vector.reciprocal(lsum[:, b, :], lsum[:, b, :]).then_inc(sem("linv"), 1)

                    def probs_evac(u):
                        ps = ring.read(dve, ("lpT", l, u))
                        nc.vector.tensor_copy(A(u % 2, LPT + 1), ps[:, 512:1024]).then_inc(sem("lpT_b"), 1)

                    def nothing(u):
                        pass

                    def add_project(u):
                        s, j = units[u]
                        ps = ring.read(dve, ("lproj", l, u))
                        b = slice(j * 128, (j + 1) * 128)
                        tt(A(s, Y1)[:, b], A(s, YA if l == 0 else YB)[:, b], ps[:, 0:128], ALU.add).then_inc(sem("y1"), 1)

                    stages = (rotate, key_evac, maxima, probs_evac, nothing, add_project)
                    for t in range(len(units) + len(stages) - 1):
                        for d, stage in enumerate(stages):
                            if 0 <= t - d < len(units):
                                stage(t - d)
                    for s in range(STREAMS):
                        ps = ring.read(dve, (("y1T", l), s))
                        step(nc.vector.memset(A(s, HT2)[64:128, 0:1], 0.0))
                        nc.vector.tensor_copy(A(s, HT2)[64:128, 1:512], ps[64:128, 0:511]).then_inc(sem("shift2_b"), 1)
                    for s in range(STREAMS):
                        ps = ring.read(dve, ("mean", l, s))
                        dve.wait_ge(sem("shift2_a"), ls + s + 1)
                        dve.wait_ge(sem("shift2_b"), ls + s + 1)
                        tt(A(s, CEN), A(s, HT2), ps[:, 0:512], ALU.subtract).then_inc(sem("centred"), 1)
                    for s in range(STREAMS):
                        dve.wait_ge(sem("var_rstd"), ls + s + 1)
                        dve.wait_ge(sem("centred"), ls + s + 1)
                        step(tt(A(s, HNT), A(s, CEN), A(s, RLN), ALU.mult))
                        settle()
                        ts(A(s, HGB), A(s, HNT), col("lg", l), col("lb", l), ALU.mult, ALU.add).then_inc(sem("hgb"), 1)
                    for s in range(STREAMS):
                        for c in range(HIDDEN_CHUNKS):
                            m = HID_ROWS[c]
                            ps = ring.read(dve, ("ag", l, s, c))
                            dve.wait_ge(sem("gelu"), 3 * (ls + s) + c + 1)
                            stt(out=A(s, HH + c)[0:m, :], in0=ps[0:m, 0:512], scalar=col("b1a", 3 * l + c, m), in1=A(s, GG + c)[0:m, :],
                                op0=ALU.add, op1=ALU.mult).then_inc(sem("hh"), 1)
                    for s in range(STREAMS):
                        ps = ring.read(dve, ("w2", l, s))
                        y = A(s, YB if l == 0 else YA)
                        tt(blocks(y), blocks(ps[:, 0:512]), row4("b2", l), ALU.add).then_inc(sem("y_raw"), 1)
                        dve.wait_ge(sem("y_raw"), ls + s + 1)
                        ins = tt(y, y, A(s, Y1), ALU.add)
                        if l + 1 < DEPTH:
                            ins.then_inc(sem("y_in"), 1)
                        else:
                            step(ins)
                            settle()
                            ln_stats(7, s, y)
                for s in range(STREAMS):
                    ln_ready(7, s)
                    dve.wait_ge(sem("ln_var"), 7 * STREAMS + s + 1)
                    ln_apply(7, s, A(s, YA), A(s, HN))
                    settle()
                    tt(A(s, HT), A(s, X3), A(s, HN), ALU.add).then_inc(sem("out"), 1)

            @block.scalar
            def _(act):
                steps = [0]

                def step(ins):
                    steps[0] += 1
                    ins.then_inc(sem("act_step"), 1)

                def settle():
                    act.wait_ge(sem("act_step"), steps[0])

                fn = nc.scalar.activation
                table = nc.scalar.preload_act_table_set

                def ln_rstd(k, s):
                    act.wait_ge(sem("ln_var"), k * STREAMS + s + 1)
                    step(fn(lnv[:, s, k, :], mv[:, s, k, :, 1], ACT.Ln, bias=eps))
                    settle()
                    fn(rstd[:, s, k, :], lnv[:, s, k, :], ACT.Exp, scale=-0.5).then_inc(sem("ln_rstd"), 1)

                table(LNEXP)
                for s in range(STREAMS):
                    ln_rstd(0, s)
                for s in range(STREAMS):
                    act.wait_ge(sem("mean_sq"), s + 1)
                    step(fn(rms[:, s, 2, :], rms[:, s, 1, :], ACT.Ln, bias=eps))
                    settle()
                    fn(rms[:, s, 3, :], rms[:, s, 2, :], ACT.Exp, scale=-0.5).then_inc(sem("rms"), 1)
                for s in range(STREAMS):
                    ps = ring.read(act, ("xrT", s))
                    fn(A(s, XRT), ps[:, 0:512], ACT.Copy, scale=col("norm_w")).then_inc(sem("xrT"), 1)
                for s in range(STREAMS):
                    ps = ring.read(act, ("bcdt", s))
                    fn(A(s, DTLOW)[0:RANK, :], ps[0:RANK, 512:1024], ACT.Copy).then_inc(sem("dt_low"), 1)
                    fn(A(s, BCS).bitcast(BF16)[0:96, 0:512], ps[0:96, 0:512], ACT.Copy).then_inc(sem("bc_high"), 1)
                for s in range(STREAMS):
                    act.wait_ge(sem("sp_z"), s + 1)
                    step(fn(A(s, SPE), A(s, SPZ), ACT.Abs))
                    settle()
                    fn(A(s, SPE), A(s, SPE), ACT.Exp, scale=-1.0).then_inc(sem("sp_exp"), 1)
                for s in range(STREAMS):
                    act.wait_ge(sem("sp_1pe"), s + 1)
                    fn(A(s, SPL), A(s, SPU), ACT.Ln).then_inc(sem("sp_ln"), 1)
                for s in range(STREAMS):
                    act.wait_ge(sem("dt"), s + 1)
                    for n_ in range(STATES):
                        i = s * STATES + n_
                        if i >= 3:
                            act.wait_ge(sem("h"), i - 2)
                        fn(work[:, W_DA + i % 3, :], A(s, DT), ACT.Exp, scale=col("A_log", n_)).then_inc(sem("da"), 1)
                table(SIGMOID)
                for s in range(STREAMS):
                    act.wait_ge(sem("yd"), s + 1)
                    fn(A(s, YSIG), A(s, YD), ACT.Sigmoid).then_inc(sem("y_sig"), 1)
                for s in range(STREAMS):
                    act.wait_ge(sem("v_raw"), s + 1)
                    fn(A(s, VSIG), A(s, VB), ACT.Sigmoid).then_inc(sem("v_sig"), 1)
                for s in range(STREAMS):
                    ps = ring.read(act, ("zr", s))
                    fn(A(s, ZSIG), ps[:, 0:512], ACT.Sigmoid, bias=col("bz")).then_inc(sem("z_sig"), 1)
                    fn(A(s, RSIG), ps[:, 512:1024], ACT.Sigmoid, bias=col("br")).then_inc(sem("r_sig"), 1)
                for s in range(STREAMS):
                    act.wait_ge(sem("u_raw"), s + 1)
                    step(fn(A(s, USIG), A(s, UB), ACT.Sigmoid))
                table(LNEXP)
                for s in range(STREAMS):
                    act.wait_ge(sem("score_max"), s + 1)
                    p = A(s, SB, 2)
                    for c in range(2):
                        for a, (lo, hi) in enumerate(((0, 128), (128, 384))):
                            v = p[:, c * 384 + lo:c * 384 + hi]
                            ins = fn(v, v, ACT.Exp, bias=sm1[:, s, 0, 2 * a + c:2 * a + c + 1],
                                     accum_out=sm1[:, s, 1, 2 * a + c:2 * a + c + 1])
                    ins.then_inc(sem("score_exp"), 1)
                for s in range(STREAMS):
                    ps = ring.read(act, ("probsT", s))
                    fn(A(s, PROB_T, 2)[:, 0:768].rearrange("p (c n) -> p c n", c=2),
                       ps.rearrange("p (c n) -> p c n", c=2)[:, :, 0:384], ACT.Copy).then_inc(sem("probsT"), 1)
                table(SIGMOID)
                for s in range(STREAMS):
                    act.wait_ge(sem("h_raw"), s + 1)
                    settle()
                    fn(A(s, HSIG), A(s, HB), ACT.Sigmoid).then_inc(sem("h_sig"), 1)
                table(LNEXP)
                for k in (1, 2):
                    for s in range(STREAMS):
                        ln_rstd(k, s)
                for s in range(STREAMS):
                    ps = ring.read(act, ("fxT", s))
                    fn(A(s, FXNT), ps[:, 0:512], ACT.Copy).then_inc(sem("fxT"), 1)
                table(SIGMOID)
                for s in range(STREAMS):
                    for c in range(HIDDEN_CHUNKS):
                        ps = ring.read(act, ("gu", s, c))
                        fn(A(s, FSIG + c), ps[:, 0:512], ACT.Sigmoid).then_inc(sem("f_sig"), 1)
                table(LNEXP)
                for k in (3, 4):
                    for s in range(STREAMS):
                        ln_rstd(k, s)
                for s in range(STREAMS):
                    ps = ring.read(act, ("axT", s))
                    fn(A(s, AXNT), ps[:, 0:512], ACT.Copy).then_inc(sem("axT"), 1)
                for s in range(STREAMS):
                    ps = ring.read(act, ("QK", s))
                    fn(A(s, QT), ps[:, 0:512], ACT.Identity, bias=col("bq")).then_inc(sem("QT"), 1)
                    fn(A(s, KPARTS, 2).bitcast(BF16)[:, 0:512], ps[:, 512:1024], ACT.Identity, bias=col("bk")).then_inc(sem("k_high"), 1)
                    ps = ring.read(act, ("QG", s))
                    fn(A(s, QPARTS, 2).bitcast(BF16)[:, 0:512], ps[:, 0:512], ACT.Copy).then_inc(sem("q_high"), 1)
                for s in range(STREAMS):
                    ps = ring.read(act, ("nmT", s))
                    fn(nm_cols[:, s, :], ps.bitcast(BF16)[0:PARTS * HEADS, 0:512], ACT.Copy).then_inc(sem("nm_cols"), 1)
                for s in range(STREAMS):
                    for p in range(PAIRS):
                        i = s * PAIRS + p
                        if i >= 2:
                            act.wait_ge(sem("value_products"), i - 1)
                        pt = work[:, 8 * (p % 2):8 * (p % 2) + 8, :].rearrange("p (k e) n -> p k e n", e=2)
                        for jk in range(NJ):
                            ps = ring.read(act, ("s2", s, p, jk))
                            w = SEQ - jk * 128
                            fn(pt[:, jk, :, 0:w], ps.rearrange("p (e n) -> p e n", e=2)[:, :, 0:w], ACT.Exp).then_inc(sem("exps"), 1)
                for s in range(STREAMS):
                    ps = ring.read(act, ("aoT", s))
                    fn(A(s, AOT), ps[:, 0:512], ACT.Copy).then_inc(sem("aoT"), 1)
                for k in (5, 6):
                    for s in range(STREAMS):
                        ln_rstd(k, s)
                for l in range(DEPTH):
                    ls = l * STREAMS
                    lu = l * len(units)
                    for s in range(STREAMS):
                        ps = ring.read(act, (("yT", l), s))
                        fn(A(s, HT)[0:64, :], ps[0:64, 0:512], ACT.Copy).then_inc(sem("shift_a"), 1)

                    def squares(u):
                        s, j = units[u]
                        ps = ring.read(act, ("lqk", l, u))
                        if lu + u >= 2:
                            act.wait_ge(sem("sum_sq"), lu + u - 1)
                        w = 8 * (u % 2)
                        for t in (1, 0):
                            if t == 0:
                                act.wait_ge(sem("turned"), 2 * (lu + u) + 1)
                            fn(work[:, w + t, :], ps[:, t * 512:(t + 1) * 512], ACT.Square).then_inc(sem("squares"), 1)
                        ps = ring.read(act, ("lv", l, u))
                        fn(A(s, LV + j), ps[:, 0:512], ACT.Copy).then_inc(sem("lv"), 1)
                        act.wait_ge(sem("sum_sq"), lu + u + 1)
                        step(fn(lnss[:, u % 2, :, :], ssq[:, u % 2, :, :], ACT.Ln, scale=TWO10 * TWO10))
                        settle()
                        if lu + u >= 4:
                            act.wait_ge(sem("lexp"), lu + u - 3)
                            act.wait_ge(sem("rotated"), 2 * (lu + u - 3))
                        fn(invn[:, u % 4, :, :], lnss[:, u % 2, :, :], ACT.Exp, scale=-0.5).then_inc(sem("inv_norm"), 1)

                    def query_evac(u):
                        s, j = units[u]
                        ps = ring.read(act, ("lqkT", l, u))
                        q = A(s, LQT, 4).rearrange("p (g n) -> p g n", g=4)
                        fn(q[:, :, j * 128:(j + 1) * 128], blocks(ps[:, 0:512]), ACT.Copy).then_inc(sem("lqT"), 1)

                    def exps(u):
                        ps = ring.read(act, ("ls", l, u))
                        b = u % 2
                        act.wait_ge(sem("lbias"), lu + u + 1)
                        act.wait_ge(sem("inv_norm"), lu + u + 1)
                        if lu + u >= 2:
                            act.wait_ge(sem("lprobs"), lu + u - 1)
                            act.wait_ge(sem("lpT_b"), lu + u - 1)
                            act.wait_ge(sem("lpT_a"), lu + u - 1)
                        pr = A(b, LP, 2)
                        for e in range(2):
                            for g in range(4):
                                i = e * 4 + g
                                ins = fn(pr[:, i * 128:(i + 1) * 128], ps[:, i * 128:(i + 1) * 128], ACT.Exp,
                                         bias=lmax[:, b, i:i + 1], scale=invn[:, u % 4, 0, 2 * g + e:2 * g + e + 1],
                                         accum_out=lsum[:, b, i:i + 1])
                        ins.then_inc(sem("lexp"), 1)

                    def probs_evac(u):
                        ps = ring.read(act, ("lpT", l, u))
                        if lu + u >= 2:
                            act.wait_ge(sem("lo"), lu + u - 1)
                        fn(A(u % 2, LPT), ps[:, 0:512], ACT.Copy).then_inc(sem("lpT_a"), 1)

                    def output_evac(u):
                        ps = ring.read(act, ("lo", l, u))
                        if lu + u >= 2:
                            act.wait_ge(sem("y1"), lu + u - 1)
                        fn(A(u % 2, LOT), ps[:, 0:512], ACT.Copy).then_inc(sem("lo"), 1)

                    def nothing(u):
                        pass

                    stages = (squares, query_evac, exps, probs_evac, output_evac, nothing)
                    for t in range(len(units) + len(stages) - 1):
                        for d, stage in enumerate(stages):
                            if 0 <= t - d < len(units):
                                stage(t - d)
                    for s in range(STREAMS):
                        ps = ring.read(act, (("y1T", l), s))
                        fn(A(s, HT2)[0:64, :], ps[0:64, 0:512], ACT.Copy).then_inc(sem("shift2_a"), 1)
                    for s in range(STREAMS):
                        act.wait_ge(sem("centred"), ls + s + 1)
                        fn(A(s, SQF), A(s, CEN), ACT.Square).then_inc(sem("centred_sq"), 1)
                    for s in range(STREAMS):
                        ps = ring.read(act, ("var", l, s))
                        fn(A(s, RLN), ps[:, 0:512], ACT.Ln, bias=eps).then_inc(sem("var_ln"), 1)
                        act.wait_ge(sem("var_ln"), ls + s + 1)
                        fn(A(s, RLN), A(s, RLN), ACT.Exp, scale=-0.5).then_inc(sem("var_rstd"), 1)
                    table(GELU)
                    for s in range(STREAMS):
                        for c in range(HIDDEN_CHUNKS):
                            m = HID_ROWS[c]
                            ps = ring.read(act, ("ag", l, s, c))
                            fn(A(s, GG + c)[0:m, :], ps[0:m, 512:1024], ACT.Gelu, bias=col("b1g", 3 * l + c, m)).then_inc(sem("gelu"), 1)
                    table(LNEXP)
                for s in range(STREAMS):
                    ln_rstd(7, s)

            @block.gpsimd
            def _(pool):
                for l in range(DEPTH):
                    lu = l * len(units)

                    def combine(u):
                        w = 8 * (u % 2)
                        pool.wait_ge(sem("turned"), 2 * (lu + u + 1))
                        if lu + u >= 2:
                            pool.wait_ge(sem("lkT"), lu + u - 1)
                            pool.wait_ge(sem("lqT"), lu + u - 1)
                        nc.gpsimd.tensor_tensor(work[:, w + 6, :], work[:, w + 2, :], work[:, w + 3, :],
                                                ALU.add).then_inc(sem("rotated"), 1)
                        nc.gpsimd.tensor_tensor(work[:, w + 4, :], work[:, w + 4, :], work[:, w + 5, :],
                                                ALU.add).then_inc(sem("k_sum"), 1)
                        pool.wait_ge(sem("k_sum"), lu + u + 1)
                        pool.wait_ge(sem("inv_norm"), lu + u + 1)
                        nc.gpsimd.tensor_tensor(work[:, w + 7, :].rearrange("p (h d) -> p h d", d=LDIM),
                                                work[:, w + 4, :].rearrange("p (h d) -> p h d", d=LDIM),
                                                invn[:, u % 4, 1, :].unsqueeze(2).to_broadcast([P, LHEADS, LDIM]),
                                                ALU.mult).then_inc(sem("rotated"), 1)

                    def normalise(u):
                        pool.wait_ge(sem("linv"), lu + u + 1)
                        pr = A(u % 2, LP, 2).rearrange("p (i n) -> p i n", n=128)
                        nc.gpsimd.tensor_tensor(pr, pr, lsum[:, u % 2, :].unsqueeze(2).to_broadcast([P, LHEADS, 128]),
                                                ALU.mult).then_inc(sem("lprobs"), 1)

                    for t in range(len(units) + 2):
                        if t < len(units):
                            combine(t)
                        if t >= 2:
                            normalise(t - 2)

            @block.sync
            def _(sp):
                for s in range(STREAMS):
                    sp.dma_start(blocks(A(s, X0)), x_v[bass.ds(it, 1), s].rearrange("a p j d -> (a p) j d")).then_inc(sem(f"x_loaded{s}"), 16)
                for s in range(STREAMS):
                    for t, (order, name, src, dst) in enumerate((((0, 0, 0, 1, 1, 2), "q", QPARTS, QSTK), ((0, 1, 2, 0, 1, 0), "k", KPARTS, KSTK))):
                        sp.wait_ge(sem(name + "_split"), s + 1)
                        part = A(s, src, 2).bitcast(BF16).rearrange("p (c n) -> p c n", n=512)
                        for c, i in enumerate(order):
                            sp.dma_start(split_scratch[s, t, c].rearrange("(f h) n -> h f n", f=8), part[:, i, :]).then_inc(sem(f"spilled{s}"), 16)
                    sp.wait_ge(sem(f"spilled{s}"), 16 * 12)
                    for t, dst in enumerate((QSTK, KSTK)):
                        st = A(s, dst, 4).bitcast(BF16).rearrange("p (a n) -> p a n", a=PAIRS)
                        for e in range(2):
                            sp.dma_start(st[e * 64:e * 64 + STACK],
                                         split_scratch[s, t].rearrange("c (f e a) n -> e (c f) a n", e=2, a=PAIRS)[e]).then_inc(sem(f"stacked{s}"), 16)
                            if t == 1:
                                sp.dma_start(st[e * 64 + STACK:e * 64 + STACK + PARTS].bitcast(U16), ones_d).then_inc(sem(f"stacked{s}"), 16)
                for s in range(STREAMS):
                    sp.wait_ge(sem("nm_cols"), s + 1)
                    sp.dma_start(max_scratch[s].rearrange("c h n -> (c h) n"), nm_cols[:, s, :]).then_inc(sem(f"max_spilled{s}"), 16)
                    sp.wait_ge(sem(f"max_spilled{s}"), 16)
                    st = A(s, QSTK, 4).bitcast(BF16).rearrange("p (a n) -> p a n", a=PAIRS)
                    for e in range(2):
                        sp.dma_start(st[e * 64 + STACK:e * 64 + STACK + PARTS], max_scratch[s, :, e * PAIRS:(e + 1) * PAIRS, :]).then_inc(sem(f"maxima_stacked{s}"), 16)
                for l in range(DEPTH):
                    lu = l * len(units)
                    for u, (s, j) in enumerate(units):
                        sp.wait_ge(sem("lv"), lu + u + 1)
                        if lu + u >= 2:
                            sp.wait_ge(sem("lo"), lu + u - 1)
                        sp.dma_start(v_prev[0:64, u % 2, :], A(s, LV + j)[0:64, :]).then_inc(sem(f"v_moved{u % 2}"), 16)
                        if j > 0:
                            sp.dma_start(v_prev[64:128, u % 2, :], A(s, LV + j - 1)[64:128, :]).then_inc(sem(f"v_moved{u % 2}"), 16)
                for s in range(STREAMS):
                    sp.wait_ge(sem("out"), s + 1)
                    sp.dma_start(out_v[bass.ds(it, 1), s].rearrange("a p j d -> (a p) j d"), blocks(A(s, HT))).then_inc(sem("stored"), 16)
                sp.wait_ge(sem("stored"), 16 * STREAMS)
        for handle in list(sems.values()):
            nc.vector.sem_clear(handle)
        nc.all_engine_barrier()
    return nc


def pack(inp):
    f = {k: np.asarray(v) for k, v in inp.items()}
    a, w, g = "L0_attn_", "L1_attn_", "L1_ffn_"

    def column(v):
        return np.ascontiguousarray(v).reshape(P, -1)

    def padded(v):
        out = np.zeros((P, v.shape[1]), np.float32)
        out[:v.shape[0]] = v
        return out

    cols = {
        "norm_w": f[a + "norm_w"], "bz": f[a + "mx_b"][128:256], "br": f[a + "mx_b"][256:384],
        "gamma0": f[a + "gamma"][0], "gamma1": f[a + "gamma"][1], "beta0": f[a + "beta"][0], "beta1": f[a + "beta"][1],
        "dt_b": f[a + "dt_b"], "D_p": f[a + "D_p"], "alpha": f[a + "alpha_rb"][0], "alpha_sw": np.roll(f[a + "alpha_rb"][0], 64),
        "beta_rb": f[a + "beta_rb"][0], "beta_rb_sw": np.roll(f[a + "beta_rb"][0], 64),
        "bq": f[w + "bq"], "bk": f[w + "bk"], "gate": np.repeat(f[w + "gate"], HEAD_DIM),
        "lg": f[g + "ln_g"].T, "lb": f[g + "ln_b"].T, "shift": np.repeat(f[w + "shift_weights"], HEAD_DIM, axis=0),
        "W_cross": f[w + "W_cross"].reshape(P, HEAD_DIM), "A_log": f[a + "A_log"],
        "b1a": np.concatenate([padded(f[g + "b1"][l, c * 128:min((c + 1) * 128, HID)][:, None]) for l in range(DEPTH) for c in range(3)], 1),
        "b1g": np.concatenate([padded(f[g + "b1"][l, HID + c * 128:HID + min((c + 1) * 128, HID)][:, None]) for l in range(DEPTH) for c in range(3)], 1),
    }
    colp = np.concatenate([column(cols[k]) for k in COLS], 1)
    rows = {
        "v_b": f[a + "v_b"], "bu": f[a + "mx_b"][0:128], "bhx": f[a + "mx_b"][384:512], "h_b": f[a + "h_b"],
        "bv": f[w + "bv"], "bo": f[w + "bo"], "b2": f[g + "b2"], "qs": f[g + "q_scale"], "qs_sw": np.roll(f[g + "q_scale"], 32, axis=1),
        "ks": f[g + "k_scale"], "ks_sw": np.roll(f[g + "k_scale"], 32, axis=1),
    }
    rowp = np.concatenate([rows[k].reshape(1, -1) for k in ROWS], 1)
    xp = f[a + "xproj_w"]

    def blocks_of(v):
        return v.reshape(-1, P, v.shape[1]).transpose(1, 0, 2).reshape(P, -1)

    mats = {
        "v_w": f[a + "v_w"].T, "mx_w": f[a + "mx_w"].T, "h_w": f[a + "h_w"].T, "bc_w": np.concatenate([xp[8:40].T] * 3, 1),
        "dtl_w": xp[0:8].T, "dt_w": padded(f[a + "dt_w"].T), "Wq": f[w + "Wq"].T, "Wk": f[w + "Wk"].T, "Wv": f[w + "Wv"].T,
        "Wo": f[w + "Wo"].T, "wqkv": np.concatenate(list(f[g + "wqkv"]), 1),
        "wo": np.concatenate([blocks_of(f[g + "wo"][l]) for l in range(DEPTH)], 1),
        "w1": np.concatenate(list(f[g + "w1"]), 1),
        "w2": np.concatenate([blocks_of(np.concatenate([f[g + "w2"][l], np.zeros((384 - HID, 128), np.float32)], 0)) for l in range(DEPTH)], 1),
    }
    wts = np.concatenate([mats[k] for k in WTS], 1)
    ints = np.concatenate([f["L0_ffn_w_gate"].T, f["L0_ffn_w_up"].T, blocks_of(f["L0_ffn_w_down"].T)], 1)
    return {"colp": colp, "rowp": rowp, "wts": wts, "ints": ints}


def constants():
    f32 = np.float32
    eye = np.eye(P, dtype=f32)
    q, k = np.arange(P)[:, None], np.arange(P)[None, :]
    causal = np.where(k > q, f32(NEG), f32(0))
    head = np.arange(P) // HEAD_DIM
    fr = np.arange(P) % HEAD_DIM
    taps = np.stack([(np.arange(HEAD_DIM)[None, :] - fr[:, None] == tau) for tau in range(4)], 1).reshape(P, 32).astype(f32)
    freqs = np.exp(np.arange(64, dtype=f32) * f32(-math.log(10000.0) / 64))
    ang = (np.arange(CHUNK, dtype=f32)[:, None] * freqs[None, :]).T
    cos0, sin0 = np.cos(ang), np.sin(ang)
    half = np.arange(0, LDIM, 2, dtype=f32)
    inv_freq = f32(1.0) / np.power(f32(10000.0), half / f32(LDIM))
    t = np.arange(SEQ, dtype=f32)
    fq = t[:, None] * inv_freq[None, :]
    base = (half + f32(0.4 * LDIM)) / f32(1.4 * LDIM)
    power = (t - SEQ // 2) / f32(WINDOW // 2)
    scale = np.power(base[None, :], power[:, None])
    two = lambda v: np.concatenate([v, v], 1)
    cos, sin, scale = two(np.cos(fq)), two(np.sin(fq)), two(scale)
    sign = np.where(np.arange(LDIM) < LDIM // 2, f32(-1), f32(1))[None, :]
    rows = lambda v: v.reshape(NJ, P, LDIM).transpose(1, 0, 2).reshape(P, NJ * LDIM)
    vals = {
        "ident": eye, "mean": np.full((P, P), 1.0 / P, f32), "causal": causal, "blocks": (head[:, None] == head[None, :]).astype(f32),
        "taps": taps, "cos0": np.concatenate([cos0, cos0], 0), "sin0": np.concatenate([-sin0, sin0], 0),
        "qcos": rows(cos * scale), "qsin": rows(sign * sin * scale), "kcos": rows(cos / scale), "ksin": rows(sign * sin / scale),
        "eps": np.full((P, 1), EPS, f32),
    }
    cst = np.concatenate([vals[n] for n in CST], 1).astype(f32)
    tab = np.concatenate([vals[n] for n in TAB], 1).astype(f32)
    i, c = np.arange(WINDOW)[:, None], np.arange(P)[None, :]
    own = c < WINDOW
    first = np.where(own, c <= i, c - WINDOW >= i)
    first0 = np.where(own, c <= i, False)
    second = np.where(own, c >= i, c - WINDOW <= i)
    mask = lambda m: np.where(m, f32(0), f32(NEG))
    sel = np.zeros((P, 32, P), f32)
    for r in range(96):
        sel[r, r % 32, :] = 1
    bvals = {"ident": eye, "causal": causal, "causal_T": causal.T, "window0": mask(np.concatenate([first0, second], 0)),
             "window": mask(np.concatenate([first, second], 0)), "select": sel.reshape(P, -1)}
    bits = lambda v: (np.ascontiguousarray(v, f32).view(np.uint32) >> 16).astype(np.uint16)
    bcst = bits(np.concatenate([bvals[n] for n in BCST], 1))
    ones = bits(np.ones((PARTS, PAIRS, SEQ), f32))
    return {"cst": cst, "tab": tab, "bcst": bcst, "ones": ones}


def kernel(**inputs):
    import concourse.bacc as _bacc
    from concourse.bass_utils import run_bass_kernel_spmd as _run

    nc = _bacc.Bacc("TRN2", target_bir_lowering=False, num_devices=1)
    packed = pack(inputs)
    packed.update(constants())
    packed["x"] = np.asarray(inputs["L0_attn_x"])
    arrays = {"in_" + n: np.ascontiguousarray(v) for n, v in packed.items()}
    ap = {n: nc.dram_tensor(n, v.shape, mybir.dt.from_np(v.dtype), kind="ExternalInput").ap() for n, v in arrays.items()}
    out = nc.dram_tensor("out", (BATCH, SEQ, DIM), F32, kind="ExternalOutput").ap()
    build(nc, *(ap["in_" + n] for n in ("x", "colp", "rowp", "wts", "ints", "cst", "tab", "bcst", "ones")), out)
    r = _run(nc, [arrays], core_ids=[0])
    return r.results[0]["out"]
```

```python
from contextlib import ExitStack
import math

import numpy as np

import concourse.bass as bass
from concourse import mybir

ALU = mybir.AluOpType
ACT = mybir.ActivationFunctionType
AX = mybir.AxisListType
F32 = mybir.dt.float32
BF16 = mybir.dt.bfloat16
I32 = mybir.dt.int32
U16 = mybir.dt.uint16

P = 128
BATCH, SEQ, DIM = 8, 512, 128
NJ = SEQ // P
STREAMS = 2
STATES = 16
GROUP = 4
RANK = 8
CHUNK = 256
HIDDEN_CHUNKS = 3
HEADS, HEAD_DIM = 16, 8
PAIRS = HEADS // 2
SPLITS = 6
STACK = SPLITS * HEAD_DIM
PARTS = 3
DEPTH, LHEADS, LDIM, WINDOW = 2, 8, 64, 64
INNER = LHEADS * LDIM
HID = 341
HID_ROWS = (128, 128, HID - 256)
EPS = 1e-5
NEG = -1e30
TWO10 = 1024.0
LNEXP = "natural_log_exp_and_others"
SIGMOID = "sigmoid_and_others"
GELU = "gelu_and_others"

COLS = {}
_n = 0
for _name, _w in (("norm_w", 1), ("bz", 1), ("br", 1), ("gamma0", 1), ("gamma1", 1), ("beta0", 1), ("beta1", 1),
                  ("dt_b", 1), ("D_p", 1), ("alpha", 1), ("alpha_sw", 1), ("beta_rb", 1), ("beta_rb_sw", 1),
                  ("bq", 1), ("bk", 1), ("gate", 1), ("lg", 2), ("lb", 2), ("shift", 4), ("W_cross", 8),
                  ("A_log", 16), ("b1a", 6), ("b1g", 6)):
    COLS[_name] = (_n, _n + _w)
    _n += _w
NCOLS = _n
ROWS = {}
_n = 0
for _name, _w in (("v_b", 128), ("bu", 128), ("bhx", 128), ("h_b", 128), ("bv", 128), ("bo", 128), ("b2", 256),
                  ("qs", 128), ("qs_sw", 128), ("ks", 128), ("ks_sw", 128)):
    ROWS[_name] = (_n, _n + _w)
    _n += _w
NROWS = _n
WTS = {}
_n = 0
for _name, _w in (("v_w", 128), ("mx_w", 512), ("h_w", 128), ("bc_w", 96), ("dtl_w", 8), ("dt_w", 128),
                  ("Wq", 128), ("Wk", 128), ("Wv", 128), ("Wo", 128), ("wqkv", 2 * 1536), ("wo", 2 * 512),
                  ("w1", 2 * 2 * HID), ("w2", 2 * 384)):
    WTS[_name] = (_n, _n + _w)
    _n += _w
NWTS = _n
CST = {}
_n = 0
for _name, _w in (("ident", 128), ("mean", 128), ("causal", 128), ("blocks", 128), ("taps", 32),
                  ("eps", 1)):
    CST[_name] = (_n, _n + _w)
    _n += _w
NCST = _n
TAB = {_name: 256 * _i for _i, _name in enumerate(("cos0", "sin0", "qcos", "qsin", "kcos", "ksin"))}
BCST = {}
_n = 0
for _name, _w in (("ident", 128), ("causal", 128), ("causal_T", 128), ("window0", 128), ("window", 128), ("select", 32 * 128)):
    BCST[_name] = (_n, _n + _w)
    _n += _w
NBCST = _n


def network_stages():
    stages = ([("load",), ("input_stats",), ("input_rms",), ("input_scale",), ("bc_dt_low",),
                ("dt_v",), ("softplus",)]
              + [("states", g) for g in range(STATES // GROUP)]
              + [("state_output",), ("mixed",), ("chunk_scores",), ("chunk_probs",), ("chunk_values",),
                ("chunk_out",), ("chunk_gate",), ("x1",), ("swiglu_in",)]
              + [("swiglu_up", c) for c in range(HIDDEN_CHUNKS)]
              + [("swiglu_down",), ("x2",), ("heads_in",), ("heads_qk",), ("spill_keys",),
                ("heads_mix",), ("spill_queries",), ("heads_v",), ("restack",)]
              + [("row_scores", j, half) for j in range(NJ) for half in range(2)]
              + [("max_parts",), ("max_turn",), ("max_stack",)]
              + [s for g in range(HEADS // 4)
                for s in (("pair_probs", 2 * g), ("pair_probs", 2 * g + 1), ("head_values", g), ("head_divide", g))]
              + [("heads_turn",), ("heads_out",), ("x3",), ("window_norm",)])
    for l in range(DEPTH):
        stages.append(("layer_in", l))
        pipeline = ((0, "qkv"), (0, "inverse_norms"), (1, "qk_transposes"), (2, "window_scores"), (3, "prob_transposes"),
                    (5, "window_project"), (4, "window_values"), (2, "window_sums"))
        for t in range(NJ + 5):
            stages += [(name, l, t - d) for d, name in pipeline if 0 <= t - d < NJ]
        stages += [("geglu_in", l), ("geglu_mean", l), ("geglu_var", l), ("geglu_norm", l)]
        stages += [("geglu_up", l, c) for c in range(HIDDEN_CHUNKS)] + [("geglu_down", l)]
    return stages + [("output",)]


INTERLEAVING = ("010001100101101111010011101010101010101110110101001110101011000111011010001011001101011100100111"
                "010111010010101000110100010011010010111010011010101101100011001100001000001001110000100010010101"
                "011010110001010100110100100011010000111001000011100111011100111110011100101001010101101011001101"
                "0101")


def interleaved(stages):
    ahead = [iter(stages) for _ in range(STREAMS)]
    return [(int(s), next(ahead[int(s)])) for s in INTERLEAVING]


EVENTS = {
    "s6_vector": ("mean_sq", "xr", "bc_low", "bc_parts", "sp_z", "v_raw", "sp_1pe", "dt", "dtu", "yd"),
    "s6_scalar": ("rms", "xrT", "dt_low", "bc_high", "sp_exp", "sp_ln", "sp_inverse", "y_sig", "v_sig"),
    "chunk_vector": ("mx", "v_rows", "z", "r", "u_raw", "scores_biased", "score_max", "probs", "hr", "h_raw"),
    "chunk_scalar": ("z_sig", "r_sig", "score_exp", "probsT", "h_sig"),
    "swiglu_vector": ("fxn", "fo"),
    "swiglu_scalar": ("fxT",),
    "heads_vector": ("axn", "k_parts", "k_split", "q_parts", "q_split", "v_ext", "nm_parts", "aout"),
    "heads_scalar": ("axT", "QT", "k_high", "q_high", "nm_cols", "aoT"),
}
EVENT_OF = {event: (name, i + 1) for name, events in EVENTS.items() for i, event in enumerate(events)}
CORE_WIDE = ("products", "dve_step", "act_step", "params_loaded", "weights_loaded", "param_funcs", "param_step", "bias_operands", "bias_products")


class PsumRing:

    def __init__(self, psum, slots, done, stream):
        self.psum, self.slots, self.done, self.stream = psum, slots, done, stream
        self.freed = [[] for _ in range(slots)]
        self.n = 0
        self.groups = 0
        self.where = {}

    def take(self, pe, name, freed_by):
        name = (self.stream[0], name)
        slot = self.n % self.slots
        self.n += 1
        for s, value in self.freed[slot]:
            pe.wait_ge(s, value)
        self.freed[slot] = freed_by
        self.where[name] = [slot, None]
        return self.psum[:, slot, :]

    def full(self, ins, name):
        name = (self.stream[0], name)
        self.groups += 1
        self.where[name][1] = self.groups
        ins.then_inc(self.done, 1)

    def read(self, eng, name):
        name = (self.stream[0], name)
        slot, value = self.where[name]
        eng.wait_ge(self.done, value)
        return self.psum[:, slot, :]


def build(nc, x_d, colp_d, rowp_d, wts_d, ints_d, cst_d, tab_d, bcst_d, ones_d, out_d, iterations=BATCH // STREAMS):
    ctx = ExitStack()
    with ctx:
        def sb(name, shape, dt=F32):
            return ctx.enter_context(nc.sbuf_tensor(name, shape, dt))

        sems = {}
        stream = [0]

        def sem(name):
            name = EVENT_OF[name][0] if name in EVENT_OF else name
            name = name if name in CORE_WIDE else f"{name}_{stream[0]}"
            if name not in sems:
                sems[name] = ctx.enter_context(nc.semaphore(name))
            return sems[name]

        def event(name):
            return sem(name), EVENT_OF[name][1]

        def own(pair):
            return pair[stream[0]]

        split_scratch = [nc.dram_tensor(f"split_scratch{s}", (2, SPLITS, P, SEQ), BF16, kind="Internal").ap() for s in range(STREAMS)]
        max_scratch = [nc.dram_tensor(f"max_scratch{s}", (PARTS, HEADS, SEQ), BF16, kind="Internal").ap() for s in range(STREAMS)]

        def by_stream(name, shape, dt=F32):
            return [sb(f"{name}{s}", shape, dt) for s in range(STREAMS)]

        colp = sb("colp", [P, NCOLS])
        rowp = sb("rowp", [P, NROWS])
        wts = sb("wts", [P, NWTS])
        cst = sb("cst", [P, NCST])
        bcst = sb("bcst", [P, NBCST], BF16)
        ffw = sb("ffw", [P, 9, 128])
        tiles = by_stream("tiles", [P, 32, SEQ])
        v_prev = by_stream("v_prev", [P, 2, INNER])
        score_bias = sb("score_bias", [P, 384])
        tables = sb("tables", [P, DEPTH, 4, NJ, LDIM])
        mix = sb("mix", [P, P])
        stats = by_stream("stats", [P, NJ, 6])
        mv = by_stream("mv", [P, 8, NJ, 2])
        lnv = by_stream("lnv", [P, 8, NJ])
        rstd = by_stream("rstd", [P, 8, NJ])
        rms = by_stream("rms", [P, 6, NJ])
        small = sb("small", [P, 128])
        sm1 = by_stream("sm1", [P, 4, 4])
        neg_max = by_stream("neg_max", [P, NJ, HEADS])
        nm_res = by_stream("nm_res", [P, NJ, HEADS])
        nm_parts = by_stream("nm_parts", [P, NJ, PARTS * HEADS], BF16)
        nm_cols = by_stream("nm_cols", [PARTS * HEADS, SEQ], BF16)
        inv_sum = by_stream("inv_sum", [P, 2, NJ, 4])
        ssq = by_stream("ssq", [P, 2, 2, LHEADS])
        lnss = by_stream("lnss", [P, 2, 2, LHEADS])
        invn = by_stream("invn", [P, NJ, 2, LHEADS])
        lmax = by_stream("lmax", [P, 2, LHEADS])
        lsum = by_stream("lsum", [P, 2, LHEADS])
        psum = ctx.enter_context(nc.psum_tensor("psum", [P, 4, 1024], F32))

        def col(name, i=0, rows=P):
            a = COLS[name][0] + i
            return colp[0:rows, a:a + 1]

        def row(name, i=0, w=128):
            a = ROWS[name][0] + i * w
            return rowp[:, a:a + w]

        def row4(name, i=0):
            return row(name, i).unsqueeze(1).to_broadcast([P, NJ, 128])

        def wt(name, a=0, w=128, rows=P):
            a += WTS[name][0]
            return wts[0:rows, a:a + w]

        def const(name, a=0, w=128):
            a += CST[name][0]
            return cst[:, a:a + w]

        def table_in(name):
            return T(8, 3)[:, TAB[name]:TAB[name] + 256]

        def bconst(name, a=0, w=128, rows=P):
            a += BCST[name][0]
            return bcst[0:rows, a:a + w]

        def T(i, n=1):
            return own(tiles)[:, i:i + n, :].rearrange("p a n -> p (a n)")

        def blocks(ap, w=128):
            return ap.rearrange("p (j d) -> p j d", d=w)

        ident = const("ident")
        identb = bconst("ident")
        eps = const("eps", 0, 1)
        ffw_gate, ffw_up, ffw_down = ffw[:, 0:3, :], ffw[:, 3:6, :], ffw[:, 6:9, :]

        with nc.Block() as block:
            @block.sync
            def _(sp):
                loaded = sem("params_loaded")
                sp.dma_start(cst[:, :], cst_d).then_inc(loaded, 16)
                sp.dma_start(colp[:, :], colp_d).then_inc(loaded, 16)
                sp.dma_start(rowp[:, :], rowp_d.to_broadcast([P, NROWS])).then_inc(loaded, 16)
                sp.dma_start(T(8, 3), tab_d).then_inc(loaded, 16)
                sp.dma_start(T(0, 3)[:, 0:1152].bitcast(I32), ints_d).then_inc(loaded, 16)
                sp.dma_start(bcst[:, :].bitcast(U16), bcst_d).then_inc(sem("weights_loaded"), 16)
                sp.dma_start(wts[:, :], wts_d).then_inc(sem("weights_loaded"), 16)
                sp.wait_ge(loaded, 80)
                sp.wait_ge(sem("weights_loaded"), 32)

            @block.gpsimd
            def _(pool):
                for s in range(STREAMS):
                    nc.gpsimd.memset(v_prev[s][:, :, :], 0.0)

            @block.scalar
            def _(act):
                act.wait_ge(sem("params_loaded"), 80)
                nc.scalar.activation(small[:, 0:1], col("gate"), ACT.Sigmoid).then_inc(sem("param_funcs"), 1)
                nc.scalar.activation(small[:, 16:32], colp[:, COLS["A_log"][0]:COLS["A_log"][1]],
                                     ACT.Exp).then_inc(sem("param_funcs"), 1)

            @block.tensor
            def _(pe):
                pe.wait_ge(sem("bias_operands"), 2)
                nc.tensor.matmul(psum[:, 0, 0:128], T(4)[:, 0:128], T(5)[:, 0:128], start=True, stop=True)
                nc.tensor.matmul(psum[:, 0, 128:384], T(4)[:, 128:256], T(5)[:, 0:256], start=True,
                                 stop=True).then_inc(sem("bias_products"), 1)

            @block.vector
            def _(dve):
                steps = [0]

                def step(ins):
                    steps[0] += 1
                    ins.then_inc(sem("param_step"), 1)
                    dve.wait_ge(sem("param_step"), steps[0])

                dve.wait_ge(sem("params_loaded"), 80)
                nc.vector.tensor_scalar(T(6)[:, 0:256], table_in("sin0"), col("alpha_sw"), None, ALU.mult)
                step(nc.vector.tensor_scalar(T(7)[:, 0:256], table_in("sin0"), col("beta_rb_sw"), None, ALU.mult))
                nc.vector.scalar_tensor_tensor(out=T(4)[:, 0:256], in0=table_in("cos0"), scalar=col("alpha"),
                                               in1=T(6)[:, 0:256], op0=ALU.mult, op1=ALU.add).then_inc(sem("bias_operands"), 1)
                nc.vector.scalar_tensor_tensor(out=T(5)[:, 0:256], in0=table_in("cos0"), scalar=col("beta_rb"),
                                               in1=T(7)[:, 0:256], op0=ALU.mult, op1=ALU.add).then_inc(sem("bias_operands"), 1)
                step(nc.vector.tensor_scalar(ffw[:, :, :].rearrange("p a n -> p (a n)"), T(0, 3)[:, 0:1152].bitcast(I32),
                                             1.0 / 127.0, None, ALU.mult))
                for name in ("gamma0", "beta0"):
                    step(nc.vector.tensor_scalar(col(name), col(name), 128 ** -0.5, None, ALU.mult))
                step(nc.vector.tensor_tensor(row("h_b"), row("h_b"), row("bhx"), ALU.add))
                for l in range(DEPTH):
                    for t, (tab, vec, f) in enumerate((("qcos", "qs", 8.0 * TWO10), ("qsin", "qs_sw", 8.0 * TWO10),
                                                       ("kcos", "ks", TWO10), ("ksin", "ks_sw", TWO10))):
                        scale = row(vec, l, 64).unsqueeze(1).to_broadcast([P, NJ, LDIM])
                        nc.vector.scalar_tensor_tensor(out=tables[:, l, t, :, :], in0=blocks(table_in(tab), LDIM),
                                                       scalar=f, in1=scale, op0=ALU.mult, op1=ALU.mult)
                dve.wait_ge(sem("param_funcs"), 2)
                A_log = colp[:, COLS["A_log"][0]:COLS["A_log"][1]]
                step(nc.vector.tensor_scalar(A_log, small[:, 16:32], -1.0, None, ALU.mult))
                s8 = HEAD_DIM ** -0.5
                nc.vector.tensor_scalar(small[:, 1:2], small[:, 0:1], s8, None, ALU.mult)
                step(nc.vector.tensor_scalar(small[:, 2:3], small[:, 0:1], -s8, s8, ALU.mult, ALU.add))
                W = colp[:, COLS["W_cross"][0]:COLS["W_cross"][1]]
                step(nc.vector.tensor_scalar(small[:, 32:40], const("taps", 0, 8), col("shift"), None, ALU.mult))
                for tau in range(1, 4):
                    step(nc.vector.scalar_tensor_tensor(out=small[:, 32:40], in0=const("taps", 8 * tau, 8),
                                                        scalar=col("shift", tau), in1=small[:, 32:40],
                                                        op0=ALU.mult, op1=ALU.add))
                step(nc.vector.tensor_scalar(small[:, 40:48], small[:, 32:40], small[:, 2:3], None, ALU.mult))
                step(nc.vector.scalar_tensor_tensor(out=small[:, 48:56], in0=W, scalar=small[:, 1:2],
                                                    in1=small[:, 40:48], op0=ALU.mult, op1=ALU.add))
                step(nc.vector.tensor_tensor(blocks(mix[:, :], 8), blocks(const("blocks"), 8),
                                             small[:, 48:56].unsqueeze(1).to_broadcast([P, HEADS, 8]), ALU.mult))
                dve.wait_ge(sem("bias_products"), 1)
                step(nc.vector.tensor_copy(score_bias[:, :], psum[:, 0, 0:384]))
                for a in (0, 256):
                    step(nc.vector.tensor_tensor(score_bias[:, a:a + 128], score_bias[:, a:a + 128], const("causal"), ALU.add))

        x_v = x_d.rearrange("(i s) (j p) d -> i s p j d", s=STREAMS, p=P)
        out_v = out_d.rearrange("(i s) (j p) d -> i s p j d", s=STREAMS, p=P)

        def moves(l, j):
            return (3, 4)[j % 2] * l + (1, 2, 3, 4)[j]

        def prob_parts(p):
            b = p % 2
            return (T((1, 24)[b], 2), T((18, 5)[b], 2)[:, 0:768], T((3, 9)[b]), T((18, 5)[b], 2)[:, 768:1024])

        X0, X1, X2 = 0, 1, 0
        XR, RES, XRT, VAL, DT, DTU = 1, 2, 3, 4, 5, 6
        SPZ, SPE, SPU, SPL, BCR, BCS, DTLOW, VB, VSIG = 7, 8, 9, 10, 11, 12, 13, 14, 15
        S6_DA, S6_DBU, S6_H, S6_HC, S6_SUM = (16, 17, 18), (19, 20), (21, 22), (7, 8, 9, 10), (11, 15)
        YD, YSIG, MX, ZSIG, RSIG, ZF, RF, QF, KF, UB, USIG, SB, PROB_T = 7, 8, 9, 10, 11, 12, 13, 14, 15, 16, 17, 18, 20
        HR, HB, HSIG, HO, HN = 5, 6, 10, 8, 22
        FXN, FXNT, FSIG, FG, FH, FO = 2, 3, 4, 7, 10, 13
        AXN, AXNT, QT, QRES, KRES, QPARTS, KPARTS, QSTK, KSTK, AO, AOT, AOUT, OCOL, VE = 2, 3, 4, 5, 6, 7, 18, 10, 14, 4, 5, 6, 7, 20
        X3, Y, Y1, HT, LQT, LKT, LV = 1, 0, 2, 3, 5, 7, 11
        LP, LPT, ROT, LOT, TURNED = (15, 17), (19, 21), (24, 26), 23, 28
        HT2, CEN, SQF, RLN, HNT, HGB, GG, HH, LAST = 3, 4, 5, 6, 7, 8, 9, 12, 15

        def values_ext():
            return T(VE, 4).rearrange("p (j h d) -> p j h d", j=NJ, h=HEADS)

        long_sum = [psum[:, 3, s * 512:(s + 1) * 512] for s in range(STREAMS)]

        def emit(schedule, x_now, out_now):
            ring = PsumRing(psum, 3, sem("products"), stream)

            def run(stages):
                for stream[0], (name, *args) in schedule:
                    if name in stages:
                        stages[name](*args)

            with nc.Block() as block:
                @block.tensor
                def _(pe):
                    take, full = ring.take, ring.full
                    mm = nc.tensor.matmul

                    def transposes(name, src, ready, freed):
                        pe.wait_ge(*ready)
                        ps = take(pe, name, freed)
                        for j in range(NJ):
                            ins = nc.tensor.transpose(ps[:, j * 128:(j + 1) * 128], src[:, j * 128:(j + 1) * 128], ident)
                        full(ins, name)

                    def by_token_block(ps, lhs, rhs):
                        for j in range(NJ):
                            ins = mm(ps[:, j * 128:(j + 1) * 128], lhs[:, j * 128:(j + 1) * 128], rhs, start=True, stop=True)
                        return ins

                    def input_scale():
                        transposes("xrT", T(XR), event("xr"), [event("xrT")])

                    def bc_dt_low():
                        pe.wait_ge(*event("xrT"))
                        ps = take(pe, "bcdt", [event("bc_low"), event("dt_low")])
                        mm(ps[0:96, 0:512], wt("bc_w", 0, 96), T(XRT), start=True, stop=True)
                        full(mm(ps[0:RANK, 512:1024], wt("dtl_w", 0, RANK), T(XRT), start=True, stop=True), "bcdt")

                    def dt_v():
                        pe.wait_ge(*event("dt_low"))
                        ps = take(pe, "dt", [event("sp_z")])
                        full(mm(ps[:, 0:512], wt("dt_w", rows=RANK), T(DTLOW)[0:RANK, :], start=True, stop=True), "dt")
                        ps = take(pe, "v", [event("v_raw")])
                        full(by_token_block(ps, T(XRT), wt("v_w")), "v")

                    def add_states(m):
                        pe.wait_ge(sem("pair_sum"), m + 1)
                        mm(own(long_sum), ident, T(S6_SUM[m % 2]), start=(m == 0),
                           stop=(m == STATES // 2 - 1)).then_inc(sem("y_products"), 1)

                    def states(g):
                        if g == 0:
                            pe.wait_ge(*event("bc_parts"))
                        parts = T(BCS).bitcast(BF16)[0:96, 0:512]
                        for n in range(GROUP * g, GROUP * (g + 1)):
                            ps = take(pe, ("bc", n), [(sem("hc"), n + 1)])
                            mm(ps[:, 0:512], bconst("select", n * 128, rows=96), parts, start=True, stop=True)
                            full(mm(ps[:, 512:1024], bconst("select", (16 + n) * 128, rows=96), parts,
                                    start=True, stop=True), ("bc", n))
                            if n % 2 == 1 and n >= 3:
                                add_states((n - 3) // 2)

                    def state_output():
                        add_states(STATES // 2 - 1)

                    def mixed():
                        pe.wait_ge(*event("mx"))
                        ps = take(pe, "zr", [event("z"), event("r")])
                        mm(ps[:, 0:512], wt("mx_w", 128), T(MX), start=True, stop=True)
                        full(mm(ps[:, 512:1024], wt("mx_w", 256), T(MX), start=True, stop=True), "zr")
                        ps = take(pe, "u", [event("u_raw")])
                        full(by_token_block(ps, T(MX), wt("mx_w", 0)), "u")

                    def chunk_scores():
                        pe.wait_ge(sem("qk_cols"), 2)
                        ps = take(pe, "scores", [event("scores_biased")])
                        q, k = T(QF), T(KF)
                        for c in range(2):
                            a = c * CHUNK
                            mm(ps[:, c * 512:c * 512 + 128], q[:, a:a + 128], k[:, a:a + 128], start=True, stop=True)
                            ins = mm(ps[:, c * 512 + 128:c * 512 + 384], q[:, a + 128:a + 256], k[:, a:a + 256],
                                     start=True, stop=True)
                        full(ins, "scores")

                    def chunk_probs():
                        pe.wait_ge(*event("probs"))
                        ps = take(pe, "probsT", [event("probsT")])
                        p = T(SB, 2)
                        for c in range(2):
                            for i in range(3):
                                ins = nc.tensor.transpose(ps[:, c * 512 + i * 128:c * 512 + (i + 1) * 128],
                                                          p[:, c * 384 + i * 128:c * 384 + (i + 1) * 128], ident)
                        full(ins, "probsT")

                    def chunk_values():
                        pe.wait_ge(*event("probsT"))
                        pe.wait_ge(*event("v_rows"))
                        ps = take(pe, "av", [event("hr")])
                        v, pt = T(VAL), T(PROB_T, 2)
                        for c in range(2):
                            mm(ps[:, c * 256:c * 256 + 128], v[:, c * 256:c * 256 + 128], pt[:, c * 384:c * 384 + 128],
                               start=True, stop=True)
                            mm(ps[:, c * 256 + 128:c * 256 + 256], v[:, c * 256:c * 256 + 128],
                               pt[:, c * 384 + 128:c * 384 + 256], start=True, stop=False)
                            ins = mm(ps[:, c * 256 + 128:c * 256 + 256], v[:, c * 256 + 128:c * 256 + 256],
                                     pt[:, c * 384 + 256:c * 384 + 384], start=False, stop=True)
                        full(ins, "av")

                    def chunk_out():
                        pe.wait_ge(*event("hr"))
                        ps = take(pe, "h", [event("h_raw")])
                        for j in range(NJ):
                            b = slice(j * 128, (j + 1) * 128)
                            mm(ps[:, b], T(MX)[:, b], wt("mx_w", 384), start=True, stop=False)
                            ins = mm(ps[:, b], T(HR)[:, b], wt("h_w"), start=False, stop=True)
                        full(ins, "h")

                    def swiglu_in():
                        transposes("fxT", T(FXN), event("fxn"), [event("fxT")])

                    def swiglu_up(c):
                        pe.wait_ge(*event("fxT"))
                        ps = take(pe, ("gu", c), [(sem("fh"), c + 1)])
                        mm(ps[:, 0:512], ffw_gate[:, c, :], T(FXNT), start=True, stop=True)
                        full(mm(ps[:, 512:1024], ffw_up[:, c, :], T(FXNT), start=True, stop=True), ("gu", c))

                    def swiglu_down():
                        pe.wait_ge(sem("fh"), 3)
                        ps = take(pe, "down", [event("fo")])
                        for j in range(NJ):
                            for c in range(HIDDEN_CHUNKS):
                                ins = mm(ps[:, j * 128:(j + 1) * 128], T(FH + c)[:, j * 128:(j + 1) * 128], ffw_down[:, c, :],
                                         start=(c == 0), stop=(c == 2))
                        full(ins, "down")

                    def heads_in():
                        transposes("axT", T(AXN), event("axn"), [event("axT")])

                    def heads_qk():
                        pe.wait_ge(*event("axT"))
                        ps = take(pe, "QK", [event("QT"), event("k_parts")])
                        mm(ps[:, 0:512], wt("Wq"), T(AXNT), start=True, stop=True)
                        full(mm(ps[:, 512:1024], wt("Wk"), T(AXNT), start=True, stop=True), "QK")

                    def heads_mix():
                        pe.wait_ge(*event("QT"))
                        ps = take(pe, "QG", [event("q_parts")])
                        full(mm(ps[:, 0:512], mix[:, :], T(QT), start=True, stop=True), "QG")

                    def heads_v():
                        ps = take(pe, "V", [event("v_ext")])
                        full(by_token_block(ps, T(AXNT), wt("Wv")), "V")

                    def stack(i, e, rows):
                        t = T(i, 4).bitcast(BF16).rearrange("p (a n) -> p a n", a=PAIRS)
                        return t[e * 64:e * 64 + rows]

                    def row_scores(j, half):
                        if (j, half) == (0, 0):
                            pe.wait_ge(sem("stacked"), 16 * 6)
                        keys = (j + 1) * 128
                        for p in range(half * 4, half * 4 + 4):
                            ps = take(pe, ("s1", j, p), [(sem("row_max"), j * PAIRS + p + 1)])
                            for e in range(2):
                                mm(ps[:, e * 512:e * 512 + keys], stack(QSTK, e, STACK)[:, p, j * 128:keys],
                                   stack(KSTK, e, STACK)[:, p, 0:keys], start=True, stop=False)
                            for e in range(2):
                                ins = mm(ps[:, e * 512 + j * 128:e * 512 + keys], identb, bconst("causal"), start=False, stop=True)
                            full(ins, ("s1", j, p))

                    def max_turn():
                        pe.wait_ge(*event("nm_parts"))
                        ps = take(pe, "nmT", [event("nm_cols")])
                        for j in range(NJ):
                            ins = nc.tensor.transpose(ps.bitcast(BF16)[0:PARTS * HEADS, j * 128:(j + 1) * 128], own(nm_parts)[:, j, :], identb)
                        full(ins, "nmT")

                    def pair_probs(p):
                        if p == 0:
                            pe.wait_ge(sem("maxima_stacked"), 32)
                        for jk in range(NJ):
                            w = SEQ - jk * 128
                            ps = take(pe, ("s2", p, jk), [(sem("exps"), p * NJ + jk + 1)])
                            for e in range(2):
                                mm(ps[:, e * 512:e * 512 + w], stack(KSTK, e, STACK + PARTS)[:, p, jk * 128:(jk + 1) * 128],
                                   stack(QSTK, e, STACK + PARTS)[:, p, jk * 128:SEQ], start=True, stop=False)
                            for e in range(2):
                                ins = mm(ps[:, e * 512:e * 512 + 128], identb, bconst("causal_T"), start=False, stop=True)
                            full(ins, ("s2", p, jk))

                    def head_values(g):
                        pe.wait_ge(sem("exps"), NJ * (2 * g + 2))
                        if g == 0:
                            pe.wait_ge(*event("v_ext"))
                        else:
                            pe.wait_ge(sem("o_cols"), g)
                        for jk in range(NJ):
                            for c in range(4):
                                e, p = c // 2, 2 * g + c % 2
                                w = SEQ - jk * 128
                                ins = mm(own(long_sum)[32 * c:32 * c + 32, jk * 128:512], values_ext()[:, jk, e * PAIRS + p, :],
                                         prob_parts(p)[jk][:, e * w:(e + 1) * w], start=(jk == 0), stop=(jk == NJ - 1))
                        ins.then_inc(sem("value_products"), 1)

                    def head_divide(g):
                        transposes(("oT", g), T(OCOL + g % 2), (sem("o_cols"), g + 1), [(sem("ao_part"), g + 1)])

                    def heads_turn():
                        transposes("aoT", T(AO), (sem("ao_part"), HEADS // 4), [event("aoT")])

                    def heads_out():
                        pe.wait_ge(*event("aoT"))
                        ps = take(pe, "proj", [event("aout")])
                        full(by_token_block(ps, T(AOT), wt("Wo")), "proj")

                    def layer_in(l):
                        transposes(("yT", l), T(Y), (sem("y_in"), l + 1), [(sem("shift_a"), l + 1), (sem("shift_b"), l + 1)])

                    def qkv(l, j):
                        n = l * NJ + j
                        wq = WTS["wqkv"][0] + l * 1536
                        if j == 0:
                            pe.wait_ge(sem("shift_a"), l + 1)
                            pe.wait_ge(sem("shift_b"), l + 1)
                        lhs = T(HT)[:, j * 128:(j + 1) * 128]
                        ps = take(pe, ("lqk", n), [(sem("squares"), 2 * (n + 1)), (sem("turned"), 2 * (n + 1))])
                        mm(ps[:, 0:512], lhs, wts[:, wq:wq + 512], start=True, stop=True)
                        full(mm(ps[:, 512:1024], lhs, wts[:, wq + 512:wq + 1024], start=True, stop=True), ("lqk", n))
                        ps = take(pe, ("lv", n), [(sem("lv"), n + 1)])
                        full(mm(ps[:, 0:512], lhs, wts[:, wq + 1024:wq + 1536], start=True, stop=True), ("lv", n))

                    def qk_transposes(l, j):
                        n = l * NJ + j
                        pe.wait_ge(sem("rotated"), 2 * (n + 1))
                        ps = take(pe, ("lqkT", n), [(sem("lqT"), n + 1), (sem("lkT"), n + 1)])
                        for t in range(2):
                            for g in range(4):
                                a = t * 512 + g * 128
                                ins = nc.tensor.transpose(ps[:, a:a + 128], T(ROT[j % 2] + t)[:, g * 128:(g + 1) * 128], ident)
                        full(ins, ("lqkT", n))

                    def window_scores(l, j):
                        n = l * NJ + j
                        pe.wait_ge(sem("lqT"), n + 1)
                        pe.wait_ge(sem("lkT"), n + 1)
                        ps = take(pe, ("ls", n), [(sem("lexp"), n + 1)])
                        q = T(LQT + j % 2).rearrange("p (g n) -> p g n", g=4)
                        k = T(LKT, 4).rearrange("p (g n) -> p g n", g=4)
                        mask = bconst("window0" if j == 0 else "window").unsqueeze(1).to_broadcast([P, 4, 128])
                        t = j * 128
                        for e in range(2):
                            mm(blocks(ps[:, e * 512:(e + 1) * 512]), identb, mask, start=True, stop=True, skip_group_check=True)
                        for g in range(4):
                            for e in range(2):
                                r = slice(e * 64, (e + 1) * 64)
                                o = e * 512 + g * 128
                                before = 64 if j > 0 else 0
                                mm(ps[0:64, o + 64 - before:o + 128], q[r, g, 0:64], k[r, g, t - before:t + 64], start=False,
                                   stop=True, skip_group_check=True)
                                ins = mm(ps[64:128, o:o + 128], q[r, g, 64:128], k[r, g, t:t + 128],
                                         start=False, stop=True, skip_group_check=True)
                        full(ins, ("ls", n))

                    def prob_transposes(l, j):
                        n = l * NJ + j
                        pe.wait_ge(sem("lprobs"), n + 1)
                        ps = take(pe, ("lpT", n), [(sem("lpT"), n + 1), (sem("lpT_b"), n + 1)])
                        p = T(LP[j % 2], 2)
                        for i in range(LHEADS):
                            ins = nc.tensor.transpose(ps[:, i * 128:(i + 1) * 128], p[:, i * 128:(i + 1) * 128], ident)
                        full(ins, ("lpT", n))

                    def window_values(l, j):
                        n = l * NJ + j
                        pe.wait_ge(sem("lpT"), n + 1)
                        pe.wait_ge(sem("lpT_b"), n + 1)
                        pe.wait_ge(sem(f"v_moved{j % 2}"), 16 * moves(l, j))
                        ps = take(pe, ("lo", n), [(sem("lo"), n + 1)])
                        pt = T(LPT[j % 2], 2)
                        for g in range(4):
                            for e in range(2):
                                r = slice(e * 64, (e + 1) * 64)
                                h = (2 * g + e) * 64
                                c = (e * 4 + g) * 128
                                mm(ps[r, g * 128:g * 128 + 64], own(v_prev)[:, j % 2, h:h + 64], pt[:, c:c + 64], start=True, stop=True)
                                ins = mm(ps[r, g * 128 + 64:g * 128 + 128], T(LV + j)[:, h:h + 64], pt[:, c + 64:c + 128],
                                         start=True, stop=True)
                        full(ins, ("lo", n))

                    def window_project(l, j):
                        n = l * NJ + j
                        pe.wait_ge(sem("lo"), n + 1)
                        ps = take(pe, ("lproj", n), [(sem("y1"), n + 1)])
                        for g in range(4):
                            ins = mm(ps[:, 0:128], T(LOT)[:, g * 128:(g + 1) * 128], wt("wo", l * 512 + g * 128),
                                     start=(g == 0), stop=(g == 3))
                        full(ins, ("lproj", n))

                    def geglu_in(l):
                        transposes(("y1T", l), T(Y1), (sem("y1"), NJ * (l + 1)), [(sem("shift2_a"), l + 1), (sem("shift2_b"), l + 1)])

                    def geglu_mean(l):
                        pe.wait_ge(sem("shift2_a"), l + 1)
                        pe.wait_ge(sem("shift2_b"), l + 1)
                        ps = take(pe, ("mean", l), [(sem("centred"), l + 1)])
                        full(mm(ps[:, 0:512], const("mean"), T(HT2), start=True, stop=True), ("mean", l))

                    def geglu_var(l):
                        pe.wait_ge(sem("centred_sq"), l + 1)
                        ps = take(pe, ("var", l), [(sem("var_ln"), l + 1)])
                        full(mm(ps[:, 0:512], const("mean"), T(SQF), start=True, stop=True), ("var", l))

                    def geglu_up(l, c):
                        pe.wait_ge(sem("hgb"), l + 1)
                        m = HID_ROWS[c]
                        ps = take(pe, ("ag", l, c), [(sem("hh"), 3 * l + c + 1)])
                        a = l * 2 * HID + c * 128
                        mm(ps[0:m, 0:512], wt("w1", a, m), T(HGB), start=True, stop=True)
                        full(mm(ps[0:m, 512:1024], wt("w1", a + HID, m), T(HGB), start=True, stop=True), ("ag", l, c))

                    def geglu_down(l):
                        pe.wait_ge(sem("hh"), 3 * (l + 1))
                        ps = take(pe, ("w2", l), [(sem("y_raw"), l + 1)])
                        for j in range(NJ):
                            for c in range(HIDDEN_CHUNKS):
                                m = HID_ROWS[c]
                                ins = mm(ps[:, j * 128:(j + 1) * 128], T(HH + c)[0:m, j * 128:(j + 1) * 128],
                                         wt("w2", l * 384 + c * 128, rows=m), start=(c == 0), stop=(c == 2))
                        full(ins, ("w2", l))

                    run({"input_scale": input_scale, "bc_dt_low": bc_dt_low, "dt_v": dt_v, "states": states,
                         "state_output": state_output, "mixed": mixed, "chunk_scores": chunk_scores, "chunk_probs": chunk_probs,
                         "chunk_values": chunk_values, "chunk_out": chunk_out, "swiglu_in": swiglu_in, "swiglu_up": swiglu_up,
                         "swiglu_down": swiglu_down, "heads_in": heads_in, "heads_qk": heads_qk, "heads_mix": heads_mix,
                         "heads_v": heads_v, "row_scores": row_scores, "max_turn": max_turn, "pair_probs": pair_probs,
                         "head_values": head_values, "head_divide": head_divide, "heads_turn": heads_turn, "heads_out": heads_out,
                         "layer_in": layer_in, "qkv": qkv, "qk_transposes": qk_transposes, "window_scores": window_scores,
                         "prob_transposes": prob_transposes, "window_values": window_values, "window_project": window_project,
                         "geglu_in": geglu_in, "geglu_mean": geglu_mean, "geglu_var": geglu_var, "geglu_up": geglu_up,
                         "geglu_down": geglu_down})

                @block.vector
                def _(dve):
                    steps = [0]

                    def step(ins):
                        steps[0] += 1
                        ins.then_inc(sem("dve_step"), 1)

                    def settle():
                        dve.wait_ge(sem("dve_step"), steps[0])

                    tt, ts, stt = nc.vector.tensor_tensor, nc.vector.tensor_scalar, nc.vector.scalar_tensor_tensor

                    def ln_stats(k, src):
                        for j in range(NJ):
                            step(nc.vector.bn_stats(own(stats)[:, j, :], src[:, j * 128:(j + 1) * 128]))
                        settle()
                        for j in range(NJ):
                            ins = nc.vector.bn_aggr(own(mv)[:, k, j, :], own(stats)[:, j, :])
                        ins.then_inc(sem("ln_var"), 1)

                    def ln_apply(k, src, dst, scale=None, signal=None):
                        for j in range(NJ):
                            ins = ts(dst[:, j * 128:(j + 1) * 128], src[:, j * 128:(j + 1) * 128], own(mv)[:, k, j, 0:1],
                                     (own(rstd)[:, k, :] if scale is None else scale)[:, j:j + 1], ALU.subtract, ALU.mult)
                            if signal is None:
                                step(ins)
                        if signal is not None:
                            ins.then_inc(signal, 1)

                    def ln_ready(k):
                        dve.wait_ge(sem("ln_rstd"), k + 1)
                        dve.wait_ge(sem("ln_var"), k + 1)

                    def sublayer_end(k, src, x_old, x_new):
                        ln_ready(k)
                        ln_apply(k, src, T(HN))
                        settle()
                        step(tt(x_new, x_old, T(HN), ALU.add))
                        settle()
                        ln_stats(k + 1, x_new)

                    def input_stats():
                        dve.wait_ge(sem("x_loaded"), 16)
                        ln_stats(0, T(X0))

                    def input_rms():
                        ln_ready(0)
                        r = own(rstd)[:, 0, :]
                        step(tt(own(rms)[:, 0, :], r, r, ALU.mult))
                        settle()
                        tt(own(rms)[:, 1, :], own(rms)[:, 0, :], own(mv)[:, 0, :, 1], ALU.mult).then_inc(sem("mean_sq"), 1)
                        ln_apply(0, T(X0), T(RES))

                    def input_scale():
                        dve.wait_ge(*event("rms"))
                        step(tt(own(rms)[:, 4, :], own(rms)[:, 3, :], own(rstd)[:, 0, :], ALU.mult))
                        settle()
                        ln_apply(0, T(X0), T(XR), own(rms)[:, 4, :], sem("xr"))

                    def bc_dt_low():
                        ps = ring.read(dve, "bcdt")
                        dve.wait_ge(*event("bc_high"))
                        bcs = T(BCS).bitcast(BF16)[:, 0:512]
                        tmp = T(BCS).bitcast(BF16)[:, 512:1024]
                        res = T(BCR)
                        tt(res[0:96, :], ps[0:96, 0:512], bcs[0:96, :], ALU.subtract).then_inc(sem("bc_low"), 1)
                        dve.wait_ge(*event("bc_low"))
                        step(nc.vector.tensor_copy(bcs[32:64, :], res[32:64, :]))
                        step(nc.vector.tensor_copy(tmp[64:96, :], res[64:96, :]))
                        settle()
                        tt(bcs[64:96, :], res[64:96, :], tmp[64:96, :], ALU.subtract).then_inc(sem("bc_parts"), 1)

                    def dt_v():
                        ps = ring.read(dve, "dt")
                        ts(T(SPZ), ps[:, 0:512], col("dt_b"), None, ALU.add).then_inc(sem("sp_z"), 1)
                        ps = ring.read(dve, "v")
                        tt(blocks(T(VB)), blocks(ps[:, 0:512]), row4("v_b"), ALU.add).then_inc(sem("v_raw"), 1)

                    def softplus():
                        dve.wait_ge(*event("sp_exp"))
                        ts(T(SPU), T(SPE), 1.0, None, ALU.add).then_inc(sem("sp_1pe"), 1)
                        dve.wait_ge(*event("sp_1pe"))
                        step(stt(out=T(SPE), in0=T(SPU), scalar=1.0, in1=T(SPE), op0=ALU.subtract, op1=ALU.subtract))
                        settle()
                        dve.wait_ge(*event("sp_inverse"))
                        step(tt(T(SPE), T(SPE), T(DTU), ALU.mult))
                        settle()
                        step(tt(T(SPL), T(SPL), T(SPE), ALU.subtract))
                        settle()
                        stt(out=T(DT), in0=T(SPZ), scalar=0.0, in1=T(SPL), op0=ALU.max, op1=ALU.add).then_inc(sem("dt"), 1)
                        dve.wait_ge(*event("dt"))
                        tt(T(DTU), T(DT), T(XRT), ALU.mult).then_inc(sem("dtu"), 1)

                    def states(g):
                        def drive(n):
                            ps = ring.read(dve, ("bc", n))
                            if n >= 2:
                                dve.wait_ge(sem("h"), n - 1)
                            tt(T(S6_DBU[n % 2]), T(DTU), ps[:, 0:512], ALU.mult).then_inc(sem("dbu"), 1)

                        if g == 0:
                            dve.wait_ge(*event("dtu"))
                        drive(GROUP * g)
                        for n in range(GROUP * g, GROUP * (g + 1)):
                            dve.wait_ge(sem("da"), n + 1)
                            dve.wait_ge(sem("dbu"), n + 1)
                            if n >= 2:
                                dve.wait_ge(sem("hc"), n - 1)
                            nc.vector.tensor_tensor_scan(T(S6_H[n % 2]), T(S6_DA[n % 3]), T(S6_DBU[n % 2]),
                                                         0.0, ALU.mult, ALU.add).then_inc(sem("h"), 1)
                            if n + 1 < GROUP * (g + 1):
                                drive(n + 1)
                            ps = ring.read(dve, ("bc", n))
                            if n >= 4:
                                dve.wait_ge(sem("pair_sum"), (n - 4) // 2 + 1)
                            dve.wait_ge(sem("h"), n + 1)
                            tt(T(S6_HC[n % 4]), T(S6_H[n % 2]), ps[:, 512:1024], ALU.mult).then_inc(sem("hc"), 1)

                    def state_output():
                        dve.wait_ge(sem("y_products"), STATES // 2)
                        stt(out=T(YD), in0=T(XRT), scalar=col("D_p"), in1=own(long_sum), op0=ALU.mult, op1=ALU.add).then_inc(sem("yd"), 1)

                    def mixed():
                        dve.wait_ge(*event("y_sig"))
                        dve.wait_ge(*event("yd"))
                        tt(T(MX), T(YD), T(YSIG), ALU.mult).then_inc(sem("mx"), 1)
                        dve.wait_ge(*event("v_sig"))
                        tt(T(VAL), T(VB), T(VSIG), ALU.mult).then_inc(sem("v_rows"), 1)
                        ps = ring.read(dve, "zr")
                        dve.wait_ge(*event("z_sig"))
                        stt(out=T(ZF), in0=ps[:, 0:512], scalar=col("bz"), in1=T(ZSIG), op0=ALU.add,
                            op1=ALU.mult).then_inc(sem("z"), 1)
                        dve.wait_ge(*event("r_sig"))
                        dve.wait_ge(*event("z"))
                        dve.wait_ge(*event("v_rows"))
                        ts(T(QF), T(ZF), col("gamma0"), col("beta0"), ALU.mult, ALU.add).then_inc(sem("qk_cols"), 1)
                        ts(T(KF), T(ZF), col("gamma1"), col("beta1"), ALU.mult, ALU.add).then_inc(sem("qk_cols"), 1)
                        stt(out=T(RF), in0=ps[:, 512:1024], scalar=col("br"), in1=T(RSIG), op0=ALU.add,
                            op1=ALU.mult).then_inc(sem("r"), 1)
                        ps = ring.read(dve, "u")
                        tt(blocks(T(UB)), blocks(ps[:, 0:512]), row4("bu"), ALU.add).then_inc(sem("u_raw"), 1)

                    def chunk_scores():
                        ps = ring.read(dve, "scores")
                        sbv = T(SB, 2)[:, 0:768].rearrange("p (c n) -> p c n", c=2)
                        tt(sbv, ps.rearrange("p (c n) -> p c n", c=2)[:, :, 0:384],
                           score_bias[:, :].unsqueeze(1).to_broadcast([P, 2, 384]), ALU.add).then_inc(sem("scores_biased"), 1)
                        dve.wait_ge(*event("scores_biased"))
                        step(nc.vector.tensor_reduce(own(sm1)[:, 0, 0:2], sbv[:, :, 0:128], AX.X, ALU.max, negate=True))
                        nc.vector.tensor_reduce(own(sm1)[:, 0, 2:4], sbv[:, :, 128:384], AX.X, ALU.max,
                                                negate=True).then_inc(sem("score_max"), 1)

                    def chunk_probs():
                        dve.wait_ge(*event("score_exp"))
                        step(nc.vector.reciprocal(own(sm1)[:, 2, :], own(sm1)[:, 1, :]))
                        settle()
                        for c in range(2):
                            ts(T(SB, 2)[:, c * 384:c * 384 + 128], T(SB, 2)[:, c * 384:c * 384 + 128],
                               own(sm1)[:, 2, c:c + 1], None, ALU.mult)
                            ins = ts(T(SB, 2)[:, c * 384 + 128:c * 384 + 384], T(SB, 2)[:, c * 384 + 128:c * 384 + 384],
                                     own(sm1)[:, 2, 2 + c:3 + c], None, ALU.mult)
                        ins.then_inc(sem("probs"), 1)

                    def chunk_values():
                        ps = ring.read(dve, "av")
                        dve.wait_ge(*event("r"))
                        tt(T(HR), ps[:, 0:512], T(RF), ALU.mult).then_inc(sem("hr"), 1)

                    def chunk_out():
                        ps = ring.read(dve, "h")
                        tt(blocks(T(HB)), blocks(ps[:, 0:512]), row4("h_b"), ALU.add).then_inc(sem("h_raw"), 1)

                    def chunk_gate():
                        dve.wait_ge(*event("h_sig"))
                        dve.wait_ge(*event("h_raw"))
                        step(tt(T(HO), T(HB), T(HSIG), ALU.mult))
                        settle()
                        step(tt(T(HO), T(HO), T(RES), ALU.subtract))
                        settle()
                        step(tt(T(HO), T(HO), T(USIG), ALU.mult))
                        settle()
                        step(tt(T(HO), T(HO), T(RES), ALU.add))
                        settle()
                        ln_stats(1, T(HO))

                    def x1():
                        sublayer_end(1, T(HO), T(X0), T(X1))

                    def swiglu_in():
                        ln_ready(2)
                        ln_apply(2, T(X1), T(FXN), None, sem("fxn"))

                    def swiglu_up(c):
                        ps = ring.read(dve, ("gu", c))
                        dve.wait_ge(sem("f_sig"), c + 1)
                        step(tt(T(FG + c), ps[:, 0:512], T(FSIG + c), ALU.mult))
                        settle()
                        tt(T(FH + c), ps[:, 512:1024], T(FG + c), ALU.mult).then_inc(sem("fh"), 1)

                    def swiglu_down():
                        ps = ring.read(dve, "down")
                        nc.vector.tensor_copy(T(FO), ps[:, 0:512]).then_inc(sem("fo"), 1)
                        dve.wait_ge(*event("fo"))
                        ln_stats(3, T(FO))

                    def x2():
                        sublayer_end(3, T(FO), T(X1), T(X2))

                    def heads_in():
                        ln_ready(4)
                        ln_apply(4, T(X2), T(AXN), None, sem("axn"))

                    def parts(i):
                        return T(i, 2).bitcast(BF16).rearrange("p (c n) -> p c n", n=512)

                    def heads_qk():
                        ps = ring.read(dve, "QK")
                        kp = parts(KPARTS)
                        dve.wait_ge(*event("k_high"))
                        stt(out=T(KRES), in0=ps[:, 512:1024], scalar=col("bk"), in1=kp[:, 0, :], op0=ALU.add,
                            op1=ALU.subtract).then_inc(sem("k_parts"), 1)
                        dve.wait_ge(*event("k_parts"))
                        step(nc.vector.tensor_copy(kp[:, 1, :], T(KRES)))
                        settle()
                        tt(kp[:, 2, :], T(KRES), kp[:, 1, :], ALU.subtract).then_inc(sem("k_split"), 1)

                    def heads_mix():
                        ps = ring.read(dve, "QG")
                        qp = parts(QPARTS)
                        dve.wait_ge(*event("q_high"))
                        tt(T(QRES), ps[:, 0:512], qp[:, 0, :], ALU.subtract).then_inc(sem("q_parts"), 1)
                        dve.wait_ge(*event("q_parts"))
                        step(nc.vector.tensor_copy(qp[:, 1, :], T(QRES)))
                        settle()
                        tt(qp[:, 2, :], T(QRES), qp[:, 1, :], ALU.subtract).then_inc(sem("q_split"), 1)

                    def heads_v():
                        ps = ring.read(dve, "V")
                        dve.wait_ge(sem("ve_ones"), 1)
                        for j in range(NJ):
                            ins = tt(values_ext()[:, j, :, 0:8], blocks(ps[:, j * 128:(j + 1) * 128], 8), blocks(row("bv"), 8), ALU.add)
                        ins.then_inc(sem("v_ext"), 1)

                    def row_scores(j, half):
                        nm = own(neg_max)[:, :, :].rearrange("p j (e a) -> p j e a", e=2)
                        for p in range(half * 4, half * 4 + 4):
                            ps = ring.read(dve, ("s1", j, p))
                            nc.vector.tensor_reduce(nm[:, j, :, p], ps.rearrange("p (e n) -> p e n", e=2)[:, :, 0:(j + 1) * 128],
                                                    AX.X, ALU.max, negate=True).then_inc(sem("row_max"), 1)

                    def max_parts():
                        dve.wait_ge(sem("row_max"), NJ * PAIRS)
                        nmp = own(nm_parts)[:, :, :].rearrange("p j (c h) -> p j c h", c=PARTS)
                        step(nc.vector.tensor_copy(nmp[:, :, 0, :], own(neg_max)[:, :, :]))
                        settle()
                        step(tt(own(nm_res)[:, :, :], own(neg_max)[:, :, :], nmp[:, :, 0, :], ALU.subtract))
                        settle()
                        step(nc.vector.tensor_copy(nmp[:, :, 1, :], own(nm_res)[:, :, :]))
                        settle()
                        tt(nmp[:, :, 2, :], own(nm_res)[:, :, :], nmp[:, :, 1, :], ALU.subtract).then_inc(sem("nm_parts"), 1)

                    def head_values(g):
                        dve.wait_ge(sem("value_products"), g + 1)
                        if g >= 2:
                            dve.wait_ge(sem("ao_part"), g - 1)
                        nc.vector.tensor_copy(T(OCOL + g % 2), own(long_sum)).then_inc(sem("o_cols"), 1)

                    def head_divide(g):
                        ps = ring.read(dve, ("oT", g))
                        o = ps[:, 0:512].rearrange("p (j c d) -> p j c d", j=NJ, d=32)
                        inv = own(inv_sum)[:, g % 2, :, :]
                        step(nc.vector.reciprocal(inv, o[:, :, :, 8]))
                        settle()
                        ao = T(AO).rearrange("p (j h d) -> p j h d", j=NJ, d=8)
                        for e in range(2):
                            h = e * PAIRS + 2 * g
                            ins = tt(ao[:, :, h:h + 2, :], o[:, :, 2 * e:2 * e + 2, 0:8],
                                     inv[:, :, 2 * e:2 * e + 2].unsqueeze(3).to_broadcast([P, NJ, 2, 8]), ALU.mult)
                        ins.then_inc(sem("ao_part"), 1)

                    def heads_out():
                        ps = ring.read(dve, "proj")
                        tt(blocks(T(AOUT)), blocks(ps[:, 0:512]), row4("bo"), ALU.add).then_inc(sem("aout"), 1)
                        dve.wait_ge(*event("aout"))
                        ln_stats(5, T(AOUT))

                    def x3():
                        sublayer_end(5, T(AOUT), T(X2), T(X3))

                    def window_norm():
                        ln_ready(6)
                        ln_apply(6, T(X3), T(Y), None, sem("y_in"))

                    def layer_in(l):
                        ps = ring.read(dve, ("yT", l))
                        step(nc.vector.memset(T(HT)[64:128, 0:1], 0.0))
                        nc.vector.tensor_copy(T(HT)[64:128, 1:512], ps[64:128, 0:511]).then_inc(sem("shift_b"), 1)

                    def qkv(l, j):
                        n = l * NJ + j
                        ps = ring.read(dve, ("lqk", n))
                        if n >= 1:
                            dve.wait_ge(sem("rotated"), 2 * n)
                        w = ROT[j % 2]
                        for t in range(2):
                            v = ps[:, t * 512:(t + 1) * 512].rearrange("p (h d) -> p h d", d=LDIM)
                            cos = tables[:, l, 2 * t, j, :].unsqueeze(1).to_broadcast([P, LHEADS, LDIM])
                            sin = tables[:, l, 2 * t + 1, j, :]
                            t1 = T(TURNED + 2 * t).rearrange("p (h d) -> p h d", d=LDIM)
                            t2 = T(TURNED + 1 + 2 * t).rearrange("p (h d) -> p h d", d=LDIM)
                            if t == 1:
                                dve.wait_ge(sem("squares"), 2 * n + 1)
                            tt(t1, v, cos, ALU.mult)
                            tt(t2[:, :, 0:32], v[:, :, 32:64], sin[:, 0:32].unsqueeze(1).to_broadcast([P, LHEADS, 32]), ALU.mult)
                            ins = tt(t2[:, :, 32:64], v[:, :, 0:32], sin[:, 32:64].unsqueeze(1).to_broadcast([P, LHEADS, 32]), ALU.mult)
                            ins.then_inc(sem("turned"), 1)
                        dve.wait_ge(sem("squares"), 2 * (n + 1))
                        if n >= 2:
                            dve.wait_ge(sem("inv_norm"), n - 1)
                        step(nc.vector.tensor_reduce(own(ssq)[:, j % 2, :, :], T(w, 2).rearrange("p (t h d) -> p t h d", t=2, d=LDIM),
                                                     AX.X, ALU.add))
                        settle()
                        ts(own(ssq)[:, j % 2, :, :], own(ssq)[:, j % 2, :, :], 1e-24, None, ALU.max).then_inc(sem("sum_sq"), 1)

                    def window_scores(l, j):
                        n = l * NJ + j
                        ps = ring.read(dve, ("ls", n))
                        b = j % 2
                        if n >= 2:
                            dve.wait_ge(sem("lexp"), n - 1)
                        step(nc.vector.tensor_reduce(own(lmax)[:, b, :], ps.rearrange("p (i n) -> p i n", n=128), AX.X, ALU.max, negate=True))
                        settle()
                        inv_q = own(invn)[:, j, 0, :].rearrange("p (g e) -> p e g", e=2)
                        m = own(lmax)[:, b, :].rearrange("p (e g) -> p e g", e=2)
                        tt(m, m, inv_q, ALU.mult).then_inc(sem("lbias"), 1)

                    def window_sums(l, j):
                        n = l * NJ + j
                        b = j % 2
                        dve.wait_ge(sem("lexp"), n + 1)
                        nc.vector.reciprocal(own(lsum)[:, b, :], own(lsum)[:, b, :]).then_inc(sem("linv"), 1)

                    def prob_transposes(l, j):
                        ps = ring.read(dve, ("lpT", l * NJ + j))
                        nc.vector.tensor_copy(T(LPT[j % 2] + 1), ps[:, 512:1024]).then_inc(sem("lpT_b"), 1)

                    def window_project(l, j):
                        ps = ring.read(dve, ("lproj", l * NJ + j))
                        b = slice(j * 128, (j + 1) * 128)
                        tt(T(Y1)[:, b], T(Y)[:, b], ps[:, 0:128], ALU.add).then_inc(sem("y1"), 1)

                    def geglu_in(l):
                        ps = ring.read(dve, ("y1T", l))
                        step(nc.vector.memset(T(HT2)[64:128, 0:1], 0.0))
                        nc.vector.tensor_copy(T(HT2)[64:128, 1:512], ps[64:128, 0:511]).then_inc(sem("shift2_b"), 1)

                    def geglu_mean(l):
                        ps = ring.read(dve, ("mean", l))
                        dve.wait_ge(sem("shift2_a"), l + 1)
                        dve.wait_ge(sem("shift2_b"), l + 1)
                        tt(T(CEN), T(HT2), ps[:, 0:512], ALU.subtract).then_inc(sem("centred"), 1)

                    def geglu_norm(l):
                        dve.wait_ge(sem("var_rstd"), l + 1)
                        dve.wait_ge(sem("centred"), l + 1)
                        step(tt(T(HNT), T(CEN), T(RLN), ALU.mult))
                        settle()
                        ts(T(HGB), T(HNT), col("lg", l), col("lb", l), ALU.mult, ALU.add).then_inc(sem("hgb"), 1)

                    def geglu_up(l, c):
                        m = HID_ROWS[c]
                        ps = ring.read(dve, ("ag", l, c))
                        dve.wait_ge(sem("gelu"), 3 * l + c + 1)
                        stt(out=T(HH + c)[0:m, :], in0=ps[0:m, 0:512], scalar=col("b1a", 3 * l + c, m), in1=T(GG + c)[0:m, :],
                            op0=ALU.add, op1=ALU.mult).then_inc(sem("hh"), 1)

                    def geglu_down(l):
                        ps = ring.read(dve, ("w2", l))
                        tt(blocks(T(Y)), blocks(ps[:, 0:512]), row4("b2", l), ALU.add).then_inc(sem("y_raw"), 1)
                        dve.wait_ge(sem("y_raw"), l + 1)
                        ins = tt(T(Y), T(Y), T(Y1), ALU.add)
                        if l + 1 < DEPTH:
                            ins.then_inc(sem("y_in"), 1)
                        else:
                            step(ins)
                            settle()
                            ln_stats(7, T(Y))

                    def output():
                        ln_ready(7)
                        ln_apply(7, T(Y), T(LAST))
                        settle()
                        tt(T(HT), T(X3), T(LAST), ALU.add).then_inc(sem("out"), 1)

                    run({"input_stats": input_stats, "input_rms": input_rms, "input_scale": input_scale, "bc_dt_low": bc_dt_low,
                         "dt_v": dt_v, "softplus": softplus, "states": states, "state_output": state_output, "mixed": mixed,
                         "chunk_scores": chunk_scores, "chunk_probs": chunk_probs, "chunk_values": chunk_values,
                         "chunk_out": chunk_out, "chunk_gate": chunk_gate, "x1": x1, "swiglu_in": swiglu_in,
                         "swiglu_up": swiglu_up, "swiglu_down": swiglu_down, "x2": x2, "heads_in": heads_in,
                         "heads_qk": heads_qk, "heads_mix": heads_mix, "heads_v": heads_v, "row_scores": row_scores,
                         "max_parts": max_parts, "head_values": head_values, "head_divide": head_divide, "heads_out": heads_out,
                         "x3": x3, "window_norm": window_norm, "layer_in": layer_in, "qkv": qkv,
                         "window_scores": window_scores, "window_sums": window_sums, "prob_transposes": prob_transposes,
                         "window_project": window_project, "geglu_in": geglu_in, "geglu_mean": geglu_mean,
                         "geglu_norm": geglu_norm, "geglu_up": geglu_up, "geglu_down": geglu_down, "output": output})

                @block.scalar
                def _(act):
                    steps = [0]
                    loaded = [None]

                    def step(ins):
                        steps[0] += 1
                        ins.then_inc(sem("act_step"), 1)

                    def settle():
                        act.wait_ge(sem("act_step"), steps[0])

                    fn = nc.scalar.activation

                    def table(name):
                        if loaded[0] != name:
                            nc.scalar.preload_act_table_set(name)
                            loaded[0] = name

                    def ln_rstd(k):
                        table(LNEXP)
                        act.wait_ge(sem("ln_var"), k + 1)
                        step(fn(own(lnv)[:, k, :], own(mv)[:, k, :, 1], ACT.Ln, bias=eps))
                        settle()
                        fn(own(rstd)[:, k, :], own(lnv)[:, k, :], ACT.Exp, scale=-0.5).then_inc(sem("ln_rstd"), 1)

                    def input_stats():
                        ln_rstd(0)

                    def input_rms():
                        table(LNEXP)
                        act.wait_ge(*event("mean_sq"))
                        step(fn(own(rms)[:, 2, :], own(rms)[:, 1, :], ACT.Ln, bias=eps))
                        settle()
                        fn(own(rms)[:, 3, :], own(rms)[:, 2, :], ACT.Exp, scale=-0.5).then_inc(sem("rms"), 1)

                    def input_scale():
                        ps = ring.read(act, "xrT")
                        fn(T(XRT), ps[:, 0:512], ACT.Copy, scale=col("norm_w")).then_inc(sem("xrT"), 1)

                    def bc_dt_low():
                        ps = ring.read(act, "bcdt")
                        fn(T(DTLOW)[0:RANK, :], ps[0:RANK, 512:1024], ACT.Copy).then_inc(sem("dt_low"), 1)
                        fn(T(BCS).bitcast(BF16)[0:96, 0:512], ps[0:96, 0:512], ACT.Copy).then_inc(sem("bc_high"), 1)

                    def dt_v():
                        table(LNEXP)
                        act.wait_ge(*event("sp_z"))
                        step(fn(T(SPE), T(SPZ), ACT.Abs))
                        settle()
                        fn(T(SPE), T(SPE), ACT.Exp, scale=-1.0).then_inc(sem("sp_exp"), 1)

                    def softplus():
                        table(LNEXP)
                        act.wait_ge(*event("sp_1pe"))
                        fn(T(SPL), T(SPU), ACT.Ln).then_inc(sem("sp_ln"), 1)
                        act.wait_ge(*event("sp_ln"))
                        fn(T(DTU), T(SPL), ACT.Exp, scale=-1.0).then_inc(sem("sp_inverse"), 1)

                    def states(g):
                        table(LNEXP)
                        if g == 0:
                            act.wait_ge(*event("dt"))
                        for n in range(GROUP * g, GROUP * (g + 1)):
                            if n >= 3:
                                act.wait_ge(sem("h"), n - 2)
                            fn(T(S6_DA[n % 3]), T(DT), ACT.Exp, scale=col("A_log", n)).then_inc(sem("da"), 1)

                    def state_output():
                        table(SIGMOID)
                        act.wait_ge(*event("v_raw"))
                        act.wait_ge(*event("yd"))
                        fn(T(YSIG), T(YD), ACT.Sigmoid).then_inc(sem("y_sig"), 1)
                        fn(T(VSIG), T(VB), ACT.Sigmoid).then_inc(sem("v_sig"), 1)

                    def mixed():
                        table(SIGMOID)
                        ps = ring.read(act, "zr")
                        fn(T(ZSIG), ps[:, 0:512], ACT.Sigmoid, bias=col("bz")).then_inc(sem("z_sig"), 1)
                        fn(T(RSIG), ps[:, 512:1024], ACT.Sigmoid, bias=col("br")).then_inc(sem("r_sig"), 1)
                        act.wait_ge(*event("u_raw"))
                        step(fn(T(USIG), T(UB), ACT.Sigmoid))

                    def chunk_scores():
                        table(LNEXP)
                        act.wait_ge(*event("score_max"))
                        p = T(SB, 2)
                        for c in range(2):
                            for a, (lo, hi) in enumerate(((0, 128), (128, 384))):
                                v = p[:, c * 384 + lo:c * 384 + hi]
                                ins = fn(v, v, ACT.Exp, bias=own(sm1)[:, 0, 2 * a + c:2 * a + c + 1],
                                         accum_out=own(sm1)[:, 1, 2 * a + c:2 * a + c + 1])
                        ins.then_inc(sem("score_exp"), 1)

                    def chunk_probs():
                        ps = ring.read(act, "probsT")
                        fn(T(PROB_T, 2)[:, 0:768].rearrange("p (c n) -> p c n", c=2),
                           ps.rearrange("p (c n) -> p c n", c=2)[:, :, 0:384], ACT.Copy).then_inc(sem("probsT"), 1)

                    def chunk_out():
                        table(SIGMOID)
                        act.wait_ge(*event("h_raw"))
                        settle()
                        fn(T(HSIG), T(HB), ACT.Sigmoid).then_inc(sem("h_sig"), 1)

                    def chunk_gate():
                        ln_rstd(1)

                    def x1():
                        ln_rstd(2)

                    def swiglu_in():
                        ps = ring.read(act, "fxT")
                        fn(T(FXNT), ps[:, 0:512], ACT.Copy).then_inc(sem("fxT"), 1)

                    def swiglu_up(c):
                        table(SIGMOID)
                        ps = ring.read(act, ("gu", c))
                        fn(T(FSIG + c), ps[:, 0:512], ACT.Sigmoid).then_inc(sem("f_sig"), 1)

                    def swiglu_down():
                        ln_rstd(3)

                    def x2():
                        ln_rstd(4)

                    def heads_in():
                        ps = ring.read(act, "axT")
                        fn(T(AXNT), ps[:, 0:512], ACT.Copy).then_inc(sem("axT"), 1)

                    def heads_qk():
                        ps = ring.read(act, "QK")
                        fn(T(QT), ps[:, 0:512], ACT.Identity, bias=col("bq")).then_inc(sem("QT"), 1)
                        fn(T(KPARTS, 2).bitcast(BF16)[:, 0:512], ps[:, 512:1024], ACT.Identity, bias=col("bk")).then_inc(sem("k_high"), 1)

                    def heads_mix():
                        ps = ring.read(act, "QG")
                        fn(T(QPARTS, 2).bitcast(BF16)[:, 0:512], ps[:, 0:512], ACT.Copy).then_inc(sem("q_high"), 1)

                    def max_turn():
                        ps = ring.read(act, "nmT")
                        fn(own(nm_cols)[:, :], ps.bitcast(BF16)[0:PARTS * HEADS, 0:512], ACT.Copy).then_inc(sem("nm_cols"), 1)

                    def pair_probs(p):
                        table(LNEXP)
                        if p >= 2:
                            act.wait_ge(sem("value_products"), (p - 2) // 2 + 1)
                        for jk in range(NJ):
                            ps = ring.read(act, ("s2", p, jk))
                            w = SEQ - jk * 128
                            fn(prob_parts(p)[jk].rearrange("p (e n) -> p e n", e=2), ps.rearrange("p (e n) -> p e n", e=2)[:, :, 0:w],
                               ACT.Exp).then_inc(sem("exps"), 1)

                    def heads_turn():
                        ps = ring.read(act, "aoT")
                        fn(T(AOT), ps[:, 0:512], ACT.Copy).then_inc(sem("aoT"), 1)

                    def heads_out():
                        ln_rstd(5)

                    def x3():
                        ln_rstd(6)

                    def layer_in(l):
                        ps = ring.read(act, ("yT", l))
                        fn(T(HT)[0:64, :], ps[0:64, 0:512], ACT.Copy).then_inc(sem("shift_a"), 1)

                    def qkv(l, j):
                        n = l * NJ + j
                        ps = ring.read(act, ("lqk", n))
                        if n >= 2:
                            act.wait_ge(sem("sum_sq"), n - 1)
                        for t in (1, 0):
                            if t == 0:
                                act.wait_ge(sem("turned"), 2 * n + 1)
                            fn(T(ROT[j % 2] + t), ps[:, t * 512:(t + 1) * 512], ACT.Square).then_inc(sem("squares"), 1)
                        ps = ring.read(act, ("lv", n))
                        fn(T(LV + j), ps[:, 0:512], ACT.Copy).then_inc(sem("lv"), 1)

                    def inverse_norms(l, j):
                        n = l * NJ + j
                        table(LNEXP)
                        act.wait_ge(sem("sum_sq"), n + 1)
                        step(fn(own(lnss)[:, j % 2, :, :], own(ssq)[:, j % 2, :, :], ACT.Ln, scale=TWO10 * TWO10))
                        settle()
                        if n >= 4:
                            act.wait_ge(sem("lexp"), n - 3)
                            act.wait_ge(sem("rotated"), 2 * (n - 3))
                        fn(own(invn)[:, j, :, :], own(lnss)[:, j % 2, :, :], ACT.Exp, scale=-0.5).then_inc(sem("inv_norm"), 1)

                    def qk_transposes(l, j):
                        ps = ring.read(act, ("lqkT", l * NJ + j))
                        fn(blocks(T(LQT + j % 2)), blocks(ps[:, 0:512]), ACT.Copy).then_inc(sem("lqT"), 1)
                        k = T(LKT, 4).rearrange("p (g n) -> p g n", g=4)
                        fn(k[:, :, j * 128:(j + 1) * 128], blocks(ps[:, 512:1024]), ACT.Copy).then_inc(sem("lkT"), 1)

                    def window_scores(l, j):
                        n = l * NJ + j
                        table(LNEXP)
                        ps = ring.read(act, ("ls", n))
                        b = j % 2
                        act.wait_ge(sem("lbias"), n + 1)
                        act.wait_ge(sem("inv_norm"), n + 1)
                        if n >= 2:
                            act.wait_ge(sem("lprobs"), n - 1)
                            act.wait_ge(sem("lpT"), n - 1)
                            act.wait_ge(sem("lpT_b"), n - 1)
                        pr = T(LP[b], 2)
                        for e in range(2):
                            for g in range(4):
                                i = e * 4 + g
                                ins = fn(pr[:, i * 128:(i + 1) * 128], ps[:, i * 128:(i + 1) * 128], ACT.Exp,
                                         bias=own(lmax)[:, b, i:i + 1], scale=own(invn)[:, j, 0, 2 * g + e:2 * g + e + 1],
                                         accum_out=own(lsum)[:, b, i:i + 1])
                        ins.then_inc(sem("lexp"), 1)

                    def prob_transposes(l, j):
                        n = l * NJ + j
                        ps = ring.read(act, ("lpT", n))
                        if n >= 2:
                            act.wait_ge(sem("lo"), n - 1)
                        fn(T(LPT[j % 2]), ps[:, 0:512], ACT.Copy).then_inc(sem("lpT"), 1)

                    def window_values(l, j):
                        n = l * NJ + j
                        ps = ring.read(act, ("lo", n))
                        if n >= 1:
                            act.wait_ge(sem("y1"), n)
                        fn(T(LOT), ps[:, 0:512], ACT.Copy).then_inc(sem("lo"), 1)

                    def geglu_in(l):
                        ps = ring.read(act, ("y1T", l))
                        fn(T(HT2)[0:64, :], ps[0:64, 0:512], ACT.Copy).then_inc(sem("shift2_a"), 1)

                    def geglu_mean(l):
                        act.wait_ge(sem("centred"), l + 1)
                        fn(T(SQF), T(CEN), ACT.Square).then_inc(sem("centred_sq"), 1)

                    def geglu_var(l):
                        table(LNEXP)
                        ps = ring.read(act, ("var", l))
                        fn(T(RLN), ps[:, 0:512], ACT.Ln, bias=eps).then_inc(sem("var_ln"), 1)
                        act.wait_ge(sem("var_ln"), l + 1)
                        fn(T(RLN), T(RLN), ACT.Exp, scale=-0.5).then_inc(sem("var_rstd"), 1)

                    def geglu_up(l, c):
                        table(GELU)
                        m = HID_ROWS[c]
                        ps = ring.read(act, ("ag", l, c))
                        fn(T(GG + c)[0:m, :], ps[0:m, 512:1024], ACT.Gelu, bias=col("b1g", 3 * l + c, m)).then_inc(sem("gelu"), 1)

                    def geglu_down(l):
                        if l == DEPTH - 1:
                            ln_rstd(7)

                    run({"input_stats": input_stats, "input_rms": input_rms, "input_scale": input_scale, "bc_dt_low": bc_dt_low,
                         "dt_v": dt_v, "softplus": softplus, "states": states, "state_output": state_output, "mixed": mixed,
                         "chunk_scores": chunk_scores, "chunk_probs": chunk_probs, "chunk_out": chunk_out,
                         "chunk_gate": chunk_gate, "x1": x1, "swiglu_in": swiglu_in, "swiglu_up": swiglu_up,
                         "swiglu_down": swiglu_down, "x2": x2, "heads_in": heads_in, "heads_qk": heads_qk,
                         "heads_mix": heads_mix, "max_turn": max_turn, "pair_probs": pair_probs, "heads_turn": heads_turn,
                         "heads_out": heads_out, "x3": x3, "layer_in": layer_in, "qkv": qkv, "inverse_norms": inverse_norms,
                         "qk_transposes": qk_transposes, "window_scores": window_scores, "prob_transposes": prob_transposes,
                         "window_values": window_values, "geglu_in": geglu_in, "geglu_mean": geglu_mean,
                         "geglu_var": geglu_var, "geglu_up": geglu_up, "geglu_down": geglu_down})

                @block.gpsimd
                def _(pool):
                    def states(g):
                        for m in range(GROUP // 2 * g, GROUP // 2 * (g + 1)):
                            pool.wait_ge(sem("hc"), 2 * m + 2)
                            if m >= 2:
                                pool.wait_ge(sem("y_products"), m - 1)
                            nc.gpsimd.tensor_tensor(T(S6_SUM[m % 2]), T(S6_HC[2 * m % 4]), T(S6_HC[(2 * m + 1) % 4]),
                                                    ALU.add).then_inc(sem("pair_sum"), 1)

                    def heads_in():
                        pool.wait_ge(*event("axn"))
                        nc.gpsimd.memset(T(VE, 4), 0.0).then_inc(sem("ve_zero"), 1)
                        pool.wait_ge(sem("ve_zero"), 1)
                        nc.gpsimd.memset(values_ext()[:, :, :, 8:9], 1.0).then_inc(sem("ve_ones"), 1)

                    def combine(l, j):
                        n = l * NJ + j
                        w = ROT[j % 2]
                        pool.wait_ge(sem("turned"), 2 * (n + 1))
                        pool.wait_ge(sem("sum_sq"), n + 1)
                        nc.gpsimd.tensor_tensor(T(w), T(TURNED), T(TURNED + 1), ALU.add).then_inc(sem("rotated"), 1)
                        nc.gpsimd.tensor_tensor(T(TURNED + 2), T(TURNED + 2), T(TURNED + 3), ALU.add).then_inc(sem("k_sum"), 1)
                        pool.wait_ge(sem("k_sum"), n + 1)
                        pool.wait_ge(sem("inv_norm"), n + 1)
                        nc.gpsimd.tensor_tensor(T(w + 1).rearrange("p (h d) -> p h d", d=LDIM),
                                                T(TURNED + 2).rearrange("p (h d) -> p h d", d=LDIM),
                                                own(invn)[:, j, 1, :].unsqueeze(2).to_broadcast([P, LHEADS, LDIM]),
                                                ALU.mult).then_inc(sem("rotated"), 1)

                    def window_sums(l, j):
                        n = l * NJ + j
                        pool.wait_ge(sem("linv"), n + 1)
                        pr = T(LP[j % 2], 2).rearrange("p (i n) -> p i n", n=128)
                        nc.gpsimd.tensor_tensor(pr, pr, own(lsum)[:, j % 2, :].unsqueeze(2).to_broadcast([P, LHEADS, 128]),
                                                ALU.mult).then_inc(sem("lprobs"), 1)

                    run({"states": states, "heads_in": heads_in, "inverse_norms": combine, "window_sums": window_sums})

                @block.sync
                def _(sp):
                    def load():
                        sp.dma_start(blocks(T(X0)), x_now[:, stream[0]].rearrange("a p j d -> (a p) j d")).then_inc(sem("x_loaded"), 16)

                    def spill_keys():
                        spill("k", 1, KPARTS, (0, 1, 2, 0, 1, 0))

                    def spill_queries():
                        spill("q", 0, QPARTS, (0, 0, 0, 1, 1, 2))

                    def spill(name, t, src, order):
                        sp.wait_ge(*event(name + "_split"))
                        part = T(src, 2).bitcast(BF16).rearrange("p (c n) -> p c n", n=512)
                        for c, i in enumerate(order):
                            sp.dma_start(own(split_scratch)[t, c].rearrange("(f h) n -> h f n", f=8), part[:, i, :]).then_inc(sem("spilled"), 16)

                    def restack():
                        sp.wait_ge(sem("spilled"), 16 * 2 * SPLITS)
                        for t, dst in enumerate((QSTK, KSTK)):
                            st = T(dst, 4).bitcast(BF16).rearrange("p (a n) -> p a n", a=PAIRS)
                            for e in range(2):
                                sp.dma_start(st[e * 64:e * 64 + STACK],
                                             own(split_scratch)[t].rearrange("c (f e a) n -> e (c f) a n", e=2, a=PAIRS)[e]).then_inc(sem("stacked"), 16)
                                if t == 1:
                                    sp.dma_start(st[e * 64 + STACK:e * 64 + STACK + PARTS].bitcast(U16), ones_d).then_inc(sem("stacked"), 16)

                    def max_turn():
                        sp.wait_ge(*event("nm_cols"))
                        sp.dma_start(own(max_scratch).rearrange("c h n -> (c h) n"), own(nm_cols)[:, :]).then_inc(sem("max_spilled"), 16)

                    def max_stack():
                        sp.wait_ge(sem("max_spilled"), 16)
                        st = T(QSTK, 4).bitcast(BF16).rearrange("p (a n) -> p a n", a=PAIRS)
                        for e in range(2):
                            sp.dma_start(st[e * 64 + STACK:e * 64 + STACK + PARTS],
                                         own(max_scratch)[:, e * PAIRS:(e + 1) * PAIRS, :]).then_inc(sem("maxima_stacked"), 16)

                    def window_before(l, j):
                        n = l * NJ + j
                        sp.wait_ge(sem("lv"), n + 1)
                        if n >= 2:
                            sp.wait_ge(sem("lo"), n - 1)
                        sp.dma_start(own(v_prev)[64:128, j % 2, :], T(LV + j)[0:64, :]).then_inc(sem(f"v_moved{j % 2}"), 16)
                        if j > 0:
                            sp.dma_start(own(v_prev)[0:64, j % 2, :], T(LV + j - 1)[64:128, :]).then_inc(sem(f"v_moved{j % 2}"), 16)

                    def output():
                        sp.wait_ge(sem("out"), 1)
                        sp.dma_start(out_now[:, stream[0]].rearrange("a p j d -> (a p) j d"), blocks(T(HT))).then_inc(sem("stored"), 16)

                    run({"load": load, "spill_keys": spill_keys, "spill_queries": spill_queries, "restack": restack,
                         "max_turn": max_turn, "max_stack": max_stack, "prob_transposes": window_before, "output": output})
                    for stream[0] in range(STREAMS):
                        sp.wait_ge(sem("stored"), 16)

        sems.clear()
        with nc.Fori(0, iterations) as it:
            emit(interleaved(network_stages()), x_v[bass.ds(it, 1)], out_v[bass.ds(it, 1)])
            numbers = sorted(handle.num for handle in sems.values())
            nc.vector.sem_clear(range(numbers[0], numbers[-1] + 1))
            nc.all_engine_barrier()
    return nc


def pack(inp):
    f = {k: np.asarray(v) for k, v in inp.items()}
    a, w, g = "L0_attn_", "L1_attn_", "L1_ffn_"

    def column(v):
        return np.ascontiguousarray(v).reshape(P, -1)

    def padded(v):
        out = np.zeros((P, v.shape[1]), np.float32)
        out[:v.shape[0]] = v
        return out

    cols = {
        "norm_w": f[a + "norm_w"], "bz": f[a + "mx_b"][128:256], "br": f[a + "mx_b"][256:384],
        "gamma0": f[a + "gamma"][0], "gamma1": f[a + "gamma"][1], "beta0": f[a + "beta"][0], "beta1": f[a + "beta"][1],
        "dt_b": f[a + "dt_b"], "D_p": f[a + "D_p"], "alpha": f[a + "alpha_rb"][0], "alpha_sw": np.roll(f[a + "alpha_rb"][0], 64),
        "beta_rb": f[a + "beta_rb"][0], "beta_rb_sw": np.roll(f[a + "beta_rb"][0], 64),
        "bq": f[w + "bq"], "bk": f[w + "bk"], "gate": np.repeat(f[w + "gate"], HEAD_DIM),
        "lg": f[g + "ln_g"].T, "lb": f[g + "ln_b"].T, "shift": np.repeat(f[w + "shift_weights"], HEAD_DIM, axis=0),
        "W_cross": f[w + "W_cross"].reshape(P, HEAD_DIM), "A_log": f[a + "A_log"],
        "b1a": np.concatenate([padded(f[g + "b1"][l, c * 128:min((c + 1) * 128, HID)][:, None]) for l in range(DEPTH) for c in range(3)], 1),
        "b1g": np.concatenate([padded(f[g + "b1"][l, HID + c * 128:HID + min((c + 1) * 128, HID)][:, None]) for l in range(DEPTH) for c in range(3)], 1),
    }
    colp = np.concatenate([column(cols[k]) for k in COLS], 1)
    rows = {
        "v_b": f[a + "v_b"], "bu": f[a + "mx_b"][0:128], "bhx": f[a + "mx_b"][384:512], "h_b": f[a + "h_b"],
        "bv": f[w + "bv"], "bo": f[w + "bo"], "b2": f[g + "b2"], "qs": f[g + "q_scale"], "qs_sw": np.roll(f[g + "q_scale"], 32, axis=1),
        "ks": f[g + "k_scale"], "ks_sw": np.roll(f[g + "k_scale"], 32, axis=1),
    }
    rowp = np.concatenate([rows[k].reshape(1, -1) for k in ROWS], 1)
    xp = f[a + "xproj_w"]

    def blocks_of(v):
        return v.reshape(-1, P, v.shape[1]).transpose(1, 0, 2).reshape(P, -1)

    mats = {
        "v_w": f[a + "v_w"].T, "mx_w": f[a + "mx_w"].T, "h_w": f[a + "h_w"].T, "bc_w": np.concatenate([xp[8:40].T] * 3, 1),
        "dtl_w": xp[0:8].T, "dt_w": padded(f[a + "dt_w"].T), "Wq": f[w + "Wq"].T, "Wk": f[w + "Wk"].T, "Wv": f[w + "Wv"].T,
        "Wo": f[w + "Wo"].T, "wqkv": np.concatenate(list(f[g + "wqkv"]), 1),
        "wo": np.concatenate([blocks_of(f[g + "wo"][l]) for l in range(DEPTH)], 1),
        "w1": np.concatenate(list(f[g + "w1"]), 1),
        "w2": np.concatenate([blocks_of(np.concatenate([f[g + "w2"][l], np.zeros((384 - HID, 128), np.float32)], 0)) for l in range(DEPTH)], 1),
    }
    wts = np.concatenate([mats[k] for k in WTS], 1)
    ints = np.concatenate([f["L0_ffn_w_gate"].T, f["L0_ffn_w_up"].T, blocks_of(f["L0_ffn_w_down"].T)], 1)
    return {"colp": colp, "rowp": rowp, "wts": wts, "ints": ints}


def constants():
    f32 = np.float32
    eye = np.eye(P, dtype=f32)
    q, k = np.arange(P)[:, None], np.arange(P)[None, :]
    causal = np.where(k > q, f32(NEG), f32(0))
    head = np.arange(P) // HEAD_DIM
    fr = np.arange(P) % HEAD_DIM
    taps = np.stack([(np.arange(HEAD_DIM)[None, :] - fr[:, None] == tau) for tau in range(4)], 1).reshape(P, 32).astype(f32)
    freqs = np.exp(np.arange(64, dtype=f32) * f32(-math.log(10000.0) / 64))
    ang = (np.arange(CHUNK, dtype=f32)[:, None] * freqs[None, :]).T
    cos0, sin0 = np.cos(ang), np.sin(ang)
    half = np.arange(0, LDIM, 2, dtype=f32)
    inv_freq = f32(1.0) / np.power(f32(10000.0), half / f32(LDIM))
    t = np.arange(SEQ, dtype=f32)
    fq = t[:, None] * inv_freq[None, :]
    base = (half + f32(0.4 * LDIM)) / f32(1.4 * LDIM)
    power = (t - SEQ // 2) / f32(WINDOW // 2)
    scale = np.power(base[None, :], power[:, None])
    two = lambda v: np.concatenate([v, v], 1)
    cos, sin, scale = two(np.cos(fq)), two(np.sin(fq)), two(scale)
    sign = np.where(np.arange(LDIM) < LDIM // 2, f32(-1), f32(1))[None, :]
    rows = lambda v: v.reshape(NJ, P, LDIM).transpose(1, 0, 2).reshape(P, NJ * LDIM)
    vals = {
        "ident": eye, "mean": np.full((P, P), 1.0 / P, f32), "causal": causal, "blocks": (head[:, None] == head[None, :]).astype(f32),
        "taps": taps, "cos0": np.concatenate([cos0, cos0], 0), "sin0": np.concatenate([-sin0, sin0], 0),
        "qcos": rows(cos * scale), "qsin": rows(sign * sin * scale), "kcos": rows(cos / scale), "ksin": rows(sign * sin / scale),
        "eps": np.full((P, 1), EPS, f32),
    }
    cst = np.concatenate([vals[n] for n in CST], 1).astype(f32)
    tab = np.concatenate([vals[n] for n in TAB], 1).astype(f32)
    i, c = np.arange(WINDOW)[:, None], np.arange(P)[None, :]
    window = np.where(c < WINDOW, c >= i, c - WINDOW <= i)
    window0 = np.where(c < WINDOW, False, c - WINDOW <= i)
    mask = lambda m: np.where(m, f32(0), f32(NEG))
    sel = np.zeros((P, 32, P), f32)
    for r in range(96):
        sel[r, r % 32, :] = 1
    bvals = {"ident": eye, "causal": causal, "causal_T": causal.T, "window0": mask(np.concatenate([window0, window], 0)),
             "window": mask(np.concatenate([window, window], 0)), "select": sel.reshape(P, -1)}
    bits = lambda v: (np.ascontiguousarray(v, f32).view(np.uint32) >> 16).astype(np.uint16)
    bcst = bits(np.concatenate([bvals[n] for n in BCST], 1))
    ones = bits(np.ones((PARTS, PAIRS, SEQ), f32))
    return {"cst": cst, "tab": tab, "bcst": bcst, "ones": ones}


def kernel(**inputs):
    import concourse.bacc as _bacc
    from concourse.bass_utils import run_bass_kernel_spmd as _run

    nc = _bacc.Bacc("TRN2", target_bir_lowering=False, num_devices=1)
    packed = pack(inputs)
    packed.update(constants())
    packed["x"] = np.asarray(inputs["L0_attn_x"])
    arrays = {"in_" + n: np.ascontiguousarray(v) for n, v in packed.items()}
    ap = {n: nc.dram_tensor(n, v.shape, mybir.dt.from_np(v.dtype), kind="ExternalInput").ap() for n, v in arrays.items()}
    out = nc.dram_tensor("out", (BATCH, SEQ, DIM), F32, kind="ExternalOutput").ap()
    build(nc, *(ap["in_" + n] for n in ("x", "colp", "rowp", "wts", "ints", "cst", "tab", "bcst", "ones")), out)
    r = _run(nc, [arrays], core_ids=[0])
    return r.results[0]["out"]
```
